# Optimizing a Trainium2 kernel written in Bass

```python
import numpy as np
import jax
import jax.numpy as jnp

def _softmax(x, axis=-1):
    return jax.nn.softmax(x, axis=axis)

def _gelu(x):
    return jax.nn.gelu(x, approximate=True)

def _silu(x):
    return jax.nn.silu(x)

def _sigmoid(x):
    return jax.nn.sigmoid(x)

def _layernorm(x, axis=-1, eps=1e-05):
    m = jnp.mean(x, axis=axis, keepdims=True)
    v = jnp.var(x, axis=axis, keepdims=True)
    return (x - m) / jnp.sqrt(v + eps)

def _scatter_add(tgt, idx, src, axis=0):
    return tgt.at[idx].add(src)

def _segment_sum(src, seg, n):
    return jax.ops.segment_sum(src, seg, n)
kernel_name = 'mk_perceiver_d1_seqx_r2_720b17'

def setup_inputs(seed: int=0):
    np.random.seed(seed)
    _w = jnp.asarray

    def _rec_inputs():
        import jax
        import jax.numpy as jnp
        _rk = jax.random.key(seed)
        x = -0.0003929 + 0.9999 * jax.random.normal(jax.random.fold_in(_rk, 1), (16, 64, 1024), jnp.float32)
        _lenS = 64 - jax.random.randint(jax.random.fold_in(_rk, 7), (16,), 0, max(1, 64 // 4) + 1, jnp.int32)
        _lenS2 = 512 - jax.random.randint(jax.random.fold_in(_rk, 8), (16,), 0, max(1, 512 // 4) + 1, jnp.int32)
        _ctx_2048P = jax.random.normal(jax.random.fold_in(_rk, 11), (16, 16, 1024), jnp.float32)
        _ctx_2048c = jax.random.dirichlet(jax.random.fold_in(_rk, 511), 0.3 * jnp.ones((16,), jnp.float32), (16, 512))
        _ctx_2048t = jnp.einsum('bsk,bkd->bsd', _ctx_2048c, _ctx_2048P)
        _ctx_2048t = _ctx_2048t * jax.lax.rsqrt(jnp.mean(jnp.square(_ctx_2048t)) + 1e-12) * 0.953939
        ctx_2048 = -1.39393e-06 + 0.999914 * (_ctx_2048t + 0.3 * jax.random.normal(jax.random.fold_in(_rk, 611), (16, 512, 1024), jnp.float32))
        itok_BxS_0_1023 = jax.random.randint(jax.random.fold_in(_rk, 12), (16, 64), 0, 512, jnp.int32)
        return (x, ctx_2048, itok_BxS_0_1023)
    x, ctx_2048, itok_BxS_0_1023 = _rec_inputs()

    def _L0_xattn_setup():
        import jax, jax.numpy as jnp
        import numpy as np
        B, Lq, Lk = (2, 2048, 512)
        Q_DIM, KV_DIM = (1024, 1024)
        H, HD = (16, 128)
        KVC, QC, R = (256, 384, 64)
        LOOKBACK = 8
        NEG = -1e+30

        def _rope(x, L):
            half = x.shape[-1] // 2
            inv_freq = 1.0 / 10000.0 ** (jnp.arange(half, dtype=jnp.float32) / half)
            ang = jnp.arange(L, dtype=jnp.float32)[:, None] * inv_freq
            cos, sin = (jnp.cos(ang), jnp.sin(ang))
            x1, x2 = (x[..., :half], x[..., half:])
            return jnp.concatenate([x1 * cos - x2 * sin, x1 * sin + x2 * cos], axis=-1)
        key = jax.random.key(seed)
        ks = jax.random.split(key, 11)

        def w(k, shape, fan_in):
            return jax.random.normal(k, shape, jnp.float32) / np.sqrt(fan_in).astype(np.float32)
        return {'q': jax.random.normal(ks[0], (B, Lq, Q_DIM), jnp.float32), 'kv': jax.random.normal(ks[1], (B, Lk, KV_DIM), jnp.float32), 'seg_id': jnp.sort(jax.random.randint(ks[2], (B, Lq), 0, Lk), axis=-1), 'W_kvc': w(ks[3], (KV_DIM, KVC), KV_DIM), 'W_dq': w(ks[4], (Q_DIM, QC), Q_DIM), 'W_uq': w(ks[5], (QC, H * HD), QC), 'W_qr': w(ks[6], (QC, H * R), QC), 'W_uk': w(ks[7], (KVC, H * HD), KVC), 'W_kr': w(ks[8], (KVC, R), KVC), 'W_uv': w(ks[9], (KVC, H * HD), KVC), 'W_o': w(ks[10], (H * HD, Q_DIM), H * HD)}
    _L0_xattn_all = _L0_xattn_setup()
    _L0_xattn_in = {k: v for k, v in _L0_xattn_all.items() if k in ('W_kvc', 'W_dq', 'W_uq', 'W_qr', 'W_uk', 'W_kr', 'W_uv', 'W_o')}
    del _L0_xattn_all

    def _L0_attn_setup():
        import jax, jax.numpy as jnp
        import numpy as np
        N_EMBD = 1024
        N_HEADS = 16
        HEAD_DIM = N_EMBD // N_HEADS
        THETA = 10000.0

        def _rope_tables(seq_len, head_dim):
            inv = 1.0 / THETA ** (jnp.arange(0, head_dim, 2, dtype=jnp.float32) / head_dim)
            pos = jnp.arange(seq_len, dtype=jnp.float32)
            freqs = jnp.outer(pos, inv)
            return (jnp.cos(freqs)[None, :, None, :], jnp.sin(freqs)[None, :, None, :])

        def _apply_rope(t, cos, sin):
            B, S, H, D = t.shape
            tr = t.reshape(B, S, H, D // 2, 2)
            x0, x1 = (tr[..., 0], tr[..., 1])
            r0 = x0 * cos - x1 * sin
            r1 = x0 * sin + x1 * cos
            return jnp.stack([r0, r1], axis=-1).reshape(B, S, H, D)
        key = jax.random.key(seed)
        ks = jax.random.split(key, 9)
        B, S, E = (4, 1024, N_EMBD)
        scale = 1.0 / np.sqrt(E)
        inp = {'x': jax.random.normal(ks[0], (B, S, E), dtype=jnp.float32), 'Wq': jax.random.normal(ks[1], (E, E), dtype=jnp.float32) * scale, 'bq': jnp.zeros((E,), dtype=jnp.float32), 'Wk': jax.random.normal(ks[2], (E, E), dtype=jnp.float32) * scale, 'bk': jnp.zeros((E,), dtype=jnp.float32), 'Wv': jax.random.normal(ks[3], (E, E), dtype=jnp.float32) * scale, 'bv': jnp.zeros((E,), dtype=jnp.float32), 'Wo': jax.random.normal(ks[4], (E, E), dtype=jnp.float32) * scale, 'bo': jnp.zeros((E,), dtype=jnp.float32)}
        return inp
    _L0_attn_all = _L0_attn_setup()
    _L0_attn_in = {k: v for k, v in _L0_attn_all.items() if k in ('Wq', 'bq', 'Wk', 'bk', 'Wv', 'bv', 'Wo', 'bo')}
    del _L0_attn_all

    def _L0_ffn_setup():
        import jax, jax.numpy as jnp
        import numpy as np
        NUM_EXPERTS = 32
        TOP_K = 6
        N_GROUPS = 4
        N_LIMITED_GROUPS = 2
        key = jax.random.key(seed)
        ks = jax.random.split(key, 8)
        H, M = (1024, 704)
        SH = 2 * M
        s = 0.02
        return {'hidden_states': jax.random.normal(ks[0], (4, 1024, H), jnp.float32), 'gate_w': jax.random.normal(ks[1], (H, NUM_EXPERTS), jnp.float32) * s, 'w_gate': jax.random.normal(ks[2], (NUM_EXPERTS, H, M), jnp.float32) * s, 'w_up': jax.random.normal(ks[3], (NUM_EXPERTS, H, M), jnp.float32) * s, 'w_down': jax.random.normal(ks[4], (NUM_EXPERTS, M, H), jnp.float32) * s, 'sw_gate': jax.random.normal(ks[5], (H, SH), jnp.float32) * s, 'sw_up': jax.random.normal(ks[6], (H, SH), jnp.float32) * s, 'sw_down': jax.random.normal(ks[7], (SH, H), jnp.float32) * s}
    _L0_ffn_all = _L0_ffn_setup()
    _L0_ffn_in = {k: v for k, v in _L0_ffn_all.items() if k in ('gate_w', 'w_gate', 'w_up', 'w_down', 'sw_gate', 'sw_up', 'sw_down')}
    del _L0_ffn_all
    return {'x': x, 'ctx_2048': ctx_2048, 'itok_BxS_0_1023': itok_BxS_0_1023, 'L0_xattn_W_kvc': _L0_xattn_in['W_kvc'], 'L0_xattn_W_dq': _L0_xattn_in['W_dq'], 'L0_xattn_W_uq': _L0_xattn_in['W_uq'], 'L0_xattn_W_qr': _L0_xattn_in['W_qr'], 'L0_xattn_W_uk': _L0_xattn_in['W_uk'], 'L0_xattn_W_kr': _L0_xattn_in['W_kr'], 'L0_xattn_W_uv': _L0_xattn_in['W_uv'], 'L0_xattn_W_o': _L0_xattn_in['W_o'], 'L0_attn_Wq': _L0_attn_in['Wq'], 'L0_attn_bq': _L0_attn_in['bq'], 'L0_attn_Wk': _L0_attn_in['Wk'], 'L0_attn_bk': _L0_attn_in['bk'], 'L0_attn_Wv': _L0_attn_in['Wv'], 'L0_attn_bv': _L0_attn_in['bv'], 'L0_attn_Wo': _L0_attn_in['Wo'], 'L0_attn_bo': _L0_attn_in['bo'], 'L0_ffn_gate_w': _L0_ffn_in['gate_w'], 'L0_ffn_w_gate': _L0_ffn_in['w_gate'], 'L0_ffn_w_up': _L0_ffn_in['w_up'], 'L0_ffn_w_down': _L0_ffn_in['w_down'], 'L0_ffn_sw_gate': _L0_ffn_in['sw_gate'], 'L0_ffn_sw_up': _L0_ffn_in['sw_up'], 'L0_ffn_sw_down': _L0_ffn_in['sw_down']}

def reference(x, ctx_2048, itok_BxS_0_1023, L0_xattn_W_kvc, L0_xattn_W_dq, L0_xattn_W_uq, L0_xattn_W_qr, L0_xattn_W_uk, L0_xattn_W_kr, L0_xattn_W_uv, L0_xattn_W_o, L0_attn_Wq, L0_attn_bq, L0_attn_Wk, L0_attn_bk, L0_attn_Wv, L0_attn_bv, L0_attn_Wo, L0_attn_bo, L0_ffn_gate_w, L0_ffn_w_gate, L0_ffn_w_up, L0_ffn_w_down, L0_ffn_sw_gate, L0_ffn_sw_up, L0_ffn_sw_down):
    import jax
    import jax.numpy as jnp

    def _L0_xattn_ref(q, kv, seg_id, W_kvc, W_dq, W_uq, W_qr, W_uk, W_kr, W_uv, W_o):
        import jax, jax.numpy as jnp
        import numpy as np
        B, Lq, Lk = (2, 2048, 512)
        Q_DIM, KV_DIM = (1024, 1024)
        H, HD = (16, 128)
        KVC, QC, R = (256, 384, 64)
        LOOKBACK = 8
        NEG = -1e+30

        def _rope(x, L):
            half = x.shape[-1] // 2
            inv_freq = 1.0 / 10000.0 ** (jnp.arange(half, dtype=jnp.float32) / half)
            ang = jnp.arange(L, dtype=jnp.float32)[:, None] * inv_freq
            cos, sin = (jnp.cos(ang), jnp.sin(ang))
            x1, x2 = (x[..., :half], x[..., half:])
            return jnp.concatenate([x1 * cos - x2 * sin, x1 * sin + x2 * cos], axis=-1)
        b, lq, _ = q.shape
        lk = kv.shape[1]
        kv_c = kv @ W_kvc
        q_c = q @ W_dq
        q_nope = (q_c @ W_uq).reshape(b, lq, H, HD).transpose(0, 2, 1, 3)
        q_rope = (q_c @ W_qr).reshape(b, lq, H, R).transpose(0, 2, 1, 3)
        k_nope = (kv_c @ W_uk).reshape(b, lk, H, HD)
        v = (kv_c @ W_uv).reshape(b, lk, H, HD)
        k_rope = kv_c @ W_kr
        q_rope = _rope(q_rope, lq)
        k_rope = _rope(k_rope, lk)
        scale = 1.0 / np.sqrt(HD + R).astype(np.float32)
        scores = (jnp.einsum('bhqd,bkhd->bhqk', q_nope, k_nope) + jnp.einsum('bhqr,bkr->bhqk', q_rope, k_rope)) * scale
        k_ids = jnp.arange(lk)[None, None, :]
        qs = seg_id[:, :, None]
        good = (k_ids <= qs) & (k_ids >= qs - LOOKBACK)
        scores = jnp.where(good[:, None, :, :], scores, NEG)
        attn = jax.nn.softmax(scores, axis=-1)
        out = jnp.einsum('bhqk,bkhd->bqhd', attn, v).reshape(b, lq, H * HD)
        return out @ W_o

    def _L0_attn_ref(x, Wq, bq, Wk, bk, Wv, bv, Wo, bo):
        import jax, jax.numpy as jnp
        import numpy as np
        N_EMBD = 1024
        N_HEADS = 16
        HEAD_DIM = N_EMBD // N_HEADS
        THETA = 10000.0

        def _rope_tables(seq_len, head_dim):
            inv = 1.0 / THETA ** (jnp.arange(0, head_dim, 2, dtype=jnp.float32) / head_dim)
            pos = jnp.arange(seq_len, dtype=jnp.float32)
            freqs = jnp.outer(pos, inv)
            return (jnp.cos(freqs)[None, :, None, :], jnp.sin(freqs)[None, :, None, :])

        def _apply_rope(t, cos, sin):
            B, S, H, D = t.shape
            tr = t.reshape(B, S, H, D // 2, 2)
            x0, x1 = (tr[..., 0], tr[..., 1])
            r0 = x0 * cos - x1 * sin
            r1 = x0 * sin + x1 * cos
            return jnp.stack([r0, r1], axis=-1).reshape(B, S, H, D)
        B, S, E = x.shape
        H, D = (N_HEADS, HEAD_DIM)
        q = (x @ Wq.T + bq).reshape(B, S, H, D)
        k = (x @ Wk.T + bk).reshape(B, S, H, D)
        v = (x @ Wv.T + bv).reshape(B, S, H, D)
        cos, sin = _rope_tables(S, D)
        q = _apply_rope(q, cos, sin)
        k = _apply_rope(k, cos, sin)
        qk = jnp.einsum('bshd,bstd->bsht', q, k) / jnp.sqrt(jnp.float32(D))
        att = jax.nn.softmax(qk, axis=-1)
        out = jnp.einsum('bsht,bstd->bshd', att, v)
        out = jnp.swapaxes(out, 1, 2).reshape(B, S, E)
        return out @ Wo.T + bo

    def _L0_ffn_ref(hidden_states, gate_w, w_gate, w_up, w_down, sw_gate, sw_up, sw_down):
        import jax, jax.numpy as jnp
        import numpy as np
        NUM_EXPERTS = 32
        TOP_K = 6
        N_GROUPS = 4
        N_LIMITED_GROUPS = 2
        B, S, H = hidden_states.shape
        E, K = (NUM_EXPERTS, TOP_K)
        x = hidden_states.reshape(-1, H)
        T = x.shape[0]
        scores = jax.nn.sigmoid(x @ gate_w)
        original_scores = scores
        epg = E // N_GROUPS
        sg = scores.reshape(T, N_GROUPS, epg)
        group_scores = jnp.max(sg, axis=-1)
        _, top_groups = jax.lax.top_k(group_scores, N_LIMITED_GROUPS)
        mask = jnp.ones((T, N_GROUPS), dtype=bool)
        mask = mask.at[jnp.arange(T)[:, None], top_groups].set(False)
        sg = jnp.where(mask[:, :, None], -jnp.inf, sg)
        masked_scores = sg.reshape(T, E)
        _, selected_experts = jax.lax.top_k(masked_scores, K)
        weights = jnp.take_along_axis(original_scores, selected_experts, axis=-1)
        weights = weights / jnp.sum(weights, axis=-1, keepdims=True)
        sel_flat = selected_experts.ravel()
        x_exp = jnp.repeat(x, K, axis=0)
        sort_idx = jnp.argsort(sel_flat)
        xs = x_exp[sort_idx]
        group_sizes = jnp.bincount(sel_flat, length=E).astype(jnp.int32)
        g = jax.lax.ragged_dot(xs, w_gate, group_sizes)
        u = jax.lax.ragged_dot(xs, w_up, group_sizes)
        d = jax.lax.ragged_dot(jax.nn.silu(g) * u, w_down, group_sizes)
        unsort_idx = jnp.argsort(sort_idx)
        out = d[unsort_idx].reshape(T, K, H)
        expert_out = jnp.sum(out * weights[..., None], axis=1)
        shared = jax.nn.silu(x @ sw_gate) * (x @ sw_up) @ sw_down
        return (expert_out + shared).reshape(B, S, H)
    x = x + _L0_xattn_ref(_layernorm(x, axis=-1), ctx_2048, itok_BxS_0_1023, L0_xattn_W_kvc, L0_xattn_W_dq, L0_xattn_W_uq, L0_xattn_W_qr, L0_xattn_W_uk, L0_xattn_W_kr, L0_xattn_W_uv, L0_xattn_W_o)
    x = x + _L0_attn_ref(_layernorm(x, axis=-1), L0_attn_Wq, L0_attn_bq, L0_attn_Wk, L0_attn_bk, L0_attn_Wv, L0_attn_bv, L0_attn_Wo, L0_attn_bo)
    x = x + _L0_ffn_ref(_layernorm(x, axis=-1), L0_ffn_gate_w, L0_ffn_w_gate, L0_ffn_w_up, L0_ffn_w_down, L0_ffn_sw_gate, L0_ffn_sw_up, L0_ffn_sw_down)
    return x

_drawn_inputs = setup_inputs


def setup_inputs(seed=0):
    import zlib

    import numpy as np

    out = dict(_drawn_inputs(seed))
    spreads = {'L0_attn_bq': (0.0, 0.317),
     'L0_attn_bk': (0.0, 0.1),
     'L0_attn_bv': (0.0, 0.1),
     'L0_attn_bo': (0.0, 0.1)}
    factors = {}
    for name, (base, spread) in spreads.items():
        noise = np.random.default_rng([zlib.crc32(name.encode()), seed]).standard_normal(out[name].shape)
        drawn = base * np.exp(spread * noise) if base else spread * noise
        out[name] = jnp.asarray(drawn.astype(out[name].dtype))
    for name, factor in factors.items():
        out[name] = (out[name] * factor).astype(out[name].dtype)
    return out
```

```python
from collections import namedtuple
from contextlib import ExitStack

import concourse.bass as bass
import numpy as np
from concourse import mybir

F32 = mybir.dt.float32
I32 = mybir.dt.int32
ALU = mybir.AluOpType
ACT = mybir.ActivationFunctionType
AX = mybir.AxisListType

P = 128
B, LQ, LK, D = 16, 64, 512, 1024
T = B * LQ
KC = D // P
HALF_B = B // 2
HT = HALF_B * LQ
XH, HD, R = 16, 128, 64
KVC, QC = 256, 384
CC, QCC = KVC // P, QC // P
LOOKBACK = 8
NEG = -1e30
X_SCALE = float(np.float32(1.0) / np.sqrt(HD + R).astype(np.float32))
NH, DH = 16, 64
TT = T // P
E, TOP, NG, KEEP_G = 32, 6, 4, 2
F = 704
FH = F // 2
FC = 6
FCW = [128] * 5 + [64]
SHARED = 2
NE = E + SHARED
SH_TILES = SHARED * TT
MAX_TILES = SH_TILES + (T * TOP + E * (P - 1)) // P
NT = 98
assert MAX_TILES + 2 <= NT
PAD = P
EPS = 1e-5


def named(items):
    return namedtuple("Named", items)(**items)


def semaphores(nc, ctx, prefix, names):
    made = {n: nc.alloc_semaphore(f"{prefix}_{n}") for n in names.split()}

    def clear():
        nc.clear_and_free_semaphores(list(made.values()))
        nc.all_engine_barrier()

    ctx.callback(clear)
    return named(made)


def hold(engine, sem, value, spare):
    engine.wait_ge(sem, value)
    engine.sem_inc(spare, 1)


def queries(nc, ps, d, half, qa, qr, ident, cst):
    with ExitStack() as ctx:
        sb = lambda n, s, t=F32: ctx.enter_context(nc.sbuf_tensor(f"q{half}_{n}", s, t))
        s = semaphores(nc, ctx, f"q{half}", "x_in wdq_in hw_in0 hw_in1 x_free xn_ready xn_free x_psum_free qc_done qc_ready"
                       " nope_done nope_ready rope_done rope_free qa_done qa_free ln sq hw_free spare qr_done")
        x = sb("x", [P, D])
        xn = sb("xn", [P, D])
        xT = sb("xT", [P, KC, HT])
        stats = sb("stats", [P, 2, 6])
        mv = sb("mv", [P, 2])
        rstd = sb("rstd", [P, 1])
        sd = sb("sd", [P, 1])
        wdq = sb("wdq", [P, KC, QC])
        qcT = sb("qcT", [P, QCC, HT])
        hw = [sb(f"hw{i}", [P, 1024]) for i in range(2)]
        qn = sb("qn", [P, HT])
        rp = sb("rp", [R, 2, HT])
        hw_in = (s.hw_in0, s.hw_in1)
        TILES = HT // P
        with nc.Block() as block:

            @block.sync
            def _(sp):
                sp.dma_start(wdq[:], d.wdq.rearrange("(k p) n -> p k n", p=P)).then_inc(s.wdq_in, 16)
                with sp.Fori(0, TILES) as t:
                    sp.wait_ge(s.x_free, t + 1)
                    sp.dma_start(x[:], d.x[bass.ds(half * HT + t * P, P), :]).then_inc(s.x_in, 16)
                with sp.Fori(0, XH // 2) as hp:
                    for i in range(2):
                        sp.wait_ge(s.hw_free, hp * 2 + i + 1)
                        sp.dma_start(hw[i][:], d.head_w[hp * 2 + i]).then_inc(hw_in[i], 16)

            @block.vector
            def _(v):
                v.sem_inc(s.x_free, 1)
                v.sem_inc(s.rope_free, 1)
                v.sem_inc(s.hw_free, 2)
                with v.Fori(0, TILES) as t:
                    layernorm(v, x, stats, mv, sd, rstd, xn, s, t)
                with v.Fori(0, XH) as h:
                    v.wait_ge(s.rope_done, h + 1)
                    v.tensor_tensor(rp[:, 0, :], ps[1][0:R, :], cst.rope_q[0:R, :], ALU.mult)
                    v.tensor_tensor(rp[:, 1, :], ps[1][R:P, :], cst.rope_q[R:P, :], ALU.mult)\
                        .then_inc(s.rope_free, 1)
                    v.wait_ge(s.rope_free, h + 2)
                    v.tensor_tensor(qr[:, :, bass.ds(h, 1), :].rearrange("p b h q -> p b (h q)"),
                                    rp[:, 0, :].rearrange("p (b q) -> p b q", q=LQ),
                                    rp[:, 1, :].rearrange("p (b q) -> p b q", q=LQ), ALU.add).then_inc(s.qr_done, 1)
                    v.wait_ge(s.qr_done, h + 1)
                    v.wait_ge(s.qa_done, 2 * h + 2)
                    v.sem_inc(s.hw_free, 1)
                    v.tensor_copy(qa[:, 1, :, bass.ds(h, 1), :].rearrange("p b h q -> p b (h q)"),
                                  ps[3][:].rearrange("p (b q) -> p b q", q=LQ)).then_inc(s.qa_free, 1)

            @block.scalar
            def _(act):
                act.sem_inc(s.x_psum_free, 1)
                act.sem_inc(s.nope_ready, 1)
                act.sem_inc(s.qa_free, 2)
                with act.Fori(0, TILES) as t:
                    act.wait_ge(s.sq, 3 * t + 1)
                    act.activation(sd[:], rstd[:], ACT.Sqrt).then_inc(s.sq, 1)
                    act.wait_ge(s.xn_free, t + 2)
                    for i in range(2):
                        cp = act.activation(xT[:, 4 * i:4 * i + 4, bass.ds(t * P, P)],
                                            ps[i][:].rearrange("p (k m) -> p k m", m=P), ACT.Copy)
                    cp.then_inc(s.x_psum_free, 1)
                for m in range(QCC):
                    act.wait_ge(s.qc_done, m + 1)
                    act.activation(qcT[:, m, :], ps[4 + m][:], ACT.Copy).then_inc(s.qc_ready, 1)
                with act.Fori(0, XH) as h:
                    act.wait_ge(s.nope_done, h + 1)
                    act.activation(qn[:], ps[0][:], ACT.Copy).then_inc(s.nope_ready, 1)
                    act.wait_ge(s.qa_done, 2 * h + 1)
                    act.activation(qa[:, 0, :, bass.ds(h, 1), :].rearrange("p b h q -> p b (h q)"),
                                   ps[2][:].rearrange("p (b q) -> p b q", q=LQ), ACT.Copy).then_inc(s.qa_free, 1)

            @block.tensor
            def _(pe):
                pe.sem_inc(s.xn_free, 1)
                with pe.Fori(0, TILES) as t:
                    pe.wait_ge(s.x_psum_free, t + 1)
                    pe.wait_ge(s.xn_ready, t + 1)
                    for k in range(KC):
                        mm = pe.transpose(ps[k // 4][:, (k % 4) * P:(k % 4 + 1) * P], xn[:, k * P:(k + 1) * P], ident)
                    mm.then_inc(s.xn_free, 1)
                pe.wait_ge(s.wdq_in, 16)
                pe.wait_ge(s.x_psum_free, TILES + 1)
                for m in range(QCC):
                    for k in range(KC):
                        mm = pe.matmul(ps[4 + m][:], wdq[:, k, m * P:(m + 1) * P], xT[:, k, :],
                                       start=(k == 0), stop=(k == KC - 1))
                    mm.then_inc(s.qc_done, 1)
                pe.wait_ge(s.qc_ready, QCC)
                with pe.Fori(0, XH // 2) as hp:
                    for i in range(2):
                        h = hp * 2 + i
                        w = hw[i]
                        pe.wait_ge(hw_in[i], hp * 16 + 16)
                        pe.wait_ge(s.nope_ready, h + 1)
                        for m in range(QCC):
                            mm = pe.matmul(ps[0][:], w[:, m * P:(m + 1) * P], qcT[:, m, :],
                                           start=(m == 0), stop=(m == QCC - 1))
                        mm.then_inc(s.nope_done, 1)
                        pe.wait_ge(s.rope_free, h + 1)
                        for m in range(QCC):
                            mm = pe.matmul(ps[1][:], w[:, (3 + m) * P:(4 + m) * P], qcT[:, m, :],
                                           start=(m == 0), stop=(m == QCC - 1))
                        mm.then_inc(s.rope_done, 1)
                        pe.wait_ge(s.nope_ready, h + 2)
                        pe.wait_ge(s.qa_free, 2 * h + 2)
                        for c in range(CC):
                            pe.matmul(ps[2 + c][:], w[:, (6 + c) * P:(7 + c) * P], qn[:],
                                      start=True, stop=True).then_inc(s.qa_done, 1)


def layernorm(v, x, stats, mv, sd, rstd, xn, s, t):
    v.wait_ge(s.x_in, t * 16 + 16)
    layernorm_steps(v, x, stats, mv, sd, rstd, xn, s, t)


def layernorm_steps(v, x, stats, mv, sd, rstd, xn, s, t):
    v.bn_stats(stats[:, 0, :], x[:, 0:D // 2])
    v.bn_stats(stats[:, 1, :], x[:, D // 2:D]).then_inc(s.ln, 1)
    hold(v, s.ln, 2 * t + 1, s.spare)
    v.bn_aggr(mv[:], stats[:]).then_inc(s.ln, 1)
    v.wait_ge(s.ln, 2 * t + 2)
    v.tensor_scalar(rstd[:], mv[:, 1:2], EPS, None, ALU.add).then_inc(s.sq, 1)
    v.wait_ge(s.sq, 3 * t + 2)
    v.reciprocal(rstd[:], sd[:]).then_inc(s.sq, 1)
    v.wait_ge(s.sq, 3 * t + 3)
    v.wait_ge(s.xn_free, t + 1)
    v.tensor_scalar(xn[:], x[:], mv[:, 0:1], rstd[:], ALU.subtract, ALU.mult).then_inc(s.xn_ready, 1)
    v.wait_ge(s.xn_ready, t + 1)
    v.sem_inc(s.x_free, 1)


def contexts(nc, ps, d, half, qa, qr, ident, cst):
    with ExitStack() as ctx:
        sb = lambda n, s, t=F32: ctx.enter_context(nc.sbuf_tensor(f"c{half}_{n}", s, t))
        s = semaphores(nc, ctx, f"c{half}", "w_in ctx_in ctx_free seg_in seg_ready mstep kv_done kvT_ready kr_done kr_free kr_ready"
                       " kvx_done kv_ready q_staged q_free score_done score_free sm rowmax exp_done prob_ready"
                       " prob_free pT_ready out_done out_free spare")
        wkvc = sb("wkvc", [P, KC, KVC])
        wkr = sb("wkr", [P, CC, P])
        cT = sb("cT", [P, KC, LK])
        seg_i = sb("seg_i", [P, B], I32)
        seg = sb("seg", [P, 2, B])
        mask = sb("mask", [P, 2, LK])
        kvT = sb("kvT", [P, CC, LK])
        kv = sb("kv", [P, 4, KVC])
        kr = sb("kr", [R, LK])
        rp = sb("rp", [R, 2, LK])
        qs = sb("qs", [P, CC, XH * LQ])
        qrs = sb("qrs", [R, XH * LQ])
        sc = sb("sc", [P, 2, LK])
        nmax = sb("nmax", [P, 2])
        rsum = sb("rsum", [P, 2])
        pr = sb("pr", [P, 2, LK])
        pT = sb("pT", [P, 4, XH * LQ])
        RT = XH * LQ // P
        SC_BANK, OUT_BANK = (5, 6), ((0, 1), (3, 4))
        with nc.Block() as block:

            @block.sync
            def _(sp):
                sp.dma_start(wkvc[:], d.wkvc.rearrange("(k p) n -> p k n", p=P)).then_inc(s.w_in, 16)
                sp.dma_start(wkr[:], d.wkr.rearrange("(k p) n -> p k n", p=P)).then_inc(s.w_in, 16)
                sp.dma_start(seg_i[:], d.seg[:, :]).then_inc(s.seg_in, 16)
                with sp.Fori(0, HALF_B) as b:
                    sp.wait_ge(s.ctx_free, b + 1)
                    sp.dma_start(cT[:], d.ctxT[b + half * HALF_B].rearrange("(k p) n -> p k n", p=P))\
                        .then_inc(s.ctx_in, 16)

            @block.gpsimd
            def _(g):
                with g.Fori(0, HALF_B) as b:
                    hold(g, s.q_free, b + 1, s.spare)
                    g.tensor_copy(qs[:].rearrange("p c (h q) -> p c h q", q=LQ)[:, 0], qa[:, 0, bass.ds(b, 1), :, :]
                                  .rearrange("p b h q -> p (b h) q")).then_inc(s.q_staged, 1)
                    g.tensor_copy(qs[:].rearrange("p c (h q) -> p c h q", q=LQ)[:, 1], qa[:, 1, bass.ds(b, 1), :, :]
                                  .rearrange("p b h q -> p (b h) q")).then_inc(s.q_staged, 1)
                    g.tensor_copy(qrs[:].rearrange("p (h q) -> p h q", q=LQ), qr[:, bass.ds(b, 1), :, :]
                                  .rearrange("p b h q -> p (b h) q")).then_inc(s.q_staged, 1)

            @block.vector
            def _(v):
                v.sem_inc(s.kr_free, 1)
                v.sem_inc(s.score_free, 2)
                v.sem_inc(s.q_free, 1)
                v.wait_ge(s.seg_in, 16)
                v.tensor_copy(seg[:, 0, :], seg_i[:]).then_inc(s.seg_ready, 1)
                v.wait_ge(s.seg_ready, 1)
                v.tensor_scalar(seg[:, 1, :], seg[:, 0, :], -float(LOOKBACK), None, ALU.add).then_inc(s.seg_ready, 1)
                v.wait_ge(s.seg_ready, 2)
                with v.Fori(0, HALF_B) as b:
                    bb = b + half * HALF_B
                    v.tensor_scalar(mask[:, 0, :], cst.iota[:], seg[:, 0, bass.ds(bb, 1)], NEG, ALU.is_gt, ALU.mult)
                    v.tensor_scalar(mask[:, 1, :], cst.iota[:], seg[:, 1, bass.ds(bb, 1)], NEG, ALU.is_lt, ALU.mult)\
                        .then_inc(s.mstep, 1)
                    v.wait_ge(s.mstep, 2 * b + 1)
                    v.tensor_tensor(mask[:, 0, :], mask[:, 0, :], mask[:, 1, :], ALU.add).then_inc(s.mstep, 1)
                    v.wait_ge(s.kr_done, b + 1)
                    v.tensor_tensor(rp[:, 0, :], ps[2][0:R, :], cst.rope_k[0:R, :], ALU.mult)
                    v.tensor_tensor(rp[:, 1, :], ps[2][R:P, :], cst.rope_k[R:P, :], ALU.mult).then_inc(s.kr_free, 1)
                    v.wait_ge(s.kr_free, b + 2)
                    v.tensor_tensor(kr[:], rp[:, 0, :], rp[:, 1, :], ALU.add).then_inc(s.kr_ready, 1)
                    v.wait_ge(s.mstep, 2 * b + 2)

                    def softmax_head(r):
                        v.wait_ge(s.score_done, b * RT + r + 1)
                        if r == RT - 1:
                            v.sem_inc(s.q_free, 1)
                        v.scalar_tensor_tensor(sc[:, r % 2, :], ps[SC_BANK[r % 2]][:], X_SCALE, mask[:, 0, :],
                                               ALU.mult, ALU.add).then_inc(s.score_free, 1)
                        v.wait_ge(s.score_free, b * RT + r + 3)
                        v.tensor_reduce(nmax[:, r % 2:r % 2 + 1], sc[:, r % 2, :], AX.X, ALU.max, negate=True)\
                            .then_inc(s.rowmax, 1)

                    def softmax_tail(r):
                        v.wait_ge(s.exp_done, b * RT + r + 1)
                        v.reciprocal(rsum[:, r % 2:r % 2 + 1], rsum[:, r % 2:r % 2 + 1]).then_inc(s.sm, 1)
                        v.wait_ge(s.sm, b * RT + r + 1)
                        v.tensor_scalar(pr[:, r % 2, :], pr[:, r % 2, :], rsum[:, r % 2:r % 2 + 1], None, ALU.mult)\
                            .then_inc(s.prob_ready, 1)

                    for r in range(RT + 1):
                        if r < RT:
                            softmax_head(r)
                        if r > 0:
                            softmax_tail(r - 1)
                    v.wait_ge(s.prob_ready, b * RT + RT)

            @block.scalar
            def _(act):
                act.sem_inc(s.pT_ready, 1)
                act.sem_inc(s.out_free, 4)
                with act.Fori(0, HALF_B) as b:
                    for c in range(CC):
                        act.wait_ge(s.kv_done, b * CC + c + 1)
                        act.activation(kvT[:, c, :], ps[c][:], ACT.Copy).then_inc(s.kvT_ready, 1)
                    act.wait_ge(s.kvx_done, b + 1)
                    for i in range(2):
                        act.activation(kv[:, 2 * i:2 * i + 2, :], ps[3 + i][:].rearrange("p (k c) -> p k c", c=KVC),
                                       ACT.Copy).then_inc(s.kv_ready, 1)

                    def exps(r):
                        act.wait_ge(s.prob_free, b * RT + r + 1)
                        act.wait_ge(s.rowmax, b * RT + r + 1)
                        act.activation(pr[:, r % 2, :], sc[:, r % 2, :], ACT.Exp, bias=nmax[:, r % 2:r % 2 + 1],
                                       scale=1.0, accum_out=rsum[:, r % 2:r % 2 + 1]).then_inc(s.exp_done, 1)

                    def take_pT(r):
                        act.wait_ge(s.prob_free, b * RT + r + 3)
                        act.activation(pT[:, :, r * P:(r + 1) * P], ps[7][:].rearrange("p (k m) -> p k m", m=P),
                                       ACT.Copy).then_inc(s.pT_ready, 1)

                    for r in range(RT + 1):
                        if r < RT:
                            exps(r)
                        if r > 0:
                            take_pT(r - 1)
                        if r > 0 and r % 4 == 0:
                            n = r // 4 - 1
                            for c in range(CC):
                                act.wait_ge(s.out_done, b * 4 + n * 2 + c + 1)
                                act.activation(qa[:, c, bass.ds(b, 1), n * 8:n * 8 + 8, :].rearrange("p b h q -> p b (h q)"),
                                               ps[OUT_BANK[n][c]][:].rearrange("p (b r) -> p b r", b=1), ACT.Copy)\
                                    .then_inc(s.out_free, 1)

            @block.tensor
            def _(pe):
                pe.sem_inc(s.ctx_free, 1)
                pe.sem_inc(s.prob_free, 2)
                pe.wait_ge(s.w_in, 32)
                with pe.Fori(0, HALF_B) as b:
                    pe.wait_ge(s.ctx_in, b * 16 + 16)
                    pe.wait_ge(s.out_free, 4 * b + 4)
                    for c in range(CC):
                        for k in range(KC):
                            mm = pe.matmul(ps[c][:], wkvc[:, k, c * P:(c + 1) * P], cT[:, k, :],
                                           start=(k == 0), stop=(k == KC - 1))
                        mm.then_inc(s.kv_done, 1)
                    pe.wait_ge(s.kvT_ready, CC * b + CC)
                    pe.sem_inc(s.ctx_free, 1)
                    pe.wait_ge(s.kr_free, b + 1)
                    for c in range(CC):
                        mm = pe.matmul(ps[2][:], wkr[:, c, :], kvT[:, c, :], start=(c == 0), stop=(c == CC - 1))
                    mm.then_inc(s.kr_done, 1)
                    for k in range(4):
                        for c in range(CC):
                            mm = pe.transpose(ps[3 + k // 2][:, (k % 2) * KVC + c * P:(k % 2) * KVC + (c + 1) * P],
                                              kvT[:, c, k * P:(k + 1) * P], ident)
                    mm.then_inc(s.kvx_done, 1)
                    pe.wait_ge(s.q_staged, 3 * b + 3)
                    pe.wait_ge(s.kr_ready, b + 1)

                    def scores(r):
                        pe.wait_ge(s.score_free, b * RT + r + 1)
                        for c in range(CC):
                            pe.matmul(ps[SC_BANK[r % 2]][:], qs[:, c, r * P:(r + 1) * P], kvT[:, c, :],
                                      start=(c == 0), stop=False)
                        mm = pe.matmul(ps[SC_BANK[r % 2]][:], qrs[:, r * P:(r + 1) * P], kr[:], start=False, stop=True)
                        mm.then_inc(s.score_done, 1)

                    def turn(r):
                        pe.wait_ge(s.prob_ready, b * RT + r + 1)
                        pe.wait_ge(s.pT_ready, b * RT + r + 1)
                        for k in range(4):
                            mm = pe.transpose(ps[7][:, k * P:(k + 1) * P], pr[:, r % 2, k * P:(k + 1) * P], ident)
                        mm.then_inc(s.prob_free, 1)

                    def weighted(n):
                        pe.wait_ge(s.pT_ready, b * RT + 4 * n + 5)
                        for c in range(CC):
                            for k in range(4):
                                mm = pe.matmul(ps[OUT_BANK[n][c]][:], kv[:, k, c * P:(c + 1) * P],
                                               pT[:, k, n * 512:(n + 1) * 512], start=(k == 0), stop=(k == 3))
                            mm.then_inc(s.out_done, 1)

                    scores(0)
                    scores(1)
                    pe.wait_ge(s.kv_ready, 2 * b + 2)
                    for r in range(RT):
                        turn(r)
                        if r + 2 < RT:
                            scores(r + 2)
                        if r == 3:
                            weighted(0)
                    weighted(1)


def merge(nc, ps, d, half, qa):
    with ExitStack() as ctx:
        sb = lambda n, s, t=F32: ctx.enter_context(nc.sbuf_tensor(f"m{half}_{n}", s, t))
        s = semaphores(nc, ctx, f"m{half}", "wo_in wv_in0 wv_in1 wv_free o_done o_ready x_in x_free y_done y_ready st0 st1")
        wo = sb("wo", [P, XH, D])
        wv = [sb(f"wv{i}", [P, CC * P]) for i in range(2)]
        oT = sb("oT", [P, XH, HT])
        x = sb("x", [P, D])
        y = [sb(f"y{i}", [P, D]) for i in range(2)]
        wv_in = (s.wv_in0, s.wv_in1)
        st = (s.st0, s.st1)
        TILES = HT // P
        with nc.Block() as block:

            @block.sync
            def _(sp):
                with sp.Fori(0, XH // 2) as hp:
                    for i in range(2):
                        sp.wait_ge(s.wv_free, hp * 2 + i + 1)
                        sp.dma_start(wv[i][:], d.head_v[hp * 2 + i]).then_inc(wv_in[i], 16)
                for t in range(TILES):
                    sp.wait_ge(s.x_free, t + 1)
                    sp.dma_start(x[:], d.x[half * HT + t * P:half * HT + (t + 1) * P, :]).then_inc(s.x_in, 16)

            @block.gpsimd
            def _(g):
                g.dma_start(wo[:], d.wo.rearrange("(h p) n -> p h n", p=P)).then_inc(s.wo_in, 16)

            @block.vector
            def _(v):
                v.sem_inc(s.x_free, 1)
                for t in range(TILES):
                    v.wait_ge(s.x_in, 16 * (t + 1))
                    if t >= 2:
                        v.wait_ge(st[t % 2], 16 * (t // 2))
                    for n in range(2):
                        v.wait_ge(s.y_done, 2 * t + n + 1)
                        a = v.tensor_tensor(y[t % 2][:, n * 512:(n + 1) * 512], ps[2 * (t % 2) + n][:],
                                            x[:, n * 512:(n + 1) * 512], ALU.add)
                        a.then_inc(s.y_ready, 1)
                    v.wait_ge(s.y_ready, 2 * t + 2)
                    v.sem_inc(s.x_free, 1)

            @block.scalar
            def _(act):
                act.sem_inc(s.o_ready, 2)
                act.sem_inc(s.wv_free, 2)
                with act.Fori(0, XH // 2) as hp:
                    for i in range(2):
                        h = hp * 2 + i
                        act.wait_ge(s.o_done, h + 1)
                        act.sem_inc(s.wv_free, 1)
                        act.activation(oT[:, bass.ds(h, 1), :].rearrange("p h m -> p (h m)"), ps[4 + i][:], ACT.Copy)\
                            .then_inc(s.o_ready, 1)
                for t in range(TILES):
                    act.wait_ge(s.y_ready, 2 * t + 2)
                    act.dma_start(d.x1[half * HT + t * P:half * HT + (t + 1) * P, :], y[t % 2][:]).then_inc(st[t % 2], 16)
                for i in range(2):
                    act.wait_ge(st[i], 16 * (TILES // 2))

            @block.tensor
            def _(pe):
                with pe.Fori(0, XH // 2) as hp:
                    for i in range(2):
                        h = hp * 2 + i
                        pe.wait_ge(wv_in[i], hp * 16 + 16)
                        pe.wait_ge(s.o_ready, h + 1)
                        for c in range(CC):
                            mm = pe.matmul(ps[4 + i][:], wv[i][:, c * P:(c + 1) * P],
                                           qa[:, c, :, bass.ds(h, 1), :].rearrange("p b h q -> p b (h q)"),
                                           start=(c == 0), stop=(c == CC - 1))
                        mm.then_inc(s.o_done, 1)
                pe.wait_ge(s.wo_in, 16)
                pe.wait_ge(s.o_ready, XH + 2)
                for t in range(TILES):
                    if t >= 2:
                        pe.wait_ge(s.y_ready, 2 * (t - 1))
                    for n in range(2):
                        for h in range(XH):
                            mm = pe.matmul(ps[2 * (t % 2) + n][:], oT[:, h, t * P:(t + 1) * P],
                                           wo[:, h, n * 512:(n + 1) * 512], start=(h == 0), stop=(h == XH - 1))
                        mm.then_inc(s.y_done, 1)


def norm_tile(v, x, stats, mv, sd, rstd, xn, s, t, loads=1):
    v.wait_ge(s.x_in, t * (16 * loads) + 16 * loads)
    layernorm_steps(v, x, stats, mv, sd, rstd, xn, s, t)


def heads(nc, ps, d, ident):
    with ExitStack() as ctx:
        sb = lambda n, s, t=F32: ctx.enter_context(nc.sbuf_tensor(f"h_{n}", s, t))
        s = semaphores(nc, ctx, "h", "gspare pspare wq_in wk_in wv_in c_in x_in x_free xn_ready xn_free ln sq spare x_psum_free proj_done"
                       " proj_free q_sum q_rot k_sum k_rot v_sum ring_done ring_free score_done score_free mx"
                       " shifted exp_done sm sm2 prob_ready o_st o_free")
        w = [sb(f"w{n}", [P, KC, D]) for n in "qkv"]
        bias = [sb(f"b{n}", [P, D]) for n in "qkv"]
        cos = sb("cos", [P, D])
        sin = sb("sin", [P, D])
        bmask = sb("bmask", [P, 512])
        x = sb("x", [P, D])
        xn = sb("xn", [P, D])
        xT = sb("xT", [P, KC, P])
        stats = sb("stats", [P, 2, 6])
        mv = sb("mv", [P, 2])
        rstd = sb("rstd", [P, 1])
        sd = sb("sd", [P, 1])
        qkv = [sb(f"t{n}", [P, D]) for n in "qkv"]
        swp = [sb(f"s{n}", [P, D]) for n in "qk"]
        hT = [sb(f"T{n}", [DH, 16, NH, 8]) for n in "qkv"]
        sc = sb("sc", [P, 2, 4, P])
        rmax = sb("rmax", [P, 2, 4])
        rsum = sb("rsum", [P, 4, 4])
        pr = sb("pr", [P, 4, 512])
        pT = sb("pT", [P, 4, 512])
        vg = sb("vg", [P, 16, DH])
        og = sb("og", [P, 16, DH])
        RING = 20

        def rotate(eng, n, start, done, t):
            a, b = qkv[n], swp[n]
            v4 = lambda z: z[:].rearrange("p (h i j) -> p h i j", i=2, j=DH // 2)
            eng.wait_ge(start, 2 * t + 2)
            eng.tensor_tensor(v4(b)[:, :, 0, :], v4(a)[:, :, 1, :], v4(sin)[:, :, 0, :], ALU.mult)
            eng.tensor_tensor(v4(b)[:, :, 1, :], v4(a)[:, :, 0, :], v4(sin)[:, :, 1, :], ALU.mult).then_inc(done, 1)
            eng.wait_ge(done, 3 * t + 1)
            eng.tensor_tensor(a[:], a[:], cos[:], ALU.mult).then_inc(done, 1)
            eng.wait_ge(done, 3 * t + 2)
            eng.tensor_tensor(a[:], a[:], b[:], ALU.add).then_inc(done, 1)

        def tiles(engine, body):
            body(0, None)
            with engine.Fori(0, TT - 1) as t:
                body(t + 1, t)
            body(None, TT - 1)

        with nc.Block() as block:

            @block.sync
            def _(sp):
                for n, src in enumerate((d.bq, d.bk, d.bv)):
                    sp.dma_start(bias[n][:], src[:, :]).then_inc(s.c_in, 16)
                sp.dma_start(cos[:], d.cos2[:, :]).then_inc(s.c_in, 16)
                sp.dma_start(sin[:], d.sin2[:, :]).then_inc(s.c_in, 16)
                sp.dma_start(bmask[:], d.bmask[:, :]).then_inc(s.c_in, 16)
                src = d.x1.rearrange("(b t g) n -> b g t n", g=8, t=8)
                with sp.Fori(0, TT) as t:
                    sp.wait_ge(s.x_free, t + 1)
                    for b in range(2):
                        sp.dma_start(x[b * LQ:(b + 1) * LQ, :], src[2 * t + b]).then_inc(s.x_in, 16)

            @block.gpsimd
            def _(g):
                for n, (src, sem) in enumerate(((d.wq, s.wq_in), (d.wk, s.wk_in), (d.wv, s.wv_in))):
                    g.dma_start(w[n][:], src.rearrange("(k p) n -> p k n", p=P)).then_inc(sem, 16)
                g.sem_inc(s.o_free, 1)
                g.wait_ge(s.c_in, 16 * 6)

                def body(p, a):
                    if p is not None:
                        rotate(g, 1, s.k_sum, s.k_rot, p)
                    if a is not None:
                        hold(g, s.ring_free, RING * a + 24, s.gspare)
                        g.dma_start((d.o2[2 * a:2 * a + 2] if isinstance(a, int) else d.o2[bass.ds(a * 2, 2)])
                                    .rearrange("b p n -> p b n"),
                                    og[:].rearrange("p (b g) n -> p b (g n)", b=2)).then_inc(s.o_st, 16)
                        g.wait_ge(s.o_st, a * 16 + 16)
                        g.sem_inc(s.o_free, 1)

                tiles(g, body)

            @block.vector
            def _(v):
                v.sem_inc(s.x_free, 1)
                v.sem_inc(s.proj_free, 2)
                v.sem_inc(s.score_free, 4)
                norm_tile(v, x, stats, mv, sd, rstd, xn, s, 0, 2)
                v.wait_ge(s.c_in, 16 * 6)

                def add_bias(p, a, g):
                    n, h = g // 2, g % 2
                    if a is not None and h == 0:
                        v.wait_ge(s.ring_done, RING * a + 4 * (n + 1))
                    v.wait_ge(s.proj_done, 6 * p + g + 1)
                    add = v.tensor_tensor(qkv[n][:, h * 512:(h + 1) * 512], ps[2 + h][:],
                                          bias[n][:, h * 512:(h + 1) * 512], ALU.add)
                    add.then_inc(s.proj_free, 1)
                    v.wait_ge(s.proj_free, 6 * p + g + 3)
                    v.sem_inc((s.q_sum, s.k_sum, s.v_sum)[n], 1)

                def head(a, i):
                    k = i % 2
                    v.wait_ge(s.score_done, 4 * a + i + 1)
                    v.tensor_tensor(sc[:, k].rearrange("p g m -> p (g m)"), ps[4 + i][:], bmask[:], ALU.add)\
                        .then_inc(s.score_free, 1)
                    v.wait_ge(s.score_free, 4 * a + i + 5)
                    v.tensor_reduce(rmax[:, k, :], sc[:, k], AX.X, ALU.max).then_inc(s.mx, 1)
                    v.wait_ge(s.mx, 4 * a + i + 1)
                    v.tensor_tensor(sc[:, k], sc[:, k], rmax[:, k, :].unsqueeze(2).broadcast_to([P, 4, P]), ALU.subtract)\
                        .then_inc(s.shifted, 1)

                def tail(a, i):
                    v.wait_ge(s.exp_done, 4 * a + i + 1)
                    e = pr[:, i, :].rearrange("p (g m) -> p g m", m=P)
                    v.tensor_reduce(rsum[:, i, :], e, AX.X, ALU.add).then_inc(s.sm, 1)
                    v.wait_ge(s.sm, 4 * a + i + 1)
                    v.reciprocal(rsum[:, i, :], rsum[:, i, :]).then_inc(s.sm2, 1)
                    v.wait_ge(s.sm2, 4 * a + i + 1)
                    v.tensor_tensor(e, e, rsum[:, i, :].unsqueeze(2).broadcast_to([P, 4, P]), ALU.mult)\
                        .then_inc(s.prob_ready, 1)

                def body(p, a):
                    if p is not None:
                        add_bias(p, a, 0)
                        add_bias(p, a, 1)
                    if a is not None:
                        head(a, 0)
                        for i in range(4):
                            if i < 3:
                                head(a, i + 1)
                            tail(a, i)
                    if p is not None:
                        add_bias(p, a, 2)
                        add_bias(p, a, 3)
                        rotate(v, 0, s.q_sum, s.q_rot, p)
                        add_bias(p, a, 4)
                        add_bias(p, a, 5)
                        if a is None:
                            norm_tile(v, x, stats, mv, sd, rstd, xn, s, 1, 2)

                body(0, None)
                with v.Fori(0, TT - 2) as t:
                    body(t + 1, t)
                    norm_tile(v, x, stats, mv, sd, rstd, xn, s, t + 2, 2)
                body(TT - 1, TT - 2)
                body(None, TT - 1)

            @block.scalar
            def _(act):
                act.sem_inc(s.x_psum_free, 1)
                act.sem_inc(s.ring_free, 4)

                def root(t):
                    act.wait_ge(s.sq, 3 * t + 1)
                    act.activation(sd[:], rstd[:], ACT.Sqrt).then_inc(s.sq, 1)

                def take_x(p):
                    act.wait_ge(s.xn_free, p + 2)
                    for i in range(2):
                        cp = act.activation(xT[:, 4 * i:4 * i + 4, :], ps[i][:].rearrange("p (k m) -> p k m", m=P), ACT.Copy)
                    cp.then_inc(s.x_psum_free, 1)

                def take(a, n, dst, src):
                    act.wait_ge(s.ring_done, RING * a + n + 1)
                    act.activation(dst, src, ACT.Copy).then_inc(s.ring_free, 1)

                def take_heads(a, n):
                    for i in range(4):
                        take(a, 4 * n + i, hT[n][:, :, 4 * i:4 * i + 4, :].rearrange("p g h t -> p h g t"),
                             ps[4 + i][0:DH, :].rearrange("p (h g t) -> p h g t", g=16, t=8))

                def body(p, a, norm):
                    if p is not None:
                        take_x(p)
                    if a is not None:
                        take_heads(a, 0)
                        take_heads(a, 1)
                        for i in range(4):
                            act.wait_ge(s.shifted, 4 * a + i + 1)
                            act.activation(pr[:, i, :], sc[:, i % 2].rearrange("p g m -> p (g m)"), ACT.Exp,
                                           scale=DH ** -0.5).then_inc(s.exp_done, 1)
                        take_heads(a, 2)
                    if norm is not None:
                        root(norm)
                    if a is not None:
                        for i in range(4):
                            take(a, 12 + i, pT[:, i, :], ps[4 + i][:])
                        for i in range(2):
                            take(a, 16 + i, vg[:, 8 * i:8 * i + 8, :].rearrange("p g n -> p (g n)"), ps[4 + i][:])
                        act.wait_ge(s.o_free, a + 1)
                        for i in range(2):
                            take(a, 18 + i, og[:, 8 * i:8 * i + 8, :].rearrange("p g n -> p (g n)"), ps[6 + i][:])

                root(0)
                body(0, None, 1)
                with act.Fori(0, TT - 2) as t:
                    body(t + 1, t, t + 2)
                body(TT - 1, TT - 2, None)
                body(None, TT - 1, None)

            @block.tensor
            def _(pe):
                pe.sem_inc(s.xn_free, 1)

                def project(p, g):
                    if isinstance(p, int) and p == 0 and g % 2 == 0:
                        pe.wait_ge((s.wq_in, s.wk_in, s.wv_in)[g // 2], 16)
                    if g == 0:
                        pe.wait_ge(s.x_psum_free, p + 2)
                    pe.wait_ge(s.proj_free, 6 * p + g + 1)
                    n, h = g // 2, g % 2
                    for k in range(KC):
                        mm = pe.matmul(ps[2 + h][:], xT[:, k, :], w[n][:, k, h * 512:(h + 1) * 512],
                                       start=(k == 0), stop=(k == KC - 1))
                    mm.then_inc(s.proj_done, 1)

                def turn(a, n):
                    if n == 0:
                        pe.wait_ge(s.q_rot, 3 * a + 3)
                    elif n == 1:
                        pe.wait_ge(s.k_rot, 3 * a + 3)
                    else:
                        pe.wait_ge(s.v_sum, 2 * a + 2)
                    for i in range(4):
                        if n < 2:
                            hold(pe, s.ring_free, RING * a + 4 * n + i + 1, s.pspare)
                        else:
                            hold(pe, s.score_free, 4 * a + i + 5, s.pspare)
                        for j in range(4):
                            h = 4 * i + j
                            mm = pe.transpose(ps[4 + i][0:DH, j * P:(j + 1) * P], qkv[n][:, h * DH:(h + 1) * DH], ident)
                        mm.then_inc(s.ring_done, 1)

                group = lambda z, g: z[:, g].rearrange("p h t -> p (h t)")

                def body(p, a):
                    if p is not None:
                        pe.wait_ge(s.x_psum_free, p + 1)
                        pe.wait_ge(s.xn_ready, p + 1)
                        for k in range(KC):
                            mm = pe.transpose(ps[k // 4][:, (k % 4) * P:(k % 4 + 1) * P], xn[:, k * P:(k + 1) * P], ident)
                        mm.then_inc(s.xn_free, 1)
                    if a is not None:
                        turn(a, 0)
                    if p is not None:
                        project(p, 0)
                    if a is not None:
                        turn(a, 1)
                    if p is not None:
                        project(p, 1)
                    if a is not None:
                        pe.wait_ge(s.ring_free, RING * a + 12)
                        for i in range(4):
                            for j in range(4):
                                mm = pe.matmul(ps[4 + i][:, j * P:(j + 1) * P], group(hT[0], 4 * i + j),
                                               group(hT[1], 4 * i + j), start=True, stop=True)
                            mm.then_inc(s.score_done, 1)
                    if p is not None:
                        project(p, 2)
                        project(p, 3)
                    if a is not None:
                        turn(a, 2)
                    if p is not None:
                        project(p, 4)
                    if a is not None:
                        for i in range(4):
                            pe.wait_ge(s.prob_ready, 4 * a + i + 1)
                            pe.wait_ge(s.ring_free, RING * a + 13 + i)
                            for j in range(4):
                                mm = pe.transpose(ps[4 + i][:, j * P:(j + 1) * P], pr[:, i, j * P:(j + 1) * P], ident)
                            mm.then_inc(s.ring_done, 1)
                    if p is not None:
                        project(p, 5)
                    if a is not None:
                        for i in range(2):
                            hold(pe, s.ring_free, RING * a + 17 + i, s.pspare)
                            for j in range(8):
                                mm = pe.transpose(ps[4 + i][:, j * DH:(j + 1) * DH], group(hT[2], 8 * i + j),
                                                  ident[0:DH, 0:DH])
                            mm.then_inc(s.ring_done, 1)
                        pe.wait_ge(s.ring_free, RING * a + 22)
                        for i in range(2):
                            for j in range(8):
                                g = 8 * i + j
                                mm = pe.matmul(ps[6 + i][:, j * DH:(j + 1) * DH], pT[:, g // 4, (g % 4) * P:(g % 4 + 1) * P],
                                               vg[:, g, :], start=True, stop=True)
                            mm.then_inc(s.ring_done, 1)

                tiles(pe, body)


def route(nc, ps, d, ident, bounds):
    with ExitStack() as ctx:
        sb = lambda n, s, t=F32: ctx.enter_context(nc.sbuf_tensor(f"r_{n}", s, t))
        s = semaphores(nc, ctx, "r", "gspare w_in g_in c_in z_ready z_st slots_st o_in o_free r_in r_free xb_ready turned"
                       " o_psum_free y_done y_free x_in x_free xn_ready xn_free ln sq spare x2_st x3_st"
                       " x_psum_free gate_done gate_taken st_free sig step pe_step scat gone")
        wo = sb("wo", [P, KC, D])
        gw = sb("gw", [P, KC, E])
        bo = sb("bo", [P, D])
        o = sb("o", [P, D])
        oT = sb("oT", [P, KC, P])
        x1 = sb("x1", [P, D])
        x = sb("x", [P, D])
        xn = sb("xn", [P, D])
        xT = sb("xT", [P, KC, P])
        stats = sb("stats", [P, 2, 6])
        mv = sb("mv", [P, 2])
        rstd = sb("rstd", [P, 1])
        sd = sb("sd", [P, 1])
        tri = sb("tri", [P, P])
        ones = sb("ones", [P, P])
        zero = sb("zero", [P, D])
        logit = sb("logit", [P, TT, E])
        prob = sb("prob", [P, TT, E])
        W8 = 48
        g16 = sb("g16", [P, TT, 16])
        g8 = sb("g8", [P, TT, 8])
        gm = sb("gm", [P, TT, 16])
        keep = sb("keep", [P, TT, NG, 2])
        ms = sb("ms", [P, TT, W8])
        t8 = sb("t8", [P, TT, 8])
        rep = sb("rep", [P, TT, W8])
        sel = sb("sel", [P, TT, E])
        cw = sb("cw", [P, TT, E])
        cs = sb("cs", [P, TT])
        rank = sb("rank", [P, TT, E])
        quo = sb("quo", [P, TT, E])
        cnt = sb("cnt", [P, E])
        ntile = sb("ntile", [P, E])
        cum = sb("cum", [P, E])
        base = sb("base", [P, E])
        slot = sb("slot", [P, TT, W8])
        s8 = sb("s8", [P, TT, 8])
        idx = sb("idx", [P, TT, TOP], I32)
        pay = sb("pay", [P, TT, TOP, 2])
        tmp = sb("tmp", [P, TT, E])
        tokens = sb("tokens", [P, TT, TOP], I32)
        o_rows = d.o2.rearrange("b p n -> (b p n)").rearrange("(r c) -> r c", c=D)
        with nc.Block() as block:

            @block.sync
            def _(sp):
                sp.dma_start(wo[:], d.wo2.rearrange("(k p) n -> p k n", p=P)).then_inc(s.w_in, 16)
                sp.dma_start(gw[:], d.gate_w.rearrange("(k p) n -> p k n", p=P)).then_inc(s.g_in, 16)
                sp.dma_start(bo[:], d.bo[:, :]).then_inc(s.c_in, 16)
                sp.dma_start(tri[:], d.tri[:, :]).then_inc(s.c_in, 16)
                sp.dma_start(ones[:], d.ones[:, :]).then_inc(s.c_in, 16)
                sp.dma_start(tokens[:], d.tokens[:, :, :]).then_inc(s.c_in, 16)
                sp.dma_start(d.slots[:, :], d.slots0[:, :]).then_inc(s.slots_st, 16)
                with sp.Fori(0, TT) as t:
                    sp.wait_ge(s.o_free, t + 1)
                    sp.dma_start(o[:], o_rows[bass.ds(t * P, P), :]).then_inc(s.o_in, 16)
                    sp.wait_ge(s.r_free, t + 1)
                    sp.dma_start(x1[:], d.x1[bass.ds(t * P, P), :]).then_inc(s.r_in, 16)
                sp.wait_ge(s.slots_st, 16)

            @block.gpsimd
            def _(g):
                g.memset(zero[:], 0.0).then_inc(s.z_ready, 1)
                g.wait_ge(s.z_ready, 1)
                g.dma_start(d.xn3[T:T + PAD, :], zero[:]).then_inc(s.z_st, 16)
                g.dma_start(d.acc[T:T + PAD, :], zero[:]).then_inc(s.z_st, 16)
                g.sem_inc(s.st_free, 1)
                g.wait_ge(s.c_in, 64)
                with g.Fori(0, TT) as t:
                    g.wait_ge(s.r_in, t * 16 + 16)
                    g.tensor_tensor(x1[:], x1[:], bo[:], ALU.add).then_inc(s.xb_ready, 1)
                    hold(g, s.y_free, 2 * t + 4, s.gspare)
                    g.dma_start(d.acc[bass.ds(t * P, P), :], x[:]).then_inc(s.x2_st, 16)
                    hold(g, s.xn_ready, t + 1, s.gspare)
                    g.dma_start(d.xn3[bass.ds(t * P, P), :], xn[:]).then_inc(s.x3_st, 16)
                    g.wait_ge(s.x2_st, t * 16 + 16)
                    g.wait_ge(s.x3_st, t * 16 + 16)
                    g.sem_inc(s.st_free, 1)
                g.wait_ge(s.z_st, 32)
                g.wait_ge(s.slots_st, 16)
                g.wait_ge(s.gone, 1)
                for t in range(TT):
                    for k in range(TOP):
                        g.indirect_dma_start(d.slots[:, :], bass.IndirectOffsetOnAxis(ap=idx[:, t, k:k + 1], axis=0),
                                             pay[:, t, k, :].bitcast(I32), None).then_inc(s.scat, 16)
                g.wait_ge(s.scat, 16 * TT * TOP)

            @block.vector
            def _(v):
                v.sem_inc(s.r_free, 1)
                v.sem_inc(s.y_free, 2)
                with v.Fori(0, TT) as t:
                    v.wait_ge(s.xb_ready, t + 1)
                    v.wait_ge(s.st_free, t + 1)
                    for h in range(2):
                        v.wait_ge(s.y_done, 2 * t + h + 1)
                        v.tensor_tensor(x[:, h * 512:(h + 1) * 512], ps[2 + h][:], x1[:, h * 512:(h + 1) * 512], ALU.add)\
                            .then_inc(s.y_free, 1)
                    v.wait_ge(s.y_free, 2 * t + 4)
                    v.sem_inc(s.r_free, 1)
                    layernorm_steps(v, x, stats, mv, sd, rstd, xn, s, t)

                n = [0]

                def link(op):
                    n[0] += 1
                    op.then_inc(s.step, 1)
                    v.wait_ge(s.step, n[0])

                v.memset(g16[:], -1.0)
                v.memset(ms[:], -2.0)
                link(v.memset(slot[:], 0.0))
                v.wait_ge(s.sig, 1)
                link(v.tensor_reduce(g16[:, :, 0:NG], prob[:].rearrange("p t (g e) -> p t g e", g=NG), AX.X, ALU.max))
                for t in range(TT):
                    op = v.max(g8[:, t, :], g16[:, t, :])
                link(op)
                link(v.memset(g8[:, :, KEEP_G:8], -1.0))
                for t in range(TT):
                    op = v.match_replace(gm[:, t, :], g8[:, t, :], g16[:, t, :], 2.0)
                link(op)
                link(v.tensor_scalar(keep[:, :, :, 0], gm[:, :, 0:NG], 2.0, None, ALU.is_equal))
                link(v.tensor_scalar(keep[:, :, :, 1], keep[:, :, :, 0], 1.0, None, ALU.subtract))
                grp = lambda z: z[:, :, 0:E].rearrange("p t (g e) -> p t g e", g=NG)
                for g in range(NG):
                    ks = [keep[:, :, g, i:i + 1].broadcast_to([P, TT, E // NG]) for i in range(2)]
                    e8 = slice(g * (E // NG), (g + 1) * (E // NG))
                    link(v.tensor_tensor(tmp[:, :, e8], prob[:, :, e8], ks[0], ALU.mult))
                    link(v.tensor_tensor(ms[:, :, e8], tmp[:, :, e8], ks[1], ALU.add))
                for t in range(TT):
                    op = v.max(t8[:, t, :], ms[:, t, :])
                link(op)
                link(v.memset(t8[:, :, TOP:8], -2.0))
                for t in range(TT):
                    op = v.match_replace(rep[:, t, :], t8[:, t, :], ms[:, t, :], 2.0)
                link(op)
                link(v.tensor_scalar(sel[:], rep[:, :, 0:E], 2.0, None, ALU.is_equal))
                v.sem_inc(s.pe_step, 1)
                link(v.tensor_tensor(cw[:], prob[:], sel[:], ALU.mult))
                link(v.tensor_reduce(cs[:], cw[:], AX.X, ALU.add))
                link(v.reciprocal(cs[:], cs[:]))
                link(v.tensor_tensor(cw[:], cw[:], cs[:].unsqueeze(2).broadcast_to([P, TT, E]), ALU.mult))
                v.wait_ge(s.pe_step, 3)
                v.tensor_copy(rank[:].rearrange("p t e -> p (t e)"), ps[0][:, 0:TT * E])
                link(v.tensor_copy(cnt[:], ps[1][:, 0:E]))
                v.memset(quo[:], 0.0)
                link(v.memset(ntile[:], 1.0))
                for j in range(1, T // P):
                    link(v.scalar_tensor_tensor(ntile[:], cnt[:], float(j * P), ntile[:], ALU.is_gt, ALU.add))
                    link(v.scalar_tensor_tensor(quo[:], rank[:], float(j * P), quo[:], ALU.is_ge, ALU.add))
                link(v.tensor_tensor_scan(cum[:], ones[:, 0:E], ntile[:], float(SH_TILES), ALU.mult, ALU.add))
                link(v.tensor_tensor(base[:], cum[:], ntile[:], ALU.subtract))
                v.memset(bounds[:, 0:1], 0)
                v.memset(bounds[:, 1:2], TT)
                v.memset(bounds[:, 2:3], SH_TILES)
                link(v.tensor_copy(bounds[:, 3:3 + E], cum[:]))
                link(v.tensor_scalar(rank[:], rank[:], float(NT), 1.0, ALU.mult, ALU.add))
                link(v.scalar_tensor_tensor(rank[:], quo[:], float(1 - P * NT), rank[:], ALU.mult, ALU.add))
                link(v.tensor_tensor(rank[:], rank[:], base[:].unsqueeze(1).broadcast_to([P, TT, E]), ALU.add))
                link(v.tensor_tensor(slot[:, :, 0:E], rank[:], sel[:], ALU.mult))
                for t in range(TT):
                    op = v.max(s8[:, t, :], slot[:, t, :])
                link(op)
                link(v.tensor_scalar(idx[:], s8[:, :, 0:TOP], 1.0, None, ALU.subtract))
                for k in range(TOP):
                    link(v.tensor_tensor(tmp[:], slot[:, :, 0:E], s8[:, :, k:k + 1].broadcast_to([P, TT, E]), ALU.is_equal))
                    link(v.tensor_tensor(tmp[:], tmp[:], cw[:], ALU.mult))
                    link(v.tensor_reduce(pay[:, :, k, 1], tmp[:], AX.X, ALU.add))
                link(v.tensor_copy(pay[:, :, :, 0].bitcast(I32), tokens[:]))
                v.sem_inc(s.gone, 1)

            @block.scalar
            def _(act):
                act.sem_inc(s.o_psum_free, 1)
                act.sem_inc(s.x_psum_free, 1)
                with act.Fori(0, TT) as t:
                    act.wait_ge(s.turned, t + 1)
                    for i in range(2):
                        cp = act.activation(oT[:, 4 * i:4 * i + 4, :], ps[i][:].rearrange("p (k m) -> p k m", m=P), ACT.Copy)
                    cp.then_inc(s.o_psum_free, 1)
                    act.wait_ge(s.sq, 3 * t + 1)
                    act.activation(sd[:], rstd[:], ACT.Sqrt).then_inc(s.sq, 1)
                    act.wait_ge(s.xn_free, t + 2)
                    for i in range(2):
                        cp = act.activation(xT[:, 4 * i:4 * i + 4, :], ps[4 + i][:].rearrange("p (k m) -> p k m", m=P), ACT.Copy)
                    cp.then_inc(s.x_psum_free, 1)
                    act.wait_ge(s.gate_done, t + 1)
                    act.activation(logit[:, bass.ds(t, 1), :].rearrange("p t e -> p (t e)"), ps[6][:, 0:E], ACT.Copy)\
                        .then_inc(s.gate_taken, 1)
                act.wait_ge(s.gate_taken, TT)
                act.activation(prob[:], logit[:], ACT.Sigmoid).then_inc(s.sig, 1)

            @block.tensor
            def _(pe):
                pe.sem_inc(s.xn_free, 1)
                pe.sem_inc(s.o_free, 1)
                pe.wait_ge(s.w_in, 16)
                pe.wait_ge(s.g_in, 16)
                with pe.Fori(0, TT) as t:
                    pe.wait_ge(s.o_in, t * 16 + 16)
                    pe.wait_ge(s.o_psum_free, t + 1)
                    for k in range(KC):
                        mm = pe.transpose(ps[k // 4][:, (k % 4) * P:(k % 4 + 1) * P], o[:, k * P:(k + 1) * P], ident)
                    mm.then_inc(s.turned, 1)
                    pe.wait_ge(s.o_psum_free, t + 2)
                    pe.sem_inc(s.o_free, 1)
                    for h in range(2):
                        pe.wait_ge(s.y_free, 2 * t + h + 1)
                        for k in range(KC):
                            mm = pe.matmul(ps[2 + h][:], oT[:, k, :], wo[:, k, h * 512:(h + 1) * 512],
                                           start=(k == 0), stop=(k == KC - 1))
                        mm.then_inc(s.y_done, 1)
                    pe.wait_ge(s.xn_ready, t + 1)
                    pe.wait_ge(s.x_psum_free, t + 1)
                    for k in range(KC):
                        mm = pe.transpose(ps[4 + k // 4][:, (k % 4) * P:(k % 4 + 1) * P], xn[:, k * P:(k + 1) * P], ident)
                    mm.then_inc(s.xn_free, 1)
                    pe.wait_ge(s.x_psum_free, t + 2)
                    for k in range(KC):
                        mm = pe.matmul(ps[6][:, 0:E], xT[:, k, :], gw[:, k, :], start=(k == 0), stop=(k == KC - 1))
                    mm.then_inc(s.gate_done, 1)
                pe.wait_ge(s.c_in, 64)
                pe.wait_ge(s.pe_step, 1)
                for t in range(TT):
                    for u in range(t):
                        pe.matmul(ps[0][:, t * E:(t + 1) * E], ones[:], sel[:, u, :], start=(u == 0), stop=False)
                    mm = pe.matmul(ps[0][:, t * E:(t + 1) * E], tri[:], sel[:, t, :], start=(t == 0), stop=True)
                mm.then_inc(s.pe_step, 1)
                for t in range(TT):
                    mm = pe.matmul(ps[1][:, 0:E], ones[:], sel[:, t, :], start=(t == 0), stop=(t == TT - 1))
                mm.then_inc(s.pe_step, 1)


def experts(nc, ps, d, ident, bounds):
    with ExitStack() as ctx:
        sb = lambda n, s, t=F32: ctx.enter_context(nc.sbuf_tensor(f"e_{n}", s, t))
        s = semaphores(nc, ctx, "e", "pspare gu_in0 gu_in1 dn_in0 dn_in1 tab_in x_in cols gate_done up_done up_free turned"
                       " xT_ready h_turned hT_ready down_done y_ready y_free y_st out_st gspare gcol silu_done")
        wg = [sb(f"wg{i}", [P, KC, F]) for i in range(2)]
        wu = [sb(f"wu{i}", [P, KC, F]) for i in range(2)]
        wd = [sb(f"wd{i}", [P, FC, D]) for i in range(2)]
        tab = sb("tab", [P, NT, 2], I32)
        gidx = sb("gidx", [P, 1], I32)
        sidx = sb("sidx", [P, 1], I32)
        wcol = sb("wcol", [P, 1])
        x = sb("x", [P, D])
        xT = sb("xT", [P, KC, P])
        g = sb("g", [P, F])
        h = sb("h", [P, F])
        hT = sb("hT", [P, FC, P])
        y = sb("y", [P, D])
        gu_in, dn_in = (s.gu_in0, s.gu_in1), (s.dn_in0, s.dn_in1)

        def each_tile(engine, before, body):
            with engine.Fori(0, NE // 2) as pair:
                for side in range(2):
                    first = engine.value_load(bounds[0:1, bass.ds(pair * 2 + side, 1)], min_val=0, max_val=MAX_TILES)
                    last = engine.value_load(bounds[0:1, bass.ds(pair * 2 + side + 1, 1)], min_val=1, max_val=MAX_TILES)
                    before(pair, side, first)
                    with engine.Fori(first, last) as i:
                        body(i, side)

        with nc.Block() as block:

            @block.sync
            def _(sp):
                def load(e, side, pair):
                    for j, (w, src) in enumerate(((wg[side], d.e_gate), (wg[side], d.e_gate), (wu[side], d.e_up), (wu[side], d.e_up))):
                        if j >= 1:
                            sp.wait_ge(gu_in[side], pair * 64 + 16 * j)
                        k = (j % 2) * 4
                        sp.dma_start(w[:, k:k + 4, :], src[e, k * P:(k + 4) * P, :].rearrange("(k p) n -> p k n", p=P))\
                            .then_inc(gu_in[side], 16)
                    sp.wait_ge(gu_in[side], pair * 64 + 64)
                    sp.dma_start(wd[side][:, 0:5, :], d.e_down[e, 0:640, :].rearrange("(k p) n -> p k n", p=P))\
                        .then_inc(dn_in[side], 16)
                    sp.dma_start(wd[side][0:64, 5, :], d.e_down[e, 640:F, :]).then_inc(dn_in[side], 16)

                load(0, 0, 0)
                load(1, 1, 0)
                with sp.Fori(0, NE // 2 - 1) as pair:
                    for side in range(2):
                        done = sp.value_load(bounds[0:1, bass.ds(pair * 2 + side + 1, 1)], min_val=1, max_val=MAX_TILES)
                        sp.wait_ge(s.down_done, done * 2)
                        load(pair * 2 + side + 2, side, pair + 1)
                total = sp.value_load(bounds[0:1, NE:NE + 1], min_val=1, max_val=MAX_TILES)
                sp.wait_ge(s.y_free, total + 1)
                sp.dma_start(d.out[:, :], d.acc[0:T, :]).then_inc(s.out_st, 16)
                sp.wait_ge(s.out_st, 16)

            @block.gpsimd
            def _(q):
                q.sem_inc(s.y_free, 1)
                q.dma_start(tab[:], d.slots.rearrange("(p t) c -> p t c", p=P)).then_inc(s.tab_in, 16)
                q.wait_ge(s.tab_in, 16)

                def gather(i):
                    q.tensor_copy(gidx[:], tab[:, i:i + 1, 0] if isinstance(i, int) else tab[:, bass.ds(i, 1), 0])\
                        .then_inc(s.gcol, 1)
                    hold(q, s.gcol, i + 1, s.gspare)
                    q.indirect_dma_start(x[:], None, d.xn3[:, :], bass.IndirectOffsetOnAxis(ap=gidx[:, 0:1], axis=0))\
                        .then_inc(s.x_in, 16)

                gather(0)
                hold(q, s.x_in, 16, s.gspare)
                hold(q, s.turned, 2, s.gspare)
                gather(1)

                def body(i, side):
                    q.tensor_copy(sidx[:], tab[:, bass.ds(i, 1), 0])
                    q.tensor_copy(wcol[:].bitcast(I32), tab[:, bass.ds(i, 1), 1]).then_inc(s.cols, 1)
                    hold(q, s.cols, i + 1, s.gspare)
                    hold(q, s.x_in, i * 16 + 32, s.gspare)
                    hold(q, s.turned, i * 2 + 4, s.gspare)
                    gather(i + 2)
                    hold(q, s.y_ready, i * 2 + 2, s.gspare)
                    q.indirect_dma_start(d.acc[:, :], bass.IndirectOffsetOnAxis(ap=sidx[:, 0:1], axis=0), y[:], None,
                                         compute_op=ALU.add).then_inc(s.y_st, 16)
                    q.wait_ge(s.y_st, i * 16 + 16)
                    q.sem_inc(s.y_free, 1)

                each_tile(q, lambda *_: None, body)
                total = q.value_load(bounds[0:1, NE:NE + 1], min_val=1, max_val=MAX_TILES)
                q.wait_ge(s.x_in, total * 16 + 32)

            @block.vector
            def _(v):
                v.sem_inc(s.up_free, 2)

                def take_turned(tile):
                    v.wait_ge(s.turned, 2 * tile + 2)
                    v.tensor_copy(xT[:, 4:8, :], ps[7][:].rearrange("p (k m) -> p k m", m=P)).then_inc(s.xT_ready, 1)

                take_turned(0)

                def body(i, side):
                    for n in range(2):
                        v.wait_ge(s.silu_done, 2 * i + n + 1)
                        v.wait_ge(s.up_done, 2 * i + n + 1)
                        v.tensor_tensor(h[:, n * FH:(n + 1) * FH], g[:, n * FH:(n + 1) * FH], ps[2 + n][:, 0:FH], ALU.mult)\
                            .then_inc(s.up_free, 1)
                    v.wait_ge(s.h_turned, i + 1)
                    v.tensor_copy(hT[:, 4, :], ps[1][:, 0:P])
                    v.tensor_copy(hT[0:64, 5, :], ps[1][0:64, P:2 * P]).then_inc(s.hT_ready, 1)
                    take_turned(i + 1)
                    v.wait_ge(s.cols, i + 1)
                    v.wait_ge(s.y_free, i + 1)
                    v.wait_ge(s.down_done, 2 * i + 2)
                    v.tensor_scalar(y[:, 512:D], ps[5][:], wcol[:, 0:1], None, ALU.mult).then_inc(s.y_ready, 1)

                each_tile(v, lambda *_: None, body)

            @block.scalar
            def _(act):
                def take_turned(tile):
                    act.wait_ge(s.turned, 2 * tile + 1)
                    act.activation(xT[:, 0:4, :], ps[6][:].rearrange("p (k m) -> p k m", m=P), ACT.Copy).then_inc(s.xT_ready, 1)

                take_turned(0)

                def body(i, side):
                    for n in range(2):
                        act.wait_ge(s.gate_done, 2 * i + n + 1)
                        act.wait_ge(s.up_free, 2 * i + n + 1)
                        act.activation(g[:, n * FH:(n + 1) * FH], ps[n][:, 0:FH], ACT.Silu).then_inc(s.silu_done, 1)
                    take_turned(i + 1)
                    act.wait_ge(s.h_turned, i + 1)
                    act.activation(hT[:, 0:4, :], ps[0][:].rearrange("p (k m) -> p k m", m=P), ACT.Copy).then_inc(s.hT_ready, 1)
                    act.wait_ge(s.cols, i + 1)
                    act.wait_ge(s.y_free, i + 1)
                    act.wait_ge(s.down_done, 2 * i + 1)
                    act.activation(y[:, 0:512], ps[4][:], ACT.Copy, scale=wcol[:, 0:1]).then_inc(s.y_ready, 1)

                each_tile(act, lambda *_: None, body)

            @block.tensor
            def _(pe):
                def turn_tokens(i, half):
                    if half == 0:
                        pe.wait_ge(s.x_in, i * 16 + 16)
                    for k in range(4 * half, 4 * half + 4):
                        mm = pe.transpose(ps[6 + half][:, (k % 4) * P:(k % 4 + 1) * P], x[:, k * P:(k + 1) * P], ident)
                    mm.then_inc(s.turned, 1)

                turn_tokens(0, 0)
                turn_tokens(0, 1)

                pe.sem_inc(s.hT_ready, 2)

                def before(pair, side, first):
                    pe.wait_ge(gu_in[side], pair * 64 + 64)
                    hold(pe, dn_in[side], pair * 32 + 32, s.pspare)

                def body(i, side):
                    pe.wait_ge(s.xT_ready, 2 * i + 2)
                    for w, bank, done in ((wg[side], 0, s.gate_done), (wu[side], 2, s.up_done)):
                        for n in range(2):
                            if bank:
                                pe.wait_ge(s.up_free, 2 * i + n + 1)
                            else:
                                pe.wait_ge(s.hT_ready, 2 * i + 2)
                            for k in range(KC):
                                mm = pe.matmul(ps[bank + n][:, 0:FH], xT[:, k, :], w[:, k, n * FH:(n + 1) * FH],
                                               start=(k == 0), stop=(k == KC - 1))
                            mm.then_inc(done, 1)
                    turn_tokens(i + 1, 0)
                    pe.wait_ge(s.up_free, 2 * i + 4)
                    for k in range(FC):
                        mm = pe.transpose(ps[k // 4][0:FCW[k], (k % 4) * P:(k % 4 + 1) * P],
                                          h[:, k * P:k * P + FCW[k]], ident)
                    mm.then_inc(s.h_turned, 1)
                    turn_tokens(i + 1, 1)
                    pe.wait_ge(s.hT_ready, 2 * i + 4)
                    for n in range(2):
                        for k in range(FC):
                            mm = pe.matmul(ps[4 + n][:], hT[0:FCW[k], k, :], wd[side][0:FCW[k], k, n * 512:(n + 1) * 512],
                                           start=(k == 0), stop=(k == FC - 1))
                        mm.then_inc(s.down_done, 1)

                each_tile(pe, before, body)


def program(nc, d, stages="ahrm"):
    with ExitStack() as ctx:
        ps = [ctx.enter_context(nc.psum_tensor(f"bank{i}", [P, 512], F32)) for i in range(8)]
        ident = ctx.enter_context(nc.sbuf_tensor("ident", [P, P], F32))
        const_in = nc.alloc_semaphore("const_in")
        with nc.Block() as block:

            @block.sync
            def _(sp):
                sp.dma_start(ident[:], d.ident[:, :]).then_inc(const_in, 16)
                sp.wait_ge(const_in, 16)

        for half in range(2):
            with nc.sbuf_tensor(f"a{half}_qa", [P, CC, HALF_B, XH, LQ], F32) as qa:
                with ExitStack() as a:
                    sb = lambda n, s: a.enter_context(nc.sbuf_tensor(f"a{half}_{n}", s, F32))
                    qr = sb("qr", [R, HALF_B, XH, LQ])
                    cst = named({"rope_q": sb("rope_q", [P, HT]), "rope_k": sb("rope_k", [P, LK]), "iota": sb("iota", [P, LK])})
                    cin = nc.alloc_semaphore(f"a{half}_const_in")
                    with nc.Block() as block:

                        @block.sync
                        def _(sp):
                            sp.dma_start(cst.rope_q[:], d.rope_q[:, :]).then_inc(cin, 16)
                            sp.dma_start(cst.rope_k[:], d.rope_k[:, :]).then_inc(cin, 16)
                            sp.dma_start(cst.iota[:], d.iota[:, :]).then_inc(cin, 16)
                            sp.wait_ge(cin, 48)

                    queries(nc, ps, d, half, qa, qr, ident[:], cst)
                    contexts(nc, ps, d, half, qa, qr, ident[:], cst)
                merge(nc, ps, d, half, qa)
        if "h" in stages:
            heads(nc, ps, d, ident[:])
        if "r" in stages:
            with ExitStack() as m:
                bounds = m.enter_context(nc.sbuf_tensor("bounds", [P, NE + 1], I32))
                route(nc, ps, d, ident[:], bounds)
                if "m" in stages:
                    experts(nc, ps, d, ident[:], bounds)


def laid_out(x, ctx_2048, itok_BxS_0_1023, L0_xattn_W_kvc, L0_xattn_W_dq, L0_xattn_W_uq, L0_xattn_W_qr, L0_xattn_W_uk,
             L0_xattn_W_kr, L0_xattn_W_uv, L0_xattn_W_o, L0_attn_Wq, L0_attn_bq, L0_attn_Wk, L0_attn_bk, L0_attn_Wv,
             L0_attn_bv, L0_attn_Wo, L0_attn_bo, L0_ffn_gate_w, L0_ffn_w_gate, L0_ffn_w_up, L0_ffn_w_down,
             L0_ffn_sw_gate, L0_ffn_sw_up, L0_ffn_sw_down):
    c = np.ascontiguousarray
    o = {}
    o["x"] = np.asarray(x).reshape(T, D)
    o["ctxT"] = c(np.asarray(ctx_2048).transpose(0, 2, 1))
    seg = np.asarray(itok_BxS_0_1023).T
    o["seg"] = c(np.concatenate([seg, seg], 0))
    o["wkvc"], o["wdq"] = np.asarray(L0_xattn_W_kvc), np.asarray(L0_xattn_W_dq)
    uq = np.asarray(L0_xattn_W_uq).reshape(QCC, P, XH, HD).transpose(2, 1, 0, 3)
    qr = np.asarray(L0_xattn_W_qr).reshape(QCC, P, XH, 2, R // 2).transpose(2, 1, 0, 3, 4)
    qr = np.concatenate([qr, qr[..., ::-1, :]], 3).reshape(XH, P, QCC, P)
    uk = np.asarray(L0_xattn_W_uk).reshape(KVC, XH, HD).transpose(1, 2, 0)
    o["head_w"] = c(np.concatenate([uq.reshape(XH, P, QCC * P), qr.reshape(XH, P, QCC * P), uk], 2))
    kr = np.asarray(L0_xattn_W_kr)
    o["wkr"] = c(np.concatenate([kr, kr[:, R // 2:], kr[:, :R // 2]], 1))
    o["head_v"] = c(np.asarray(L0_xattn_W_uv).reshape(CC, P, XH, HD).transpose(2, 1, 0, 3).reshape(XH, P, CC * P))
    o["wo"] = np.asarray(L0_xattn_W_o)
    split = lambda a: a.reshape((NH, DH // 2, 2) + a.shape[1:]).swapaxes(1, 2).reshape(a.shape)
    o["wq"], o["wk"] = c(split(np.asarray(L0_attn_Wq)).T), c(split(np.asarray(L0_attn_Wk)).T)
    o["wv"], o["wo2"] = c(np.asarray(L0_attn_Wv).T), c(np.asarray(L0_attn_Wo).T)
    rows = lambda a: c(np.broadcast_to(a, (P, D)))
    o["bq"], o["bk"] = rows(split(np.asarray(L0_attn_bq))), rows(split(np.asarray(L0_attn_bk)))
    o["bv"], o["bo"] = rows(np.asarray(L0_attn_bv)), rows(np.asarray(L0_attn_bo))
    cat = np.concatenate
    halves = lambda a: [np.asarray(a)[None, :, :F], np.asarray(a)[None, :, F:]]
    o["gate_w"] = np.asarray(L0_ffn_gate_w)
    o["e_gate"] = cat(halves(L0_ffn_sw_gate) + [np.asarray(L0_ffn_w_gate)])
    o["e_up"] = cat(halves(L0_ffn_sw_up) + [np.asarray(L0_ffn_w_up)])
    o["e_down"] = cat([np.asarray(L0_ffn_sw_down).reshape(SHARED, F, D), np.asarray(L0_ffn_w_down)])

    o["ident"] = np.eye(P, dtype=np.float32)
    o["iota"] = c(np.broadcast_to(np.arange(LK, dtype=np.float32), (P, LK)))

    def angles(half, length):
        inv = (np.float32(1.0) / np.float32(10000.0) ** (np.arange(half, dtype=np.float32) / np.float32(half)))
        return np.arange(length, dtype=np.float32)[:, None] * inv.astype(np.float32)

    ang = angles(R // 2, LK).T
    cs, sn = np.cos(ang), np.sin(ang)
    o["rope_k"] = c(cat([cs, cs, -sn, sn], 0)).astype(np.float32)
    o["rope_q"] = c(np.tile(o["rope_k"][:, :LQ], (1, HALF_B)))
    a2 = angles(DH // 2, LQ)
    order = (np.arange(8)[None, :] * 8 + np.arange(8)[:, None]).reshape(-1)
    a2 = np.tile(a2[order], (2, 1))
    o["cos2"] = c(np.tile(cat([np.cos(a2)] * 2, 1), (1, NH))).astype(np.float32)
    o["sin2"] = c(np.tile(cat([-np.sin(a2), np.sin(a2)], 1), (1, NH))).astype(np.float32)
    tok = np.arange(P) % 8
    same = tok[:, None] == tok[None, :]
    o["bmask"] = c(np.tile(np.where(same, 0.0, NEG).astype(np.float32), (1, 4)))
    o["tri"] = np.triu(np.ones((P, P), np.float32), 1)
    o["ones"] = np.ones((P, P), np.float32)
    slot = np.zeros((P, NT, 2), np.int32)
    slot[:, :, 0] = T + np.arange(P)[:, None]
    slot[:, :SH_TILES, 0] = (np.arange(SH_TILES)[None, :] % TT) * P + np.arange(P)[:, None]
    slot[:, :SH_TILES, 1] = np.float32(1.0).view(np.int32)
    o["slots0"] = slot.reshape(P * NT, 2)
    o["tokens"] = c((np.arange(TT)[None, :, None] * P + np.arange(P)[:, None, None]) * np.ones((1, 1, TOP))).astype(np.int32)
    return o


SCRATCH = {"x1": ([T, D], F32), "o2": ([B, P, 512], F32), "xn3": ([T + PAD, D], F32), "acc": ([T + PAD, D], F32),
           "slots": ([P * NT, 2], I32)}


def build(nc, arrays, stages="ahrm", scratch="Internal"):
    d = {}
    for name, a in arrays.items():
        d[name] = nc.dram_tensor(f"in_{name}", a.shape, mybir.dt.from_np(a.dtype), kind="ExternalInput").ap()
    for name, (shape, dt) in SCRATCH.items():
        d[name] = nc.dram_tensor(f"tmp_{name}", shape, dt, kind=scratch).ap()
    d["out"] = nc.dram_tensor("out", [T, D], F32, kind="ExternalOutput").ap()
    program(nc, named(d), stages)


def kernel(**inputs):
    import concourse.bacc as bacc
    from concourse.bass_utils import run_bass_kernel_spmd

    arrays = laid_out(**inputs)
    nc = bacc.Bacc("TRN2", target_bir_lowering=False, num_devices=1)
    build(nc, arrays)
    r = run_bass_kernel_spmd(nc, [{f"in_{k}": v for k, v in arrays.items()}], core_ids=[0])
    return r.results[0]["out"].reshape(B, LQ, D)
```

```python
from collections import namedtuple
from contextlib import ExitStack

import concourse.bass as bass
import numpy as np
from concourse import mybir

F32 = mybir.dt.float32
F32R = mybir.dt.float32r
I32 = mybir.dt.int32
ALU = mybir.AluOpType
ACT = mybir.ActivationFunctionType
AX = mybir.AxisListType

P = 128
B, LQ, LK, D = 16, 64, 512, 1024
T = B * LQ
KC = D // P
HALF_B = B // 2
HT = HALF_B * LQ
THREE = ((0, 0), (0, 1), (1, 0))
XH, HD, R = 16, 128, 64
KVC, QC = 256, 384
CC, QCC = KVC // P, QC // P
LOOKBACK = 8
NEG = -1e30
X_SCALE = float(np.float32(1.0) / np.sqrt(HD + R).astype(np.float32))
NH, DH = 16, 64
TT = T // P
E, TOP, NG, KEEP_G = 32, 6, 4, 2
F = 704
FH = F // 2
FC = 6
FCW = [128] * 5 + [64]
SHARED = 2
NE = E + SHARED
SH_TILES = SHARED * TT
MAX_TILES = SH_TILES + (T * TOP + E * (P - 1)) // P
NT = 98
assert MAX_TILES + 2 <= NT
PAD = P
EPS = 1e-5


def named(items):
    return namedtuple("Named", items)(**items)


def semaphores(nc, ctx, prefix, names):
    made = {n: nc.alloc_semaphore(f"{prefix}_{n}") for n in names.split()}

    def clear():
        nc.clear_and_free_semaphores(list(made.values()))
        nc.all_engine_barrier()

    ctx.callback(clear)
    return named(made)


def hold(engine, sem, value, spare):
    engine.wait_ge(sem, value)
    engine.sem_inc(spare, 1)


def queries(nc, ps, d, half, qa, qr, ident, cst):
    with ExitStack() as ctx:
        sb = lambda n, s, t=F32: ctx.enter_context(nc.sbuf_tensor(f"q{half}_{n}", s, t))
        s = semaphores(nc, ctx, f"q{half}", "x_in wdq_in hw_in0 hw_in1 x_free xn_ready xn_free x_psum_free qc_done qc_ready"
                       " nope_done nope_ready rope_done rope_free qa_done qa_free ln sq hw_free spare qr_done")
        x = sb("x", [P, D])
        xn = sb("xn", [P, D])
        xT = sb("xT", [P, KC, HT])
        stats = sb("stats", [P, 2, 6])
        mv = sb("mv", [P, 2])
        rstd = sb("rstd", [P, 1])
        sd = sb("sd", [P, 1])
        wdq = sb("wdq", [P, KC, QC])
        qcT = sb("qcT", [P, QCC, HT])
        hw = [sb(f"hw{i}", [P, 1024]) for i in range(2)]
        qn = sb("qn", [P, HT])
        rp = sb("rp", [R, 2, HT])
        hw_in = (s.hw_in0, s.hw_in1)
        TILES = HT // P
        with nc.Block() as block:

            @block.sync
            def _(sp):
                sp.dma_start(x[:], d.x[half * HT:half * HT + P, :]).then_inc(s.x_in, 16)
                sp.dma_start(wdq[:], d.wdq.rearrange("(k p) n -> p k n", p=P)).then_inc(s.wdq_in, 16)
                with sp.Fori(1, TILES) as t:
                    sp.wait_ge(s.x_free, t)
                    sp.dma_start(x[:], d.x[bass.ds(half * HT + t * P, P), :]).then_inc(s.x_in, 16)
                with sp.Fori(0, XH // 2) as hp:
                    for i in range(2):
                        sp.wait_ge(s.hw_free, hp * 2 + i + 1)
                        sp.dma_start(hw[i][:], d.head_w[hp * 2 + i]).then_inc(hw_in[i], 16)

            @block.vector
            def _(v):
                v.sem_inc(s.rope_free, 1)
                v.sem_inc(s.hw_free, 2)
                with v.Fori(0, TILES) as t:
                    layernorm(v, x, stats, mv, sd, rstd, xn, s, t)
                with v.Fori(0, XH) as h:
                    v.wait_ge(s.rope_done, h + 1)
                    v.tensor_tensor(rp[:, 0, :], ps[1][0:R, :], cst.rope_q[0:R, :], ALU.mult)
                    v.tensor_tensor(rp[:, 1, :], ps[1][R:P, :], cst.rope_q[R:P, :], ALU.mult)\
                        .then_inc(s.rope_free, 1)
                    v.wait_ge(s.rope_free, h + 2)
                    v.tensor_tensor(qr[:, :, bass.ds(h, 1), :].rearrange("p b h q -> p b (h q)"),
                                    rp[:, 0, :].rearrange("p (b q) -> p b q", q=LQ),
                                    rp[:, 1, :].rearrange("p (b q) -> p b q", q=LQ), ALU.add).then_inc(s.qr_done, 1)
                    v.wait_ge(s.qr_done, h + 1)
                    v.wait_ge(s.qa_done, 2 * h + 2)
                    v.sem_inc(s.hw_free, 1)
                    v.tensor_copy(qa[:, 1, :, bass.ds(h, 1), :].rearrange("p b h q -> p b (h q)"),
                                  ps[3][:].rearrange("p (b q) -> p b q", q=LQ)).then_inc(s.qa_free, 1)

            @block.scalar
            def _(act):
                act.sem_inc(s.x_psum_free, 1)
                act.sem_inc(s.nope_ready, 1)
                act.sem_inc(s.qa_free, 2)
                with act.Fori(0, TILES) as t:
                    act.wait_ge(s.sq, 3 * t + 1)
                    act.activation(sd[:], rstd[:], ACT.Sqrt).then_inc(s.sq, 1)
                    act.wait_ge(s.xn_free, t + 2)
                    for i in range(2):
                        cp = act.activation(xT[:, 4 * i:4 * i + 4, bass.ds(t * P, P)],
                                            ps[i][:].rearrange("p (k m) -> p k m", m=P), ACT.Copy)
                    cp.then_inc(s.x_psum_free, 1)
                for m in range(QCC):
                    act.wait_ge(s.qc_done, m + 1)
                    act.activation(qcT[:, m, :], ps[4 + m][:], ACT.Copy).then_inc(s.qc_ready, 1)
                with act.Fori(0, XH) as h:
                    act.wait_ge(s.nope_done, h + 1)
                    act.activation(qn[:], ps[0][:], ACT.Copy).then_inc(s.nope_ready, 1)
                    act.wait_ge(s.qa_done, 2 * h + 1)
                    act.activation(qa[:, 0, :, bass.ds(h, 1), :].rearrange("p b h q -> p b (h q)"),
                                   ps[2][:].rearrange("p (b q) -> p b q", q=LQ), ACT.Copy).then_inc(s.qa_free, 1)

            @block.tensor
            def _(pe):
                pe.sem_inc(s.xn_free, 1)
                with pe.Fori(0, TILES) as t:
                    pe.wait_ge(s.x_psum_free, t + 1)
                    pe.wait_ge(s.xn_ready, t + 1)
                    for k in range(KC):
                        mm = pe.transpose(ps[k // 4][:, (k % 4) * P:(k % 4 + 1) * P], xn[:, k * P:(k + 1) * P], ident)
                    mm.then_inc(s.xn_free, 1)
                pe.wait_ge(s.wdq_in, 16)
                pe.wait_ge(s.x_psum_free, TILES + 1)
                for m in range(QCC):
                    for k in range(KC):
                        mm = pe.matmul(ps[4 + m][:], wdq[:, k, m * P:(m + 1) * P], xT[:, k, :],
                                       start=(k == 0), stop=(k == KC - 1))
                    mm.then_inc(s.qc_done, 1)
                pe.wait_ge(s.qc_ready, QCC)
                with pe.Fori(0, XH // 2) as hp:
                    for i in range(2):
                        h = hp * 2 + i
                        w = hw[i]
                        pe.wait_ge(hw_in[i], hp * 16 + 16)
                        pe.wait_ge(s.nope_ready, h + 1)
                        for m in range(QCC):
                            mm = pe.matmul(ps[0][:], w[:, m * P:(m + 1) * P], qcT[:, m, :],
                                           start=(m == 0), stop=(m == QCC - 1))
                        mm.then_inc(s.nope_done, 1)
                        pe.wait_ge(s.rope_free, h + 1)
                        for m in range(QCC):
                            mm = pe.matmul(ps[1][:], w[:, (3 + m) * P:(4 + m) * P], qcT[:, m, :],
                                           start=(m == 0), stop=(m == QCC - 1))
                        mm.then_inc(s.rope_done, 1)
                        pe.wait_ge(s.nope_ready, h + 2)
                        pe.wait_ge(s.qa_free, 2 * h + 2)
                        for c in range(CC):
                            pe.matmul(ps[2 + c][:], w[:, (6 + c) * P:(7 + c) * P], qn[:],
                                      start=True, stop=True).then_inc(s.qa_done, 1)


def layernorm(v, x, stats, mv, sd, rstd, xn, s, t):
    v.wait_ge(s.x_in, t * 16 + 16)
    layernorm_steps(v, x, stats, mv, sd, rstd, xn, s, t)


def layernorm_steps(v, x, stats, mv, sd, rstd, xn, s, t):
    v.bn_stats(stats[:, 0, :], x[:, 0:D // 2])
    v.bn_stats(stats[:, 1, :], x[:, D // 2:D]).then_inc(s.ln, 1)
    hold(v, s.ln, 2 * t + 1, s.spare)
    v.bn_aggr(mv[:], stats[:]).then_inc(s.ln, 1)
    v.wait_ge(s.ln, 2 * t + 2)
    v.tensor_scalar(rstd[:], mv[:, 1:2], EPS, None, ALU.add).then_inc(s.sq, 1)
    v.wait_ge(s.sq, 3 * t + 2)
    v.reciprocal(rstd[:], sd[:]).then_inc(s.sq, 1)
    v.wait_ge(s.sq, 3 * t + 3)
    v.wait_ge(s.xn_free, t + 1)
    v.tensor_scalar(xn[:], x[:], mv[:, 0:1], rstd[:], ALU.subtract, ALU.mult).then_inc(s.xn_ready, 1)
    v.wait_ge(s.xn_ready, t + 1)
    v.sem_inc(s.x_free, 1)


def at(i):
    return slice(i, i + 1) if isinstance(i, int) else bass.ds(i, 1)


def contexts(nc, ps, d, half, qa, qr, ident, cst):
    with ExitStack() as ctx:
        sb = lambda n, s, t=F32: ctx.enter_context(nc.sbuf_tensor(f"c{half}_{n}", s, t))
        s = semaphores(nc, ctx, f"c{half}", "w_in ctx_in ctx_free seg_in seg_ready mstep kv_done kvT_raw kvT_hi kvT_lo"
                       " kr_done kr_free kr_step kvx_done kv_hi kv_lo q_hi q_lo q_free score_done score_free sm rowmax"
                       " exp_done prob_ready prob_free pT_hi pT_lo out_done out_free spare")
        pair = lambda n, s: [sb(n + "_hi", s, F32R), sb(n + "_lo", s, F32R)]
        wkvc = sb("wkvc", [P, KC, KVC])
        wkr = sb("wkr", [P, CC, P])
        cT = sb("cT", [P, KC, LK])
        seg_i = sb("seg_i", [P, B], I32)
        seg = sb("seg", [P, 2, B])
        late = sb("late", [P, LK])
        mask = sb("mask", [P, LK])
        kvT_raw = sb("kvT_raw", [P, CC, LK])
        kvT = pair("kvT", [P, CC, LK])
        kv = pair("kv", [P, 4, KVC])
        kr_raw = sb("kr_raw", [R, LK])
        kr = pair("kr", [R, LK])
        rp = sb("rp", [R, 2, LK])
        qs = pair("qs", [P, CC, XH * LQ])
        qrs = pair("qrs", [R, XH * LQ])
        DEEP = 3
        sc = sb("sc", [P, DEEP, LK])
        nmax = sb("nmax", [P, DEEP])
        rsum = sb("rsum", [P, DEEP])
        pT = pair("pT", [P, 4, 4 * P])
        RT = XH * LQ // P
        SC_BANK, OUT_BANK, TURN_BANK, KR_BANK = (5, 6, 2), ((0, 1), (4, 3)), (7, 3), 7

        def deep_free(b, r):
            return b * RT + max(r + 1, DEEP)

        def each_row(engine, prepare, attend):
            prepare(0)
            with engine.Fori(0, HALF_B - 1) as b:
                attend(b, True)
            attend(HALF_B - 1, False)

        def query_parts(b):
            v = lambda z: z.rearrange("p (h q) -> p h q", q=LQ)
            row = lambda z: z.rearrange("p b h q -> p (b h) q")
            return [(row(qa[:, c, at(b), :, :]), v(qs[0][:, c, :]), v(qs[1][:, c, :])) for c in range(CC)] + \
                [(row(qr[:, at(b), :, :]), v(qrs[0][:]), v(qrs[1][:]))]

        with nc.Block() as block:

            @block.sync
            def _(sp):
                sp.dma_start(wkvc[:], d.wkvc.rearrange("(k p) n -> p k n", p=P)).then_inc(s.w_in, 16)
                sp.dma_start(wkr[:], d.wkr.rearrange("(k p) n -> p k n", p=P)).then_inc(s.w_in, 16)
                sp.dma_start(seg_i[:], d.seg[:, :]).then_inc(s.seg_in, 16)
                with sp.Fori(0, HALF_B) as b:
                    sp.wait_ge(s.ctx_free, b + 1)
                    sp.dma_start(cT[:], d.ctxT[b + half * HALF_B].rearrange("(k p) n -> p k n", p=P))\
                        .then_inc(s.ctx_in, 16)

            @block.gpsimd
            def _(g):
                with g.Fori(0, HALF_B) as b:
                    hold(g, s.q_free, b + 1, s.spare)
                    for src, hi, _ in query_parts(b):
                        g.tensor_copy(hi, src).then_inc(s.q_hi, 1)

            @block.vector
            def _(v):
                v.sem_inc(s.kr_free, 1)
                v.sem_inc(s.score_free, DEEP)
                v.sem_inc(s.q_free, 1)
                v.wait_ge(s.seg_in, 16)
                v.tensor_copy(seg[:, 0, :], seg_i[:]).then_inc(s.seg_ready, 1)
                v.wait_ge(s.seg_ready, 1)
                v.tensor_scalar(seg[:, 1, :], seg[:, 0, :], -float(LOOKBACK), None, ALU.add).then_inc(s.seg_ready, 1)
                v.wait_ge(s.seg_ready, 2)

                def make_mask(n):
                    bb = n + half * HALF_B
                    v.tensor_scalar(mask[:], cst.iota[:], seg[:, 0, at(bb)], NEG, ALU.is_gt, ALU.mult)
                    v.tensor_scalar(late[:], cst.iota[:], seg[:, 1, at(bb)], NEG, ALU.is_lt, ALU.mult).then_inc(s.mstep, 1)
                    v.wait_ge(s.mstep, 2 * n + 1)
                    v.tensor_tensor(mask[:], mask[:], late[:], ALU.add).then_inc(s.mstep, 1)

                def split_latents(n, c):
                    v.wait_ge(s.kvT_hi, CC * n + c + 1)
                    v.tensor_tensor(kvT[1][:, c, :], kvT_raw[:, c, :], kvT[0][:, c, :], ALU.subtract).then_inc(s.kvT_lo, 1)

                def split_queries(n):
                    for i, (src, hi, lo) in enumerate(query_parts(n)):
                        v.wait_ge(s.q_hi, 3 * n + i + 1)
                        v.tensor_tensor(lo, src, hi, ALU.subtract).then_inc(s.q_lo, 1)

                def turn_keys(n):
                    v.wait_ge(s.kr_done, n + 1)
                    v.tensor_tensor(rp[:, 0, :], ps[KR_BANK][0:R, :], cst.rope_k[0:R, :], ALU.mult)
                    v.tensor_tensor(rp[:, 1, :], ps[KR_BANK][R:P, :], cst.rope_k[R:P, :], ALU.mult).then_inc(s.kr_free, 1)
                    v.wait_ge(s.kr_free, n + 2)
                    v.tensor_tensor(kr_raw[:], rp[:, 0, :], rp[:, 1, :], ALU.add).then_inc(s.kr_step, 1)
                    v.wait_ge(s.kr_step, 3 * n + 1)
                    v.tensor_copy(kr[0][:], kr_raw[:]).then_inc(s.kr_step, 1)
                    v.wait_ge(s.kr_step, 3 * n + 2)
                    v.tensor_tensor(kr[1][:], kr_raw[:], kr[0][:], ALU.subtract).then_inc(s.kr_step, 1)

                def split_turned(n):
                    for i in range(2):
                        v.wait_ge(s.kv_hi, 2 * n + i + 1)
                        v.tensor_tensor(kv[1][:, 2 * i:2 * i + 2, :], ps[i][:].rearrange("p (k c) -> p k c", c=KVC),
                                        kv[0][:, 2 * i:2 * i + 2, :], ALU.subtract).then_inc(s.kv_lo, 1)

                def prepare(n):
                    make_mask(n)
                    for c in range(CC):
                        split_latents(n, c)
                    split_queries(n)
                    turn_keys(n)
                    split_turned(n)

                def attend(b, follows):
                    v.wait_ge(s.mstep, 2 * b + 2)
                    v.wait_ge(s.kr_step, 3 * b + 3)

                    def softmax_head(r):
                        k = r % DEEP
                        v.wait_ge(s.score_done, b * RT + r + 1)
                        if r == RT - 1:
                            v.sem_inc(s.q_free, 1)
                        v.scalar_tensor_tensor(sc[:, k, :], ps[SC_BANK[k]][:], X_SCALE, mask[:],
                                               ALU.mult, ALU.add).then_inc(s.score_free, 1)
                        v.wait_ge(s.score_free, b * RT + r + DEEP + 1)
                        v.tensor_reduce(nmax[:, k:k + 1], sc[:, k, :], AX.X, ALU.max, negate=True).then_inc(s.rowmax, 1)

                    def softmax_tail(r):
                        k = r % DEEP
                        v.wait_ge(s.exp_done, b * RT + r + 1)
                        v.reciprocal(rsum[:, k:k + 1], rsum[:, k:k + 1]).then_inc(s.sm, 1)
                        v.wait_ge(s.sm, b * RT + r + 1)
                        v.tensor_scalar(sc[:, k, :], sc[:, k, :], rsum[:, k:k + 1], None, ALU.mult).then_inc(s.prob_ready, 1)

                    def split_pT(r):
                        at_r = slice((r % 4) * P, (r % 4 + 1) * P)
                        v.wait_ge(s.pT_hi, b * RT + r + 1)
                        v.tensor_tensor(pT[1][:, :, at_r], ps[TURN_BANK[r % 2]][:].rearrange("p (k m) -> p k m", m=P),
                                        pT[0][:, :, at_r], ALU.subtract).then_inc(s.pT_lo, 1)

                    for r in range(RT + 1):
                        if r < RT:
                            softmax_head(r)
                        if r > 0:
                            softmax_tail(r - 1)
                        if r > 1:
                            split_pT(r - 2)
                    if follows:
                        split_latents(b + 1, 0)
                    split_pT(RT - 1)
                    if follows:
                        make_mask(b + 1)
                        split_latents(b + 1, 1)
                        split_queries(b + 1)
                        turn_keys(b + 1)
                        split_turned(b + 1)

                each_row(v, prepare, attend)

            @block.scalar
            def _(act):
                act.sem_inc(s.out_free, 4)

                def take_latents(n, c):
                    act.wait_ge(s.kv_done, n * CC + c + 1)
                    act.activation(kvT_raw[:, c, :], ps[c][:], ACT.Copy).then_inc(s.kvT_raw, 1)
                    act.activation(kvT[0][:, c, :], ps[c][:], ACT.Copy).then_inc(s.kvT_hi, 1)

                def take_turned(n):
                    act.wait_ge(s.kvx_done, n + 1)
                    for i in range(2):
                        act.activation(kv[0][:, 2 * i:2 * i + 2, :], ps[i][:].rearrange("p (k c) -> p k c", c=KVC),
                                       ACT.Copy).then_inc(s.kv_hi, 1)

                def prepare(n):
                    for c in range(CC):
                        take_latents(n, c)
                    take_turned(n)

                def attend(b, follows):
                    def exps(r):
                        k = r % DEEP
                        act.wait_ge(s.prob_free, deep_free(b, r))
                        act.wait_ge(s.rowmax, b * RT + r + 1)
                        act.activation(sc[:, k, :], sc[:, k, :], ACT.Exp, bias=nmax[:, k:k + 1],
                                       scale=1.0, accum_out=rsum[:, k:k + 1]).then_inc(s.exp_done, 1)

                    def take_pT(r):
                        act.wait_ge(s.prob_free, b * RT + r + DEEP + 1)
                        act.activation(pT[0][:, :, (r % 4) * P:(r % 4 + 1) * P],
                                       ps[TURN_BANK[r % 2]][:].rearrange("p (k m) -> p k m", m=P), ACT.Copy).then_inc(s.pT_hi, 1)

                    def take_out(n):
                        for c in range(CC):
                            act.wait_ge(s.out_done, b * 4 + n * 2 + c + 1)
                            act.activation(qa[:, c, at(b), n * 8:n * 8 + 8, :].rearrange("p b h q -> p b (h q)"),
                                           ps[OUT_BANK[n][c]][:].rearrange("p (b r) -> p b r", b=1), ACT.Copy)\
                                .then_inc(s.out_free, 1)

                    exps(0)
                    exps(1)
                    for r in range(RT):
                        take_pT(r)
                        if r + 2 < RT:
                            exps(r + 2)
                        if r == 3:
                            take_out(0)
                        if r >= 6 and follows:
                            take_latents(b + 1, r - 6)
                    take_out(1)
                    if follows:
                        take_turned(b + 1)

                each_row(act, prepare, attend)

            @block.tensor
            def _(pe):
                pe.sem_inc(s.ctx_free, 1)
                pe.sem_inc(s.prob_free, DEEP)
                pe.sem_inc(s.pT_lo, 2)
                pe.wait_ge(s.w_in, 32)

                def latents(n, c, ks):
                    if c == 0 and ks[0] == 0:
                        pe.wait_ge(s.ctx_in, n * 16 + 16)
                    for k in ks:
                        mm = pe.matmul(ps[c][:], wkvc[:, k, c * P:(c + 1) * P], cT[:, k, :],
                                       start=(k == 0), stop=(k == KC - 1))
                    if ks[-1] == KC - 1:
                        mm.then_inc(s.kv_done, 1)

                def keys(n):
                    pe.wait_ge(s.kvT_raw, CC * n + CC)
                    pe.sem_inc(s.ctx_free, 1)
                    pe.wait_ge(s.kr_free, n + 1)
                    pe.wait_ge(s.pT_lo, n * RT + 2)
                    for c in range(CC):
                        mm = pe.matmul(ps[KR_BANK][:], wkr[:, c, :], kvT_raw[:, c, :], start=(c == 0), stop=(c == CC - 1))
                    mm.then_inc(s.kr_done, 1)

                def turn_latents(n):
                    pe.wait_ge(s.kvT_hi, CC * n + CC)
                    for k in range(4):
                        for c in range(CC):
                            mm = pe.transpose(ps[k // 2][:, (k % 2) * KVC + c * P:(k % 2) * KVC + (c + 1) * P],
                                              kvT_raw[:, c, k * P:(k + 1) * P], ident)
                    mm.then_inc(s.kvx_done, 1)

                def prepare(n):
                    for c in range(CC):
                        latents(n, c, range(KC))
                    keys(n)
                    turn_latents(n)

                def attend(b, follows):
                    def scores(r):
                        bank = ps[SC_BANK[r % DEEP]]
                        rows = slice(r * P, (r + 1) * P)
                        pe.wait_ge(s.score_free, deep_free(b, r))
                        for c in range(CC):
                            for q, k in THREE:
                                pe.matmul(bank[:], qs[q][:, c, rows], kvT[k][:, c, :], start=(c == 0 and q == 0 and k == 0),
                                          stop=False)
                        if r == 0:
                            pe.wait_ge(s.kr_step, 3 * b + 3)
                        for q, k in THREE:
                            mm = pe.matmul(bank[:], qrs[q][:, rows], kr[k][:], start=False, stop=(q == 1))
                        mm.then_inc(s.score_done, 1)

                    def turn(r):
                        pe.wait_ge(s.prob_ready, b * RT + r + 1)
                        pe.wait_ge(s.pT_lo, b * RT + r + 1)
                        if r == 1:
                            pe.wait_ge(s.out_free, 4 * b + 4)
                        for k in range(4):
                            mm = pe.transpose(ps[TURN_BANK[r % 2]][:, k * P:(k + 1) * P], sc[:, r % DEEP, k * P:(k + 1) * P], ident)
                        mm.then_inc(s.prob_free, 1)

                    def weighted(n):
                        if n == 0:
                            pe.wait_ge(s.kv_lo, 2 * b + 2)
                        pe.wait_ge(s.pT_hi, b * RT + 4 * n + 4)
                        for c in range(CC):
                            bank, cols = ps[OUT_BANK[n][c]], slice(c * P, (c + 1) * P)
                            if n == 1 and c == 1:
                                if follows:
                                    keys(b + 1)
                                pe.wait_ge(s.pT_lo, b * RT + RT + 2)
                            for i in range(2):
                                for k in range(4):
                                    pe.matmul(bank[:], kv[i][:, k, cols], pT[0][:, k, :], start=(i == 0 and k == 0), stop=False)
                            pe.wait_ge(s.pT_lo, b * RT + 4 * n + 6)
                            for k in range(4):
                                mm = pe.matmul(bank[:], kv[0][:, k, cols], pT[1][:, k, :], start=False, stop=(k == 3))
                            mm.then_inc(s.out_done, 1)

                    pe.wait_ge(s.kvT_lo, CC * b + CC)
                    pe.wait_ge(s.q_lo, 3 * b + 3)
                    for r in range(DEEP):
                        scores(r)
                    for r in range(RT):
                        turn(r)
                        if r == 3:
                            weighted(0)
                        if r + DEEP < RT:
                            scores(r + DEEP)
                        elif follows and r == 5:
                            pe.wait_ge(s.out_free, 4 * b + 6)
                            latents(b + 1, 0, range(0, 4))
                        elif follows and r == 6:
                            latents(b + 1, 0, range(4, 8))
                    if follows:
                        latents(b + 1, 1, range(KC))
                    weighted(1)
                    if follows:
                        turn_latents(b + 1)

                each_row(pe, prepare, attend)


def merge(nc, ps, d, half, qa):
    with ExitStack() as ctx:
        sb = lambda n, s, t=F32: ctx.enter_context(nc.sbuf_tensor(f"m{half}_{n}", s, t))
        s = semaphores(nc, ctx, f"m{half}", "wo_in wv_in0 wv_in1 wv_free o_done o_ready x_in x_free y_done y_ready st0 st1")
        wo = sb("wo", [P, XH, D])
        wv = [sb(f"wv{i}", [P, CC * P]) for i in range(2)]
        oT = sb("oT", [P, XH, HT])
        x = sb("x", [P, D])
        y = [sb(f"y{i}", [P, D]) for i in range(2)]
        wv_in = (s.wv_in0, s.wv_in1)
        st = (s.st0, s.st1)
        TILES = HT // P
        with nc.Block() as block:

            @block.sync
            def _(sp):
                src = d.wo.rearrange("(h p) n -> p h n", p=P)
                for h in range(XH):
                    sp.wait_ge(s.wv_free, h + 1)
                    sp.dma_start(wv[h % 2][:], d.head_v[h]).then_inc(wv_in[h % 2], 16)
                    if h % 2:
                        sp.dma_start(wo[:, h - 1:h + 1, :], src[:, h - 1:h + 1, :]).then_inc(s.wo_in, 16)
                for t in range(TILES):
                    sp.wait_ge(s.x_free, t + 1)
                    sp.dma_start(x[:], d.x[half * HT + t * P:half * HT + (t + 1) * P, :]).then_inc(s.x_in, 16)

            @block.vector
            def _(v):
                v.sem_inc(s.x_free, 1)
                for t in range(TILES):
                    v.wait_ge(s.x_in, 16 * (t + 1))
                    if t >= 2:
                        v.wait_ge(st[t % 2], 16 * (t // 2))
                    for n in range(2):
                        v.wait_ge(s.y_done, 2 * t + n + 1)
                        a = v.tensor_tensor(y[t % 2][:, n * 512:(n + 1) * 512], ps[2 * (t % 2) + n][:],
                                            x[:, n * 512:(n + 1) * 512], ALU.add)
                        a.then_inc(s.y_ready, 1)
                    v.wait_ge(s.y_ready, 2 * t + 2)
                    v.sem_inc(s.x_free, 1)

            @block.scalar
            def _(act):
                act.sem_inc(s.o_ready, 2)
                act.sem_inc(s.wv_free, 2)
                with act.Fori(0, XH // 2) as hp:
                    for i in range(2):
                        h = hp * 2 + i
                        act.wait_ge(s.o_done, h + 1)
                        act.sem_inc(s.wv_free, 1)
                        act.activation(oT[:, bass.ds(h, 1), :].rearrange("p h m -> p (h m)"), ps[4 + i][:], ACT.Copy)\
                            .then_inc(s.o_ready, 1)
                for t in range(TILES):
                    act.wait_ge(s.y_ready, 2 * t + 2)
                    act.dma_start(d.x1[half * HT + t * P:half * HT + (t + 1) * P, :], y[t % 2][:]).then_inc(st[t % 2], 16)
                for i in range(2):
                    act.wait_ge(st[i], 16 * (TILES // 2))

            @block.tensor
            def _(pe):
                with pe.Fori(0, XH // 2) as hp:
                    for i in range(2):
                        h = hp * 2 + i
                        pe.wait_ge(wv_in[i], hp * 16 + 16)
                        pe.wait_ge(s.o_ready, h + 1)
                        for c in range(CC):
                            mm = pe.matmul(ps[4 + i][:], wv[i][:, c * P:(c + 1) * P],
                                           qa[:, c, :, bass.ds(h, 1), :].rearrange("p b h q -> p b (h q)"),
                                           start=(c == 0), stop=(c == CC - 1))
                        mm.then_inc(s.o_done, 1)
                pe.wait_ge(s.wo_in, 16 * (XH // 2))
                pe.wait_ge(s.o_ready, XH + 2)
                for t in range(TILES):
                    if t >= 2:
                        pe.wait_ge(s.y_ready, 2 * (t - 1))
                    for n in range(2):
                        for h in range(XH):
                            mm = pe.matmul(ps[2 * (t % 2) + n][:], oT[:, h, t * P:(t + 1) * P],
                                           wo[:, h, n * 512:(n + 1) * 512], start=(h == 0), stop=(h == XH - 1))
                        mm.then_inc(s.y_done, 1)


def norm_tile(v, x, stats, mv, sd, rstd, xn, s, t, loads=1):
    v.wait_ge(s.x_in, t * (16 * loads) + 16 * loads)
    layernorm_steps(v, x, stats, mv, sd, rstd, xn, s, t)


def heads(nc, ps, d, ident):
    with ExitStack() as ctx:
        sb = lambda n, s, t=F32: ctx.enter_context(nc.sbuf_tensor(f"h_{n}", s, t))
        s = semaphores(nc, ctx, "h", "gspare pspare wq0_in wq1_in wk0_in wk1_in wv0_in wv1_in"
                       " bq_in bk_in bv_in c_in x_in x_free xn_ready xn_free ln sq spare x_psum_free proj_done"
                       " proj_free q_sum q_rot k_sum k_rot v_sum ring_done ring_free score_done score_free mx"
                       " shifted exp_done sm sm2 prob_ready o_st o_free")
        w_in = (s.wq0_in, s.wq1_in, s.wk0_in, s.wk1_in, s.wv0_in, s.wv1_in)
        b_in = (s.bq_in, s.bk_in, s.bv_in)
        w = [sb(f"w{n}", [P, KC, D]) for n in "qkv"]
        bias = [sb(f"b{n}", [P, D]) for n in "qkv"]
        cos = sb("cos", [P, D])
        sin = sb("sin", [P, D])
        bmask = sb("bmask", [P, 512])
        x = sb("x", [P, D])
        xn = sb("xn", [P, D])
        xT = sb("xT", [P, KC, P])
        stats = sb("stats", [P, 2, 6])
        mv = sb("mv", [P, 2])
        rstd = sb("rstd", [P, 1])
        sd = sb("sd", [P, 1])
        qkv = [sb(f"t{n}", [P, D]) for n in "qkv"]
        swp = [sb(f"s{n}", [P, D]) for n in "qk"]
        hT = [sb(f"T{n}", [DH, 16, NH, 8]) for n in "qkv"]
        sc = sb("sc", [P, 2, 4, P])
        rmax = sb("rmax", [P, 2, 4])
        rsum = sb("rsum", [P, 4, 4])
        pr = sb("pr", [P, 4, 512])
        pT = sb("pT", [P, 4, 512])
        vg = sb("vg", [P, 16, DH])
        og = sb("og", [P, 16, DH])
        RING = 20

        def rotate(eng, n, start, done, t):
            a, b = qkv[n], swp[n]
            v4 = lambda z: z[:].rearrange("p (h i j) -> p h i j", i=2, j=DH // 2)
            eng.wait_ge(start, 2 * t + 2)
            eng.tensor_tensor(v4(b)[:, :, 0, :], v4(a)[:, :, 1, :], v4(sin)[:, :, 0, :], ALU.mult)
            eng.tensor_tensor(v4(b)[:, :, 1, :], v4(a)[:, :, 0, :], v4(sin)[:, :, 1, :], ALU.mult).then_inc(done, 1)
            eng.wait_ge(done, 3 * t + 1)
            eng.tensor_tensor(a[:], a[:], cos[:], ALU.mult).then_inc(done, 1)
            eng.wait_ge(done, 3 * t + 2)
            eng.tensor_tensor(a[:], a[:], b[:], ALU.add).then_inc(done, 1)

        def tiles(engine, body):
            body(0, None)
            with engine.Fori(0, TT - 1) as t:
                body(t + 1, t)
            body(None, TT - 1)

        with nc.Block() as block:

            @block.sync
            def _(sp):
                rows = d.x1.rearrange("(b t g) n -> b g t n", g=8, t=8)

                def load_x(t):
                    if not isinstance(t, int) or t > 0:
                        sp.wait_ge(s.x_free, t)
                    for b in range(2):
                        sp.dma_start(x[b * LQ:(b + 1) * LQ, :], rows[2 * t + b]).then_inc(s.x_in, 16)

                load_x(0)
                for n, (src, b_src) in enumerate(((d.wq, d.bq), (d.wk, d.bk), (d.wv, d.bv))):
                    if n == 2:
                        load_x(1)
                    for h in range(2):
                        sp.dma_start(w[n][:, :, h * 512:(h + 1) * 512], src[:, h * 512:(h + 1) * 512]
                                     .rearrange("(k p) n -> p k n", p=P)).then_inc(w_in[2 * n + h], 16)
                        if h == 0:
                            sp.dma_start(bias[n][:], b_src[:, :]).then_inc(b_in[n], 16)
                    if n == 0:
                        sp.dma_start(cos[:], d.cos2[:, :]).then_inc(s.c_in, 16)
                        sp.dma_start(sin[:], d.sin2[:, :]).then_inc(s.c_in, 16)
                        sp.dma_start(bmask[:], d.bmask[:, :]).then_inc(s.c_in, 16)
                with sp.Fori(2, TT) as t:
                    load_x(t)

            @block.gpsimd
            def _(g):
                g.sem_inc(s.o_free, 1)
                g.wait_ge(s.c_in, 48)

                def body(p, a):
                    if p is not None:
                        rotate(g, 1, s.k_sum, s.k_rot, p)
                    if a is not None:
                        hold(g, s.ring_free, RING * a + 24, s.gspare)
                        g.dma_start((d.o2[2 * a:2 * a + 2] if isinstance(a, int) else d.o2[bass.ds(a * 2, 2)])
                                    .rearrange("b p n -> p b n"),
                                    og[:].rearrange("p (b g) n -> p b (g n)", b=2)).then_inc(s.o_st, 16)
                        g.wait_ge(s.o_st, a * 16 + 16)
                        g.sem_inc(s.o_free, 1)

                tiles(g, body)

            @block.vector
            def _(v):
                v.sem_inc(s.proj_free, 2)
                v.sem_inc(s.score_free, 4)
                norm_tile(v, x, stats, mv, sd, rstd, xn, s, 0, 2)

                def add_bias(p, a, g):
                    n, h = g // 2, g % 2
                    if a is not None and h == 0:
                        v.wait_ge(s.ring_done, RING * a + 4 * (n + 1))
                    if isinstance(p, int) and p == 0 and h == 0:
                        v.wait_ge(b_in[n], 16)
                    v.wait_ge(s.proj_done, 6 * p + g + 1)
                    add = v.tensor_tensor(qkv[n][:, h * 512:(h + 1) * 512], ps[2 + h][:],
                                          bias[n][:, h * 512:(h + 1) * 512], ALU.add)
                    add.then_inc(s.proj_free, 1)
                    v.wait_ge(s.proj_free, 6 * p + g + 3)
                    v.sem_inc((s.q_sum, s.k_sum, s.v_sum)[n], 1)

                def head(a, i):
                    k = i % 2
                    v.wait_ge(s.score_done, 4 * a + i + 1)
                    v.tensor_tensor(sc[:, k].rearrange("p g m -> p (g m)"), ps[4 + i][:], bmask[:], ALU.add)\
                        .then_inc(s.score_free, 1)
                    v.wait_ge(s.score_free, 4 * a + i + 5)
                    v.tensor_reduce(rmax[:, k, :], sc[:, k], AX.X, ALU.max).then_inc(s.mx, 1)
                    v.wait_ge(s.mx, 4 * a + i + 1)
                    v.tensor_tensor(sc[:, k], sc[:, k], rmax[:, k, :].unsqueeze(2).broadcast_to([P, 4, P]), ALU.subtract)\
                        .then_inc(s.shifted, 1)

                def tail(a, i):
                    v.wait_ge(s.exp_done, 4 * a + i + 1)
                    e = pr[:, i, :].rearrange("p (g m) -> p g m", m=P)
                    v.tensor_reduce(rsum[:, i, :], e, AX.X, ALU.add).then_inc(s.sm, 1)
                    v.wait_ge(s.sm, 4 * a + i + 1)
                    v.reciprocal(rsum[:, i, :], rsum[:, i, :]).then_inc(s.sm2, 1)
                    v.wait_ge(s.sm2, 4 * a + i + 1)
                    v.tensor_tensor(e, e, rsum[:, i, :].unsqueeze(2).broadcast_to([P, 4, P]), ALU.mult)\
                        .then_inc(s.prob_ready, 1)

                def body(p, a):
                    if p is not None:
                        add_bias(p, a, 0)
                        add_bias(p, a, 1)
                    if a is not None:
                        head(a, 0)
                        for i in range(4):
                            if i < 3:
                                head(a, i + 1)
                            tail(a, i)
                    if p is not None:
                        add_bias(p, a, 2)
                        add_bias(p, a, 3)
                        if isinstance(p, int) and p == 0:
                            v.wait_ge(s.c_in, 48)
                        rotate(v, 0, s.q_sum, s.q_rot, p)
                        add_bias(p, a, 4)
                        add_bias(p, a, 5)
                        if a is None:
                            norm_tile(v, x, stats, mv, sd, rstd, xn, s, 1, 2)

                body(0, None)
                with v.Fori(0, TT - 2) as t:
                    body(t + 1, t)
                    norm_tile(v, x, stats, mv, sd, rstd, xn, s, t + 2, 2)
                body(TT - 1, TT - 2)
                body(None, TT - 1)

            @block.scalar
            def _(act):
                act.sem_inc(s.x_psum_free, 1)
                act.sem_inc(s.ring_free, 4)

                def root(t):
                    act.wait_ge(s.sq, 3 * t + 1)
                    act.activation(sd[:], rstd[:], ACT.Sqrt).then_inc(s.sq, 1)

                def take_x(p):
                    act.wait_ge(s.xn_free, p + 2)
                    for i in range(2):
                        cp = act.activation(xT[:, 4 * i:4 * i + 4, :], ps[i][:].rearrange("p (k m) -> p k m", m=P), ACT.Copy)
                    cp.then_inc(s.x_psum_free, 1)

                def take(a, n, dst, src):
                    act.wait_ge(s.ring_done, RING * a + n + 1)
                    act.activation(dst, src, ACT.Copy).then_inc(s.ring_free, 1)

                def take_heads(a, n):
                    for i in range(4):
                        take(a, 4 * n + i, hT[n][:, :, 4 * i:4 * i + 4, :].rearrange("p g h t -> p h g t"),
                             ps[4 + i][0:DH, :].rearrange("p (h g t) -> p h g t", g=16, t=8))

                def body(p, a, norm):
                    if p is not None:
                        take_x(p)
                    if a is not None:
                        take_heads(a, 0)
                        take_heads(a, 1)
                        for i in range(4):
                            act.wait_ge(s.shifted, 4 * a + i + 1)
                            act.activation(pr[:, i, :], sc[:, i % 2].rearrange("p g m -> p (g m)"), ACT.Exp,
                                           scale=DH ** -0.5).then_inc(s.exp_done, 1)
                        take_heads(a, 2)
                    if norm is not None:
                        root(norm)
                    if a is not None:
                        for i in range(4):
                            take(a, 12 + i, pT[:, i, :], ps[4 + i][:])
                        for i in range(2):
                            take(a, 16 + i, vg[:, 8 * i:8 * i + 8, :].rearrange("p g n -> p (g n)"), ps[4 + i][:])
                        act.wait_ge(s.o_free, a + 1)
                        for i in range(2):
                            take(a, 18 + i, og[:, 8 * i:8 * i + 8, :].rearrange("p g n -> p (g n)"), ps[6 + i][:])

                root(0)
                body(0, None, 1)
                with act.Fori(0, TT - 2) as t:
                    body(t + 1, t, t + 2)
                body(TT - 1, TT - 2, None)
                body(None, TT - 1, None)

            @block.tensor
            def _(pe):
                pe.sem_inc(s.xn_free, 1)

                def project(p, g):
                    if isinstance(p, int) and p == 0:
                        pe.wait_ge(w_in[g], 16)
                    if g == 0:
                        pe.wait_ge(s.x_psum_free, p + 2)
                    pe.wait_ge(s.proj_free, 6 * p + g + 1)
                    n, h = g // 2, g % 2
                    for k in range(KC):
                        mm = pe.matmul(ps[2 + h][:], xT[:, k, :], w[n][:, k, h * 512:(h + 1) * 512],
                                       start=(k == 0), stop=(k == KC - 1))
                    mm.then_inc(s.proj_done, 1)

                def turn(a, n):
                    if n == 0:
                        pe.wait_ge(s.q_rot, 3 * a + 3)
                    elif n == 1:
                        pe.wait_ge(s.k_rot, 3 * a + 3)
                    else:
                        pe.wait_ge(s.v_sum, 2 * a + 2)
                    for i in range(4):
                        if n < 2:
                            hold(pe, s.ring_free, RING * a + 4 * n + i + 1, s.pspare)
                        else:
                            hold(pe, s.score_free, 4 * a + i + 5, s.pspare)
                        for j in range(4):
                            h = 4 * i + j
                            mm = pe.transpose(ps[4 + i][0:DH, j * P:(j + 1) * P], qkv[n][:, h * DH:(h + 1) * DH], ident)
                        mm.then_inc(s.ring_done, 1)

                group = lambda z, g: z[:, g].rearrange("p h t -> p (h t)")

                def body(p, a):
                    if p is not None:
                        pe.wait_ge(s.x_psum_free, p + 1)
                        pe.wait_ge(s.xn_ready, p + 1)
                        for k in range(KC):
                            mm = pe.transpose(ps[k // 4][:, (k % 4) * P:(k % 4 + 1) * P], xn[:, k * P:(k + 1) * P], ident)
                        mm.then_inc(s.xn_free, 1)
                    if a is not None:
                        turn(a, 0)
                    if p is not None:
                        project(p, 0)
                    if a is not None:
                        turn(a, 1)
                    if p is not None:
                        project(p, 1)
                    if a is not None:
                        pe.wait_ge(s.ring_free, RING * a + 12)
                        for i in range(4):
                            for j in range(4):
                                mm = pe.matmul(ps[4 + i][:, j * P:(j + 1) * P], group(hT[0], 4 * i + j),
                                               group(hT[1], 4 * i + j), start=True, stop=True)
                            mm.then_inc(s.score_done, 1)
                    if p is not None:
                        project(p, 2)
                        project(p, 3)
                    if a is not None:
                        turn(a, 2)
                    if p is not None:
                        project(p, 4)
                    if a is not None:
                        for i in range(4):
                            pe.wait_ge(s.prob_ready, 4 * a + i + 1)
                            pe.wait_ge(s.ring_free, RING * a + 13 + i)
                            for j in range(4):
                                mm = pe.transpose(ps[4 + i][:, j * P:(j + 1) * P], pr[:, i, j * P:(j + 1) * P], ident)
                            mm.then_inc(s.ring_done, 1)
                    if p is not None:
                        project(p, 5)
                    if a is not None:
                        for i in range(2):
                            hold(pe, s.ring_free, RING * a + 17 + i, s.pspare)
                            for j in range(8):
                                mm = pe.transpose(ps[4 + i][:, j * DH:(j + 1) * DH], group(hT[2], 8 * i + j),
                                                  ident[0:DH, 0:DH])
                            mm.then_inc(s.ring_done, 1)
                        pe.wait_ge(s.ring_free, RING * a + 22)
                        for i in range(2):
                            for j in range(8):
                                g = 8 * i + j
                                mm = pe.matmul(ps[6 + i][:, j * DH:(j + 1) * DH], pT[:, g // 4, (g % 4) * P:(g % 4 + 1) * P],
                                               vg[:, g, :], start=True, stop=True)
                            mm.then_inc(s.ring_done, 1)

                tiles(pe, body)


def route(nc, ps, d, ident, bounds, idx, pay):
    with ExitStack() as ctx:
        sb = lambda n, s, t=F32: ctx.enter_context(nc.sbuf_tensor(f"r_{n}", s, t))
        s = semaphores(nc, ctx, "r", "gspare w0_in w1_in g_in c_in z_ready z_st slots_st o_in o_free r_in r_free xb_ready turned"
                       " o_psum_free y_done y_free x_in x_free xn_ready xn_free ln sq spare x2_st x3_st"
                       " x_psum_free gate_done gate_taken st_free sig step pe_step")
        wo = sb("wo", [P, KC, D])
        gw = sb("gw", [P, KC, E])
        bo = sb("bo", [P, D])
        o = sb("o", [P, D])
        oT = sb("oT", [P, KC, P])
        x1 = sb("x1", [P, D])
        x = sb("x", [P, D])
        xn = sb("xn", [P, D])
        xT = sb("xT", [P, KC, P])
        stats = sb("stats", [P, 2, 6])
        mv = sb("mv", [P, 2])
        rstd = sb("rstd", [P, 1])
        sd = sb("sd", [P, 1])
        tri = sb("tri", [P, P])
        ones = sb("ones", [P, P])
        zero = sb("zero", [P, D])
        logit = sb("logit", [P, TT, E])
        prob = sb("prob", [P, TT, E])
        W8 = 48
        g16 = sb("g16", [P, TT, 16])
        g8 = sb("g8", [P, TT, 8])
        gm = sb("gm", [P, TT, 16])
        keep = sb("keep", [P, TT, NG, 2])
        ms = sb("ms", [P, TT, W8])
        t8 = sb("t8", [P, TT, 8])
        rep = sb("rep", [P, TT, W8])
        sel = sb("sel", [P, TT, E])
        cw = sb("cw", [P, TT, E])
        cs = sb("cs", [P, TT])
        rank = sb("rank", [P, TT, E])
        quo = sb("quo", [P, TT, E])
        cnt = sb("cnt", [P, E])
        ntile = sb("ntile", [P, E])
        cum = sb("cum", [P, E])
        base = sb("base", [P, E])
        slot = sb("slot", [P, TT, W8])
        s8 = sb("s8", [P, TT, 8])
        tmp = sb("tmp", [P, TT, E])
        tokens = sb("tokens", [P, TT, TOP], I32)
        o_rows = d.o2.rearrange("b p n -> (b p n)").rearrange("(r c) -> r c", c=D)

        def staggered(engine, project, gate):
            project(0)
            project(1)
            gate(0)
            with engine.Fori(1, TT - 1) as t:
                project(t + 1)
                gate(t)
            gate(TT - 1)

        with nc.Block() as block:

            @block.sync
            def _(sp):
                def load_o(t):
                    if not isinstance(t, int):
                        sp.wait_ge(s.o_free, t)
                    sp.dma_start(o[:], o_rows[t * P:(t + 1) * P, :] if isinstance(t, int) else o_rows[bass.ds(t * P, P), :])\
                        .then_inc(s.o_in, 16)

                load_o(0)
                for h in range(2):
                    sp.dma_start(wo[:, :, h * 512:(h + 1) * 512], d.wo2[:, h * 512:(h + 1) * 512]
                                 .rearrange("(k p) n -> p k n", p=P)).then_inc((s.w0_in, s.w1_in)[h], 16)
                sp.dma_start(x1[:], d.x1[0:P, :]).then_inc(s.r_in, 16)
                sp.dma_start(gw[:], d.gate_w.rearrange("(k p) n -> p k n", p=P)).then_inc(s.g_in, 16)
                sp.dma_start(bo[:], d.bo[:, :]).then_inc(s.c_in, 16)
                sp.dma_start(tri[:], d.tri[:, :]).then_inc(s.c_in, 16)
                sp.dma_start(ones[:], d.ones[:, :]).then_inc(s.c_in, 16)
                sp.dma_start(tokens[:], d.tokens[:, :, :]).then_inc(s.c_in, 16)
                sp.dma_start(d.slots[:, :], d.slots0[:, :]).then_inc(s.slots_st, 16)
                with sp.Fori(1, TT) as t:
                    load_o(t)
                    sp.wait_ge(s.r_free, t)
                    sp.dma_start(x1[:], d.x1[bass.ds(t * P, P), :]).then_inc(s.r_in, 16)
                sp.wait_ge(s.slots_st, 16)

            @block.gpsimd
            def _(g):
                g.memset(zero[:], 0.0).then_inc(s.z_ready, 1)
                g.wait_ge(s.z_ready, 1)
                g.dma_start(d.xn3[T:T + PAD, :], zero[:]).then_inc(s.z_st, 16)
                g.dma_start(d.acc[T:T + PAD, :], zero[:]).then_inc(s.z_st, 16)
                g.sem_inc(s.st_free, 1)
                g.wait_ge(s.c_in, 64)
                with g.Fori(0, TT) as t:
                    g.wait_ge(s.r_in, t * 16 + 16)
                    g.tensor_tensor(x1[:], x1[:], bo[:], ALU.add).then_inc(s.xb_ready, 1)
                    hold(g, s.y_free, 2 * t + 4, s.gspare)
                    g.dma_start(d.acc[bass.ds(t * P, P), :], x[:]).then_inc(s.x2_st, 16)
                    hold(g, s.xn_ready, t + 1, s.gspare)
                    g.dma_start(d.xn3[bass.ds(t * P, P), :], xn[:]).then_inc(s.x3_st, 16)
                    g.wait_ge(s.x2_st, t * 16 + 16)
                    g.wait_ge(s.x3_st, t * 16 + 16)
                    g.sem_inc(s.st_free, 1)
                g.wait_ge(s.z_st, 32)

            @block.vector
            def _(v):
                v.sem_inc(s.y_free, 2)
                with v.Fori(0, TT) as t:
                    v.wait_ge(s.xb_ready, t + 1)
                    v.wait_ge(s.st_free, t + 1)
                    for h in range(2):
                        v.wait_ge(s.y_done, 2 * t + h + 1)
                        v.tensor_tensor(x[:, h * 512:(h + 1) * 512], ps[2 + h][:], x1[:, h * 512:(h + 1) * 512], ALU.add)\
                            .then_inc(s.y_free, 1)
                    v.wait_ge(s.y_free, 2 * t + 4)
                    v.sem_inc(s.r_free, 1)
                    layernorm_steps(v, x, stats, mv, sd, rstd, xn, s, t)

                n = [0]

                def link(op):
                    n[0] += 1
                    op.then_inc(s.step, 1)
                    v.wait_ge(s.step, n[0])

                v.memset(g16[:], -1.0)
                v.memset(ms[:], -2.0)
                link(v.memset(slot[:], 0.0))
                v.wait_ge(s.sig, 1)
                link(v.tensor_reduce(g16[:, :, 0:NG], prob[:].rearrange("p t (g e) -> p t g e", g=NG), AX.X, ALU.max))
                for t in range(TT):
                    op = v.max(g8[:, t, :], g16[:, t, :])
                link(op)
                link(v.memset(g8[:, :, KEEP_G:8], -1.0))
                for t in range(TT):
                    op = v.match_replace(gm[:, t, :], g8[:, t, :], g16[:, t, :], 2.0)
                link(op)
                link(v.tensor_scalar(keep[:, :, :, 0], gm[:, :, 0:NG], 2.0, None, ALU.is_equal))
                link(v.tensor_scalar(keep[:, :, :, 1], keep[:, :, :, 0], 1.0, None, ALU.subtract))
                grp = lambda z: z[:, :, 0:E].rearrange("p t (g e) -> p t g e", g=NG)
                for g in range(NG):
                    ks = [keep[:, :, g, i:i + 1].broadcast_to([P, TT, E // NG]) for i in range(2)]
                    e8 = slice(g * (E // NG), (g + 1) * (E // NG))
                    link(v.tensor_tensor(tmp[:, :, e8], prob[:, :, e8], ks[0], ALU.mult))
                    link(v.tensor_tensor(ms[:, :, e8], tmp[:, :, e8], ks[1], ALU.add))
                for t in range(TT):
                    op = v.max(t8[:, t, :], ms[:, t, :])
                link(op)
                link(v.memset(t8[:, :, TOP:8], -2.0))
                for t in range(TT):
                    op = v.match_replace(rep[:, t, :], t8[:, t, :], ms[:, t, :], 2.0)
                link(op)
                link(v.tensor_scalar(sel[:], rep[:, :, 0:E], 2.0, None, ALU.is_equal))
                v.sem_inc(s.pe_step, 1)
                link(v.tensor_tensor(cw[:], prob[:], sel[:], ALU.mult))
                link(v.tensor_reduce(cs[:], cw[:], AX.X, ALU.add))
                link(v.reciprocal(cs[:], cs[:]))
                link(v.tensor_tensor(cw[:], cw[:], cs[:].unsqueeze(2).broadcast_to([P, TT, E]), ALU.mult))
                v.wait_ge(s.pe_step, 3)
                v.tensor_copy(rank[:].rearrange("p t e -> p (t e)"), ps[0][:, 0:TT * E])
                link(v.tensor_copy(cnt[:], ps[1][:, 0:E]))
                v.memset(quo[:], 0.0)
                link(v.memset(ntile[:], 1.0))
                for j in range(1, T // P):
                    link(v.scalar_tensor_tensor(ntile[:], cnt[:], float(j * P), ntile[:], ALU.is_gt, ALU.add))
                    link(v.scalar_tensor_tensor(quo[:], rank[:], float(j * P), quo[:], ALU.is_ge, ALU.add))
                link(v.tensor_tensor_scan(cum[:], ones[:, 0:E], ntile[:], float(SH_TILES), ALU.mult, ALU.add))
                link(v.tensor_tensor(base[:], cum[:], ntile[:], ALU.subtract))
                v.memset(bounds[:, 0:1], 0)
                v.memset(bounds[:, 1:2], TT)
                v.memset(bounds[:, 2:3], SH_TILES)
                v.tensor_copy(bounds[:, 3:3 + E], cum[:])
                v.memset(bounds[:, NE + 1:NE + 2], TT - 1)
                v.memset(bounds[:, NE + 2:NE + 3], SH_TILES - 1)
                link(v.tensor_scalar(bounds[:, NE + 3:2 * NE + 1], cum[:], 1.0, None, ALU.subtract))
                link(v.tensor_scalar(rank[:], rank[:], float(NT), 1.0, ALU.mult, ALU.add))
                link(v.scalar_tensor_tensor(rank[:], quo[:], float(1 - P * NT), rank[:], ALU.mult, ALU.add))
                link(v.tensor_tensor(rank[:], rank[:], base[:].unsqueeze(1).broadcast_to([P, TT, E]), ALU.add))
                link(v.tensor_tensor(slot[:, :, 0:E], rank[:], sel[:], ALU.mult))
                for t in range(TT):
                    op = v.max(s8[:, t, :], slot[:, t, :])
                link(op)
                link(v.tensor_scalar(idx[:], s8[:, :, 0:TOP], 1.0, None, ALU.subtract))
                for k in range(TOP):
                    link(v.tensor_tensor(tmp[:], slot[:, :, 0:E], s8[:, :, k:k + 1].broadcast_to([P, TT, E]), ALU.is_equal))
                    link(v.tensor_tensor(tmp[:], tmp[:], cw[:], ALU.mult))
                    link(v.tensor_reduce(pay[:, :, k, 1], tmp[:], AX.X, ALU.add))
                link(v.tensor_copy(pay[:, :, :, 0].bitcast(I32), tokens[:]))

            @block.scalar
            def _(act):
                act.sem_inc(s.o_psum_free, 1)
                act.sem_inc(s.x_psum_free, 1)

                def take_o(t):
                    act.wait_ge(s.turned, t + 1)
                    for i in range(2):
                        cp = act.activation(oT[:, 4 * i:4 * i + 4, :], ps[i][:].rearrange("p (k m) -> p k m", m=P), ACT.Copy)
                    cp.then_inc(s.o_psum_free, 1)

                def gate(t):
                    act.wait_ge(s.sq, 3 * t + 1)
                    act.activation(sd[:], rstd[:], ACT.Sqrt).then_inc(s.sq, 1)
                    act.wait_ge(s.xn_free, t + 2)
                    for i in range(2):
                        cp = act.activation(xT[:, 4 * i:4 * i + 4, :], ps[4 + i][:].rearrange("p (k m) -> p k m", m=P), ACT.Copy)
                    cp.then_inc(s.x_psum_free, 1)
                    act.wait_ge(s.gate_done, t + 1)
                    act.activation(logit[:, at(t), :].rearrange("p t e -> p (t e)"), ps[6][:, 0:E], ACT.Copy)\
                        .then_inc(s.gate_taken, 1)

                staggered(act, take_o, gate)
                act.wait_ge(s.gate_taken, TT)
                act.activation(prob[:], logit[:], ACT.Sigmoid).then_inc(s.sig, 1)

            @block.tensor
            def _(pe):
                pe.sem_inc(s.xn_free, 1)

                def project(t):
                    pe.wait_ge(s.o_in, t * 16 + 16)
                    pe.wait_ge(s.o_psum_free, t + 1)
                    for k in range(KC):
                        mm = pe.transpose(ps[k // 4][:, (k % 4) * P:(k % 4 + 1) * P], o[:, k * P:(k + 1) * P], ident)
                    mm.then_inc(s.turned, 1)
                    pe.wait_ge(s.o_psum_free, t + 2)
                    pe.sem_inc(s.o_free, 1)
                    for h in range(2):
                        if isinstance(t, int) and t == 0:
                            pe.wait_ge((s.w0_in, s.w1_in)[h], 16)
                        pe.wait_ge(s.y_free, 2 * t + h + 1)
                        for k in range(KC):
                            mm = pe.matmul(ps[2 + h][:], oT[:, k, :], wo[:, k, h * 512:(h + 1) * 512],
                                           start=(k == 0), stop=(k == KC - 1))
                        mm.then_inc(s.y_done, 1)

                def gate(t):
                    if isinstance(t, int) and t == 0:
                        pe.wait_ge(s.g_in, 16)
                    pe.wait_ge(s.xn_ready, t + 1)
                    pe.wait_ge(s.x_psum_free, t + 1)
                    for k in range(KC):
                        mm = pe.transpose(ps[4 + k // 4][:, (k % 4) * P:(k % 4 + 1) * P], xn[:, k * P:(k + 1) * P], ident)
                    mm.then_inc(s.xn_free, 1)
                    pe.wait_ge(s.x_psum_free, t + 2)
                    for k in range(KC):
                        mm = pe.matmul(ps[6][:, 0:E], xT[:, k, :], gw[:, k, :], start=(k == 0), stop=(k == KC - 1))
                    mm.then_inc(s.gate_done, 1)

                staggered(pe, project, gate)
                pe.wait_ge(s.c_in, 64)
                pe.wait_ge(s.pe_step, 1)
                for t in range(TT):
                    for u in range(t):
                        pe.matmul(ps[0][:, t * E:(t + 1) * E], ones[:], sel[:, u, :], start=(u == 0), stop=False)
                    mm = pe.matmul(ps[0][:, t * E:(t + 1) * E], tri[:], sel[:, t, :], start=(t == 0), stop=True)
                mm.then_inc(s.pe_step, 1)
                for t in range(TT):
                    mm = pe.matmul(ps[1][:, 0:E], ones[:], sel[:, t, :], start=(t == 0), stop=(t == TT - 1))
                mm.then_inc(s.pe_step, 1)


def experts(nc, ps, d, ident, bounds, idx, pay):
    with ExitStack() as ctx:
        sb = lambda n, s, t=F32: ctx.enter_context(nc.sbuf_tensor(f"e_{n}", s, t))
        s = semaphores(nc, ctx, "e", "raw_in0 raw_in1 raw_in2 w_hi w_lo tab_in sent_ready sent_st x_in cols gate_done up_done up_free turned"
                       " xT_hi xT_lo h_turned hT_hi hT_lo down_done y_ready y_free y_st out_st gspare gcol silu_done")
        SENT = 4
        SENDERS = TT * TOP // SENT
        assert SENDERS + 3 <= SH_TILES
        pair = lambda n, s: [sb(n + "_hi", s, F32R), sb(n + "_lo", s, F32R)]
        wg = pair("wg", [P, KC, F])
        wu = pair("wu", [P, KC, F])
        wd = pair("wd", [P, FC, D])
        raw = [sb(f"raw{i}", [P, 3 * D]) for i in range(3)]
        tab = sb("tab", [P, NT, 2], I32)
        sent_idx = sb("sent_idx", [P, SENT], I32)
        sent = sb("sent", [P, SENT, 2], I32)
        gidx = sb("gidx", [P, 1], I32)
        sidx = sb("sidx", [P, 1], I32)
        wcol = sb("wcol", [P, 1])
        x = sb("x", [P, D])
        xT = pair("xT", [P, KC, P])
        g = sb("g", [P, F])
        h = sb("h", [P, F])
        hT = pair("hT", [P, FC, P])
        y = sb("y", [P, D])
        raw_in = (s.raw_in0, s.raw_in1, s.raw_in2)
        PIECES = 6
        COUNTS = (32, 32, 48)

        def parts(j):
            slot = raw[j % 3]
            if j < 4:
                k = (j % 2) * 4
                return [((wg, wu)[j // 2], slice(0, P), slice(k, k + 4),
                         slot[:, 0:4 * F].rearrange("p (k n) -> p k n", n=F))]
            v = slot[:].rearrange("p (k n) -> p k n", n=D)
            if j == 4:
                return [(wd, slice(0, P), slice(0, 3), v)]
            return [(wd, slice(0, P), slice(3, 5), v[:, 0:2, :]), (wd, slice(0, 64), slice(5, 6), v[0:64, 2:3, :])]

        def loaded(e, j):
            return e * COUNTS[j % 3] + (16 if j < 3 else COUNTS[j % 3])

        def each_tile(engine, body, split=True):
            start = lambda e: engine.value_load(bounds[0:1, bass.ds(e, 1)], min_val=0, max_val=MAX_TILES)
            with engine.Fori(0, NE - 1) as e:
                first = start(e)
                if split:
                    final = engine.value_load(bounds[0:1, bass.ds(e + NE + 1, 1)], min_val=0, max_val=MAX_TILES - 1)
                    with engine.If(first < final):
                        with engine.Fori(first, final) as i:
                            body(e, i, False)
                    body(e, final, True)
                else:
                    with engine.Fori(first, start(e + 1)) as i:
                        body(e, i, False)
            with engine.Fori(start(NE - 1), start(NE)) as i:
                body(NE - 1, i, False)

        with nc.Block() as block:

            @block.sync
            def _(sp):
                def load(e, j):
                    if not (isinstance(e, int) and j < 3):
                        sp.wait_ge(s.w_lo, PIECES * e + j - 2)
                    for w, rows, ks, dst in parts(j):
                        if j < 4:
                            r0, r1 = ks.start * P, ks.stop * P
                            src = (d.e_gate, d.e_up)[j // 2][e, r0:r1, :].rearrange("(k p) n -> p k n", p=P)
                        else:
                            r0, r1 = ks.start * P, min(ks.stop * P, F)
                            src = d.e_down[e, r0:r1, :].rearrange("(k p) n -> p k n", p=rows.stop)
                        sp.dma_start(dst, src).then_inc(raw_in[j % 3], 16)

                for j in range(PIECES):
                    load(0, j)
                with sp.Fori(1, NE) as e:
                    for j in range(PIECES):
                        load(e, j)
                total = sp.value_load(bounds[0:1, NE:NE + 1], min_val=1, max_val=MAX_TILES)
                sp.wait_ge(s.y_free, total + 1)
                sp.dma_start(d.out[:, :], d.acc[0:T, :]).then_inc(s.out_st, 16)
                sp.wait_ge(s.out_st, 16)

            @block.gpsimd
            def _(q):
                q.sem_inc(s.y_free, 1)
                rows = lambda z: z.rearrange("(p t) c -> p t c", p=P)
                q.dma_start(tab[:, 0:SH_TILES, :], rows(d.slots0)[:, 0:SH_TILES, :]).then_inc(s.tab_in, 16)
                q.wait_ge(s.tab_in, 16)

                def gather(i):
                    q.tensor_copy(gidx[:], tab[:, i:i + 1, 0] if isinstance(i, int) else tab[:, bass.ds(i, 1), 0])\
                        .then_inc(s.gcol, 1)
                    hold(q, s.gcol, i + 1, s.gspare)
                    q.indirect_dma_start(x[:], None, d.xn3[:, :], bass.IndirectOffsetOnAxis(ap=gidx[:, 0:1], axis=0))\
                        .then_inc(s.x_in, 16)

                gather(0)
                hold(q, s.x_in, 16, s.gspare)
                hold(q, s.turned, 2, s.gspare)
                gather(1)

                def body(e, i, _):
                    q.tensor_copy(sidx[:], tab[:, bass.ds(i, 1), 0])
                    q.tensor_copy(wcol[:].bitcast(I32), tab[:, bass.ds(i, 1), 1]).then_inc(s.cols, 1)
                    hold(q, s.cols, i + 1, s.gspare)
                    hold(q, s.x_in, i * 16 + 32, s.gspare)
                    hold(q, s.turned, i * 2 + 4, s.gspare)
                    gather(i + 2)
                    hold(q, s.y_ready, i * 2 + 2, s.gspare)
                    q.indirect_dma_start(d.acc[:, :], bass.IndirectOffsetOnAxis(ap=sidx[:, 0:1], axis=0), y[:], None,
                                         compute_op=ALU.add).then_inc(s.y_st, 16)
                    q.wait_ge(s.y_st, i * 16 + 16)
                    q.sem_inc(s.y_free, 1)

                def send(i):
                    q.tensor_copy(sent_idx[:], idx[:].rearrange("p t k -> p (t k)")[:, bass.ds(i * SENT, SENT)])
                    q.tensor_copy(sent[:], pay[:].bitcast(I32).rearrange("p t k c -> p (t k) c")[:, bass.ds(i * SENT, SENT), :])\
                        .then_inc(s.sent_ready, 1)
                    hold(q, s.sent_ready, i + 1, s.gspare)
                    for k in range(SENT):
                        q.indirect_dma_start(d.slots[:, :], bass.IndirectOffsetOnAxis(ap=sent_idx[:, k:k + 1], axis=0),
                                             sent[:, k, :], None).then_inc(s.sent_st, 16)
                    hold(q, s.sent_st, i * 16 * SENT + 16 * SENT, s.gspare)

                with q.Fori(0, SENDERS) as i:
                    body(0, i, False)
                    send(i)
                q.dma_start(tab[:, SH_TILES:NT, :], rows(d.slots)[:, SH_TILES:NT, :]).then_inc(s.tab_in, 16)
                q.wait_ge(s.tab_in, 32)
                total = q.value_load(bounds[0:1, NE:NE + 1], min_val=SH_TILES + 1, max_val=MAX_TILES)
                with q.Fori(SENDERS, total) as i:
                    body(0, i, False)
                q.wait_ge(s.x_in, total * 16 + 32)

            @block.vector
            def _(v):
                v.sem_inc(s.up_free, 2)

                def split_weights(e, j):
                    v.wait_ge(s.w_hi, PIECES * e + j + 1)
                    for w, rows, ks, src in parts(j):
                        op = v.tensor_tensor(w[1][rows, ks, :], src, w[0][rows, ks, :], ALU.subtract)
                    op.then_inc(s.w_lo, 1)

                def split_tokens(tile):
                    for half in range(2):
                        v.wait_ge(s.xT_hi, 2 * tile + half + 1)
                        v.tensor_tensor(xT[1][:, 4 * half:4 * half + 4, :], ps[6 + half][:].rearrange("p (k m) -> p k m", m=P),
                                        xT[0][:, 4 * half:4 * half + 4, :], ALU.subtract).then_inc(s.xT_lo, 1)

                split_tokens(0)
                for j in range(PIECES):
                    split_weights(0, j)

                def body(e, i, split):
                    for n in range(2):
                        if split and n == 1:
                            split_weights(e + 1, 0)
                        v.wait_ge(s.silu_done, 2 * i + n + 1)
                        v.wait_ge(s.up_done, 2 * i + n + 1)
                        v.tensor_tensor(h[:, n * FH:(n + 1) * FH], g[:, n * FH:(n + 1) * FH], ps[2 + n][:, 0:FH], ALU.mult)\
                            .then_inc(s.up_free, 1)
                    v.wait_ge(s.hT_hi, 2 * i + 1)
                    v.tensor_tensor(hT[1][:, 0:4, :], ps[0][:].rearrange("p (k m) -> p k m", m=P), hT[0][:, 0:4, :], ALU.subtract)\
                        .then_inc(s.hT_lo, 1)
                    v.wait_ge(s.hT_hi, 2 * i + 2)
                    v.tensor_tensor(hT[1][:, 4:6, :], ps[1][:, 0:2 * P].rearrange("p (k m) -> p k m", m=P), hT[0][:, 4:6, :],
                                    ALU.subtract).then_inc(s.hT_lo, 1)
                    split_tokens(i + 1)
                    if split:
                        split_weights(e + 1, 1)
                        split_weights(e + 1, 2)
                        split_weights(e + 1, 3)
                    v.wait_ge(s.cols, i + 1)
                    v.wait_ge(s.y_free, i + 1)
                    v.wait_ge(s.down_done, 2 * i + 2)
                    v.tensor_scalar(y[:, 512:D], ps[5][:], wcol[:, 0:1], None, ALU.mult).then_inc(s.y_ready, 1)
                    if split:
                        split_weights(e + 1, 4)
                        split_weights(e + 1, 5)

                each_tile(v, body)

            @block.scalar
            def _(act):
                def split_weights(e, j):
                    act.wait_ge(raw_in[j % 3], loaded(e, j))
                    for w, rows, ks, src in parts(j):
                        op = act.activation(w[0][rows, ks, :], src, ACT.Copy)
                    op.then_inc(s.w_hi, 1)

                def take_turned(tile, half):
                    act.wait_ge(s.turned, 2 * tile + half + 1)
                    act.activation(xT[0][:, 4 * half:4 * half + 4, :], ps[6 + half][:].rearrange("p (k m) -> p k m", m=P),
                                   ACT.Copy).then_inc(s.xT_hi, 1)

                take_turned(0, 0)
                take_turned(0, 1)
                for j in range(PIECES):
                    split_weights(0, j)

                def body(e, i, split):
                    for n in range(2):
                        act.wait_ge(s.gate_done, 2 * i + n + 1)
                        act.wait_ge(s.up_free, 2 * i + n + 1)
                        act.activation(g[:, n * FH:(n + 1) * FH], ps[n][:, 0:FH], ACT.Silu).then_inc(s.silu_done, 1)
                    if split:
                        split_weights(e + 1, 0)
                        split_weights(e + 1, 1)
                    take_turned(i + 1, 0)
                    act.wait_ge(s.h_turned, 2 * i + 1)
                    act.activation(hT[0][:, 0:4, :], ps[0][:].rearrange("p (k m) -> p k m", m=P), ACT.Copy).then_inc(s.hT_hi, 1)
                    act.wait_ge(s.h_turned, 2 * i + 2)
                    act.activation(hT[0][:, 4:6, :], ps[1][:, 0:2 * P].rearrange("p (k m) -> p k m", m=P), ACT.Copy)\
                        .then_inc(s.hT_hi, 1)
                    take_turned(i + 1, 1)
                    if split:
                        split_weights(e + 1, 2)
                        split_weights(e + 1, 3)
                    act.wait_ge(s.cols, i + 1)
                    act.wait_ge(s.y_free, i + 1)
                    act.wait_ge(s.down_done, 2 * i + 1)
                    act.activation(y[:, 0:512], ps[4][:], ACT.Copy, scale=wcol[:, 0:1]).then_inc(s.y_ready, 1)
                    if split:
                        act.wait_ge(s.down_done, 2 * i + 2)
                        split_weights(e + 1, 4)
                        split_weights(e + 1, 5)

                each_tile(act, body)

            @block.tensor
            def _(pe):
                def turn_tokens(i, half):
                    if half == 0:
                        pe.wait_ge(s.x_in, i * 16 + 16)
                    for k in range(4 * half, 4 * half + 4):
                        mm = pe.transpose(ps[6 + half][:, (k % 4) * P:(k % 4 + 1) * P], x[:, k * P:(k + 1) * P], ident)
                    mm.then_inc(s.turned, 1)

                def product(bank, at, w, widths, cols, lo_ready, hi_ready={}):
                    n = len(widths)
                    for k in range(n):
                        if k in hi_ready:
                            pe.wait_ge(*hi_ready[k])
                        for side in range(2):
                            pe.matmul(bank, at[0][0:widths[k], k, :], w[side][0:widths[k], k, cols],
                                      start=(k == 0 and side == 0), stop=False)
                    pe.wait_ge(*lo_ready)
                    for k in range(n):
                        mm = pe.matmul(bank, at[1][0:widths[k], k, :], w[0][0:widths[k], k, cols],
                                       start=False, stop=(k == n - 1))
                    return mm

                turn_tokens(0, 0)
                turn_tokens(0, 1)
                pe.sem_inc(s.hT_lo, 2)

                def body(e, i, _):
                    pe.wait_ge(s.xT_lo, 2 * i + 2)
                    for n in range(2):
                        pe.wait_ge(s.hT_lo, 2 * i + 2)
                        pe.wait_ge(s.w_lo, PIECES * e + 2)
                        product(ps[n][:, 0:FH], xT, wg, [P] * KC, slice(n * FH, (n + 1) * FH), (s.xT_lo, 2 * i + 2))\
                            .then_inc(s.gate_done, 1)
                    for n in range(2):
                        pe.wait_ge(s.up_free, 2 * i + n + 1)
                        pe.wait_ge(s.w_lo, PIECES * e + 4)
                        product(ps[2 + n][:, 0:FH], xT, wu, [P] * KC, slice(n * FH, (n + 1) * FH), (s.xT_lo, 2 * i + 2))\
                            .then_inc(s.up_done, 1)
                    turn_tokens(i + 1, 0)
                    pe.wait_ge(s.silu_done, 2 * i + 2)
                    pe.wait_ge(s.up_free, 2 * i + 3)
                    for k in range(FC):
                        if k == FH // P:
                            pe.wait_ge(s.up_free, 2 * i + 4)
                        mm = pe.transpose(ps[k // 4][0:FCW[k], (k % 4) * P:(k % 4 + 1) * P],
                                          h[:, k * P:k * P + FCW[k]], ident)
                        if k in (3, FC - 1):
                            mm.then_inc(s.h_turned, 1)
                    turn_tokens(i + 1, 1)
                    pe.wait_ge(s.w_lo, PIECES * e + 6)
                    for n in range(2):
                        product(ps[4 + n][:], hT, wd, FCW, slice(n * 512, (n + 1) * 512), (s.hT_lo, 2 * i + 4),
                                {0: (s.hT_hi, 2 * i + 1), 4: (s.hT_hi, 2 * i + 2)}).then_inc(s.down_done, 1)

                each_tile(pe, body, split=False)


def program(nc, d, stages="ahrm"):
    with ExitStack() as ctx:
        ps = [ctx.enter_context(nc.psum_tensor(f"bank{i}", [P, 512], F32)) for i in range(8)]
        ident = ctx.enter_context(nc.sbuf_tensor("ident", [P, P], F32))
        const_in = nc.alloc_semaphore("const_in")
        with nc.Block() as block:

            @block.sync
            def _(sp):
                sp.dma_start(ident[:], d.ident[:, :]).then_inc(const_in, 16)
                sp.wait_ge(const_in, 16)

        for half in range(2):
            with nc.sbuf_tensor(f"a{half}_qa", [P, CC, HALF_B, XH, LQ], F32) as qa:
                with ExitStack() as a:
                    sb = lambda n, s: a.enter_context(nc.sbuf_tensor(f"a{half}_{n}", s, F32))
                    qr = sb("qr", [R, HALF_B, XH, LQ])
                    cst = named({"rope_q": sb("rope_q", [P, HT]), "rope_k": sb("rope_k", [P, LK]), "iota": sb("iota", [P, LK])})
                    cin = nc.alloc_semaphore(f"a{half}_const_in")
                    with nc.Block() as block:

                        @block.sync
                        def _(sp):
                            sp.dma_start(cst.rope_q[:], d.rope_q[:, :]).then_inc(cin, 16)
                            sp.dma_start(cst.rope_k[:], d.rope_k[:, :]).then_inc(cin, 16)
                            sp.dma_start(cst.iota[:], d.iota[:, :]).then_inc(cin, 16)
                            sp.wait_ge(cin, 48)

                    queries(nc, ps, d, half, qa, qr, ident[:], cst)
                    contexts(nc, ps, d, half, qa, qr, ident[:], cst)
                merge(nc, ps, d, half, qa)
        if "h" in stages:
            heads(nc, ps, d, ident[:])
        if "r" in stages:
            with ExitStack() as m:
                bounds = m.enter_context(nc.sbuf_tensor("bounds", [P, 2 * NE + 1], I32))
                idx = m.enter_context(nc.sbuf_tensor("idx", [P, TT, TOP], I32))
                pay = m.enter_context(nc.sbuf_tensor("pay", [P, TT, TOP, 2], F32))
                route(nc, ps, d, ident[:], bounds, idx, pay)
                if "m" in stages:
                    experts(nc, ps, d, ident[:], bounds, idx, pay)


def laid_out(x, ctx_2048, itok_BxS_0_1023, L0_xattn_W_kvc, L0_xattn_W_dq, L0_xattn_W_uq, L0_xattn_W_qr, L0_xattn_W_uk,
             L0_xattn_W_kr, L0_xattn_W_uv, L0_xattn_W_o, L0_attn_Wq, L0_attn_bq, L0_attn_Wk, L0_attn_bk, L0_attn_Wv,
             L0_attn_bv, L0_attn_Wo, L0_attn_bo, L0_ffn_gate_w, L0_ffn_w_gate, L0_ffn_w_up, L0_ffn_w_down,
             L0_ffn_sw_gate, L0_ffn_sw_up, L0_ffn_sw_down):
    c = np.ascontiguousarray
    o = {}
    o["x"] = np.asarray(x).reshape(T, D)
    o["ctxT"] = c(np.asarray(ctx_2048).transpose(0, 2, 1))
    seg = np.asarray(itok_BxS_0_1023).T
    o["seg"] = c(np.concatenate([seg, seg], 0))
    o["wkvc"], o["wdq"] = np.asarray(L0_xattn_W_kvc), np.asarray(L0_xattn_W_dq)
    uq = np.asarray(L0_xattn_W_uq).reshape(QCC, P, XH, HD).transpose(2, 1, 0, 3)
    qr = np.asarray(L0_xattn_W_qr).reshape(QCC, P, XH, 2, R // 2).transpose(2, 1, 0, 3, 4)
    qr = np.concatenate([qr, qr[..., ::-1, :]], 3).reshape(XH, P, QCC, P)
    uk = np.asarray(L0_xattn_W_uk).reshape(KVC, XH, HD).transpose(1, 2, 0)
    o["head_w"] = c(np.concatenate([uq.reshape(XH, P, QCC * P), qr.reshape(XH, P, QCC * P), uk], 2))
    kr = np.asarray(L0_xattn_W_kr)
    o["wkr"] = c(np.concatenate([kr, kr[:, R // 2:], kr[:, :R // 2]], 1))
    o["head_v"] = c(np.asarray(L0_xattn_W_uv).reshape(CC, P, XH, HD).transpose(2, 1, 0, 3).reshape(XH, P, CC * P))
    o["wo"] = np.asarray(L0_xattn_W_o)
    split = lambda a: a.reshape((NH, DH // 2, 2) + a.shape[1:]).swapaxes(1, 2).reshape(a.shape)
    o["wq"], o["wk"] = c(split(np.asarray(L0_attn_Wq)).T), c(split(np.asarray(L0_attn_Wk)).T)
    o["wv"], o["wo2"] = c(np.asarray(L0_attn_Wv).T), c(np.asarray(L0_attn_Wo).T)
    rows = lambda a: c(np.broadcast_to(a, (P, D)))
    o["bq"], o["bk"] = rows(split(np.asarray(L0_attn_bq))), rows(split(np.asarray(L0_attn_bk)))
    o["bv"], o["bo"] = rows(np.asarray(L0_attn_bv)), rows(np.asarray(L0_attn_bo))
    cat = np.concatenate
    halves = lambda a: [np.asarray(a)[None, :, :F], np.asarray(a)[None, :, F:]]
    o["gate_w"] = np.asarray(L0_ffn_gate_w)
    o["e_gate"] = cat(halves(L0_ffn_sw_gate) + [np.asarray(L0_ffn_w_gate)])
    o["e_up"] = cat(halves(L0_ffn_sw_up) + [np.asarray(L0_ffn_w_up)])
    o["e_down"] = cat([np.asarray(L0_ffn_sw_down).reshape(SHARED, F, D), np.asarray(L0_ffn_w_down)])

    o["ident"] = np.eye(P, dtype=np.float32)
    o["iota"] = c(np.broadcast_to(np.arange(LK, dtype=np.float32), (P, LK)))

    def angles(half, length):
        inv = (np.float32(1.0) / np.float32(10000.0) ** (np.arange(half, dtype=np.float32) / np.float32(half)))
        return np.arange(length, dtype=np.float32)[:, None] * inv.astype(np.float32)

    ang = angles(R // 2, LK).T
    cs, sn = np.cos(ang), np.sin(ang)
    o["rope_k"] = c(cat([cs, cs, -sn, sn], 0)).astype(np.float32)
    o["rope_q"] = c(np.tile(o["rope_k"][:, :LQ], (1, HALF_B)))
    a2 = angles(DH // 2, LQ)
    order = (np.arange(8)[None, :] * 8 + np.arange(8)[:, None]).reshape(-1)
    a2 = np.tile(a2[order], (2, 1))
    o["cos2"] = c(np.tile(cat([np.cos(a2)] * 2, 1), (1, NH))).astype(np.float32)
    o["sin2"] = c(np.tile(cat([-np.sin(a2), np.sin(a2)], 1), (1, NH))).astype(np.float32)
    tok = np.arange(P) % 8
    same = tok[:, None] == tok[None, :]
    o["bmask"] = c(np.tile(np.where(same, 0.0, NEG).astype(np.float32), (1, 4)))
    o["tri"] = np.triu(np.ones((P, P), np.float32), 1)
    o["ones"] = np.ones((P, P), np.float32)
    slot = np.zeros((P, NT, 2), np.int32)
    slot[:, :, 0] = T + np.arange(P)[:, None]
    slot[:, :SH_TILES, 0] = (np.arange(SH_TILES)[None, :] % TT) * P + np.arange(P)[:, None]
    slot[:, :SH_TILES, 1] = np.float32(1.0).view(np.int32)
    o["slots0"] = slot.reshape(P * NT, 2)
    o["tokens"] = c((np.arange(TT)[None, :, None] * P + np.arange(P)[:, None, None]) * np.ones((1, 1, TOP))).astype(np.int32)
    return o


SCRATCH = {"x1": ([T, D], F32), "o2": ([B, P, 512], F32), "xn3": ([T + PAD, D], F32), "acc": ([T + PAD, D], F32),
           "slots": ([P * NT, 2], I32)}


def build(nc, arrays, stages="ahrm", scratch="Internal"):
    d = {}
    for name, a in arrays.items():
        d[name] = nc.dram_tensor(f"in_{name}", a.shape, mybir.dt.from_np(a.dtype), kind="ExternalInput").ap()
    for name, (shape, dt) in SCRATCH.items():
        d[name] = nc.dram_tensor(f"tmp_{name}", shape, dt, kind=scratch).ap()
    d["out"] = nc.dram_tensor("out", [T, D], F32, kind="ExternalOutput").ap()
    program(nc, named(d), stages)


def kernel(**inputs):
    import concourse.bacc as bacc
    from concourse.bass_utils import run_bass_kernel_spmd

    arrays = laid_out(**inputs)
    nc = bacc.Bacc("TRN2", target_bir_lowering=False, num_devices=1)
    build(nc, arrays)
    r = run_bass_kernel_spmd(nc, [{f"in_{k}": v for k, v in arrays.items()}], core_ids=[0])
    return r.results[0]["out"].reshape(B, LQ, D)
```

```python
from collections import namedtuple
from contextlib import ExitStack

import concourse.bass as bass
import numpy as np
from concourse import mybir

F32 = mybir.dt.float32
F32R = mybir.dt.float32r
I32 = mybir.dt.int32
ALU = mybir.AluOpType
ACT = mybir.ActivationFunctionType
AX = mybir.AxisListType

P = 128
B, LQ, LK, D = 16, 64, 512, 1024
T = B * LQ
KC = D // P
HALF_B = B // 2
HT = HALF_B * LQ
THREE = ((0, 0), (0, 1), (1, 0))
XH, HD, R = 16, 128, 64
KVC, QC = 256, 384
CC, QCC = KVC // P, QC // P
LOOKBACK = 8
NEG = -1e30
X_SCALE = float(np.float32(1.0) / np.sqrt(HD + R).astype(np.float32))
NH, DH = 16, 64
TT = T // P
E, TOP, NG, KEEP_G = 32, 6, 4, 2
F = 704
FH = F // 2
FC = 6
FCW = [128] * 5 + [64]
SHARED = 2
NE = E + SHARED
SH_TILES = SHARED * TT
MAX_TILES = SH_TILES + (T * TOP + E * (P - 1)) // P
NT = 98
assert MAX_TILES + 2 <= NT
PAD = P
EPS = 1e-5


def named(items):
    return namedtuple("Named", items)(**items)


def semaphores(nc, ctx, prefix, names):
    made = {n: nc.alloc_semaphore(f"{prefix}_{n}") for n in names.split()}

    def clear():
        nc.clear_and_free_semaphores(list(made.values()))
        nc.all_engine_barrier()

    ctx.callback(clear)
    return named(made)


def hold(engine, sem, value, spare):
    engine.wait_ge(sem, value)
    engine.sem_inc(spare, 1)


def at(i):
    return slice(i, i + 1) if isinstance(i, int) else bass.ds(i, 1)


def queries(nc, ps, d, half, qa, qr, ident, cst):
    with ExitStack() as ctx:
        sb = lambda n, s, t=F32: ctx.enter_context(nc.sbuf_tensor(f"q{half}_{n}", s, t))
        s = semaphores(nc, ctx, f"q{half}", "x_in wdq_in hw_in0 hw_in1 x_free xn_ready xn_free x_psum_free qc_done qc_hi qc_lo"
                       " w_hi w_lo nope_done qn_hi qn_lo rope_done rope_free qa_done qa_free ln sq hw_free spare qr_done")
        pair = lambda n, s: [sb(n + "_hi", s, F32R), sb(n + "_lo", s, F32R)]
        x = sb("x", [P, D])
        xn = sb("xn", [P, D])
        xT = sb("xT", [P, KC, HT])
        stats = sb("stats", [P, 2, 6])
        mv = sb("mv", [P, 2])
        rstd = sb("rstd", [P, 1])
        sd = sb("sd", [P, 1])
        wdq = sb("wdq", [P, KC, QC])
        qcT = pair("qcT", [P, QCC, HT])
        hw = [sb(f"hw{i}", [P, 1024]) for i in range(2)]
        w = [pair(f"w{i}", [P, 1024]) for i in range(2)]
        qn = pair("qn", [P, HT])
        rp = sb("rp", [R, 2, HT])
        hw_in = (s.hw_in0, s.hw_in1)
        TILES = HT // P

        def each_head(engine, body):
            with engine.Fori(0, XH // 2 - 1) as hp:
                body(hp * 2, 0, True)
                body(hp * 2 + 1, 1, True)
            body(XH - 2, 0, True)
            body(XH - 1, 1, False)

        with nc.Block() as block:

            @block.sync
            def _(sp):
                sp.dma_start(x[:], d.x[half * HT:half * HT + P, :]).then_inc(s.x_in, 16)
                sp.dma_start(wdq[:], d.wdq.rearrange("(k p) n -> p k n", p=P)).then_inc(s.wdq_in, 16)
                with sp.Fori(1, TILES) as t:
                    sp.wait_ge(s.x_free, t)
                    sp.dma_start(x[:], d.x[bass.ds(half * HT + t * P, P), :]).then_inc(s.x_in, 16)
                with sp.Fori(0, XH // 2) as hp:
                    for i in range(2):
                        sp.wait_ge(s.hw_free, hp * 2 + i + 1)
                        sp.dma_start(hw[i][:], d.head_w[hp * 2 + i]).then_inc(hw_in[i], 16)

            @block.vector
            def _(v):
                v.sem_inc(s.rope_free, 1)
                v.sem_inc(s.hw_free, 2)
                with v.Fori(0, TILES) as t:
                    layernorm(v, x, stats, mv, sd, rstd, xn, s, t)
                for m in range(QCC):
                    v.wait_ge(s.qc_hi, m + 1)
                    v.tensor_tensor(qcT[1][:, m, :], ps[4 + m][:], qcT[0][:, m, :], ALU.subtract).then_inc(s.qc_lo, 1)

                def split_weights(h, side):
                    v.wait_ge(s.w_hi, h + 1)
                    v.tensor_tensor(w[side][1][:], hw[side][:], w[side][0][:], ALU.subtract).then_inc(s.w_lo, 1)
                    v.wait_ge(s.w_lo, h + 1)
                    v.sem_inc(s.hw_free, 1)

                split_weights(0, 0)

                def body(h, side, follows):
                    v.wait_ge(s.qn_hi, h + 1)
                    v.tensor_tensor(qn[1][:], ps[0][:], qn[0][:], ALU.subtract).then_inc(s.qn_lo, 1)
                    if follows:
                        split_weights(h + 1, 1 - side)
                    v.wait_ge(s.rope_done, h + 1)
                    v.tensor_tensor(rp[:, 0, :], ps[1][0:R, :], cst.rope_q[0:R, :], ALU.mult)
                    v.tensor_tensor(rp[:, 1, :], ps[1][R:P, :], cst.rope_q[R:P, :], ALU.mult)\
                        .then_inc(s.rope_free, 1)
                    v.wait_ge(s.rope_free, h + 2)
                    v.tensor_tensor(qr[:, :, at(h), :].rearrange("p b h q -> p b (h q)"),
                                    rp[:, 0, :].rearrange("p (b q) -> p b q", q=LQ),
                                    rp[:, 1, :].rearrange("p (b q) -> p b q", q=LQ), ALU.add).then_inc(s.qr_done, 1)
                    v.wait_ge(s.qr_done, h + 1)
                    v.wait_ge(s.qa_done, 2 * h + 2)
                    v.tensor_copy(qa[:, 1, :, at(h), :].rearrange("p b h q -> p b (h q)"),
                                  ps[3][:].rearrange("p (b q) -> p b q", q=LQ)).then_inc(s.qa_free, 1)

                each_head(v, body)

            @block.scalar
            def _(act):
                act.sem_inc(s.x_psum_free, 1)
                act.sem_inc(s.qa_free, 2)
                with act.Fori(0, TILES) as t:
                    act.wait_ge(s.sq, 3 * t + 1)
                    act.activation(sd[:], rstd[:], ACT.Sqrt).then_inc(s.sq, 1)
                    act.wait_ge(s.xn_free, t + 2)
                    for i in range(2):
                        cp = act.activation(xT[:, 4 * i:4 * i + 4, bass.ds(t * P, P)],
                                            ps[i][:].rearrange("p (k m) -> p k m", m=P), ACT.Copy)
                    cp.then_inc(s.x_psum_free, 1)
                def split_weights(h, side):
                    act.wait_ge(hw_in[side], h * 8 + (16 - 8 * side))
                    act.activation(w[side][0][:], hw[side][:], ACT.Copy).then_inc(s.w_hi, 1)

                split_weights(0, 0)
                for m in range(QCC):
                    act.wait_ge(s.qc_done, m + 1)
                    act.activation(qcT[0][:, m, :], ps[4 + m][:], ACT.Copy).then_inc(s.qc_hi, 1)

                def body(h, side, follows):
                    act.wait_ge(s.nope_done, h + 1)
                    act.activation(qn[0][:], ps[0][:], ACT.Copy).then_inc(s.qn_hi, 1)
                    if follows:
                        act.wait_ge(s.qa_free, 2 * h + 2)
                        split_weights(h + 1, 1 - side)
                    act.wait_ge(s.qa_done, 2 * h + 1)
                    act.activation(qa[:, 0, :, at(h), :].rearrange("p b h q -> p b (h q)"),
                                   ps[2][:].rearrange("p (b q) -> p b q", q=LQ), ACT.Copy).then_inc(s.qa_free, 1)

                each_head(act, body)

            @block.tensor
            def _(pe):
                pe.sem_inc(s.xn_free, 1)
                for t in range(TILES):
                    pe.wait_ge(s.x_psum_free, t + 1)
                    pe.wait_ge(s.xn_ready, t + 1)
                    for k in range(KC):
                        mm = pe.transpose(ps[k // 4][:, (k % 4) * P:(k % 4 + 1) * P], xn[:, k * P:(k + 1) * P], ident)
                    mm.then_inc(s.xn_free, 1)
                    if t == 0:
                        pe.wait_ge(s.wdq_in, 16)
                    pe.wait_ge(s.x_psum_free, t + 2)
                    cols = slice(t * P, (t + 1) * P)
                    for m in range(QCC):
                        for k in range(KC):
                            mm = pe.matmul(ps[4 + m][:, cols], wdq[:, k, m * P:(m + 1) * P], xT[:, k, cols],
                                           start=(k == 0), stop=(k == KC - 1))
                        if t == TILES - 1:
                            mm.then_inc(s.qc_done, 1)
                pe.sem_inc(s.qn_lo, 1)

                def product(bank, cols, rhs):
                    for n, (i, j) in enumerate(((0, 0), (1, 0), (0, 1))):
                        for m, (lhs, r) in enumerate(zip(cols, rhs)):
                            mm = pe.matmul(bank, lhs[i], r[j], start=(n == 0 and m == 0), stop=(n == 2 and m == len(rhs) - 1))
                    return mm

                def body(h, side, follows):
                    part = lambda m: [z[:, m * P:(m + 1) * P] for z in w[side]]
                    qc = [[z[:, m, :] for z in qcT] for m in range(QCC)]
                    pe.wait_ge(s.w_lo, h + 1)
                    pe.wait_ge(s.qn_lo, h + 1)
                    product(ps[0][:], [part(m) for m in range(QCC)], qc).then_inc(s.nope_done, 1)
                    pe.wait_ge(s.rope_free, h + 1)
                    product(ps[1][:], [part(3 + m) for m in range(QCC)], qc).then_inc(s.rope_done, 1)
                    pe.wait_ge(s.qn_lo, h + 2)
                    pe.wait_ge(s.qa_free, 2 * h + 2)
                    for c in range(CC):
                        product(ps[2 + c][:], [part(6 + c)], [[z[:] for z in qn]]).then_inc(s.qa_done, 1)

                pe.wait_ge(s.qc_lo, QCC)
                each_head(pe, body)


def layernorm(v, x, stats, mv, sd, rstd, xn, s, t):
    v.wait_ge(s.x_in, t * 16 + 16)
    layernorm_steps(v, x, stats, mv, sd, rstd, xn, s, t)


def layernorm_steps(v, x, stats, mv, sd, rstd, xn, s, t):
    v.bn_stats(stats[:, 0, :], x[:, 0:D // 2])
    v.bn_stats(stats[:, 1, :], x[:, D // 2:D]).then_inc(s.ln, 1)
    hold(v, s.ln, 2 * t + 1, s.spare)
    v.bn_aggr(mv[:], stats[:]).then_inc(s.ln, 1)
    v.wait_ge(s.ln, 2 * t + 2)
    v.tensor_scalar(rstd[:], mv[:, 1:2], EPS, None, ALU.add).then_inc(s.sq, 1)
    v.wait_ge(s.sq, 3 * t + 2)
    v.reciprocal(rstd[:], sd[:]).then_inc(s.sq, 1)
    v.wait_ge(s.sq, 3 * t + 3)
    v.wait_ge(s.xn_free, t + 1)
    v.tensor_scalar(xn[:], x[:], mv[:, 0:1], rstd[:], ALU.subtract, ALU.mult).then_inc(s.xn_ready, 1)
    v.wait_ge(s.xn_ready, t + 1)
    v.sem_inc(s.x_free, 1)


def contexts(nc, ps, d, half, qa, qr, ident, cst):
    with ExitStack() as ctx:
        sb = lambda n, s, t=F32: ctx.enter_context(nc.sbuf_tensor(f"c{half}_{n}", s, t))
        s = semaphores(nc, ctx, f"c{half}", "w_in0 w_in1 wkr_in ctx_in0 ctx_in1 ctx_free seg_in seg_ready mstep kv_done kvT_raw kvT_hi kvT_lo"
                       " kr_done kr_free kr_step kvx_done kv_hi kv_lo q_hi q_lo q_free score_done score_free sm rowmax"
                       " exp_done prob_ready prob_free pT_hi pT_lo out_done out_free spare")
        pair = lambda n, s: [sb(n + "_hi", s, F32R), sb(n + "_lo", s, F32R)]
        w_in, ctx_in = (s.w_in0, s.w_in1), (s.ctx_in0, s.ctx_in1)
        wkvc = sb("wkvc", [P, KC, KVC])
        wkr = sb("wkr", [P, CC, P])
        cT = sb("cT", [P, KC, LK])
        seg_i = sb("seg_i", [P, B], I32)
        seg = sb("seg", [P, 2, B])
        late = sb("late", [P, LK])
        mask = sb("mask", [P, LK])
        kvT_raw = sb("kvT_raw", [P, CC, LK])
        kvT = pair("kvT", [P, CC, LK])
        kv = pair("kv", [P, 4, KVC])
        kr_raw = sb("kr_raw", [R, LK])
        kr = pair("kr", [R, LK])
        rp = sb("rp", [R, 2, LK])
        qs = pair("qs", [P, CC, XH * LQ])
        qrs = pair("qrs", [R, XH * LQ])
        DEEP = 3
        sc = sb("sc", [P, DEEP, LK])
        nmax = sb("nmax", [P, DEEP])
        rsum = sb("rsum", [P, DEEP])
        pT = pair("pT", [P, 4, 4 * P])
        RT = XH * LQ // P
        SC_BANK, OUT_BANK, TURN_BANK, KR_BANK = (5, 6, 2), ((0, 1), (4, 3)), (7, 3), 7

        def deep_free(b, r):
            return b * RT + max(r + 1, DEEP)

        def each_row(engine, prepare, attend):
            prepare(0)
            with engine.Fori(0, HALF_B - 1) as b:
                attend(b, True)
            attend(HALF_B - 1, False)

        def query_parts(b):
            v = lambda z: z.rearrange("p (h q) -> p h q", q=LQ)
            row = lambda z: z.rearrange("p b h q -> p (b h) q")
            return [(row(qa[:, c, at(b), :, :]), v(qs[0][:, c, :]), v(qs[1][:, c, :])) for c in range(CC)] + \
                [(row(qr[:, at(b), :, :]), v(qrs[0][:]), v(qrs[1][:]))]

        with nc.Block() as block:

            @block.sync
            def _(sp):
                def load_half(dst, src, i, sem):
                    sp.dma_start(dst[:, 4 * i:4 * i + 4, :], src[4 * P * i:4 * P * (i + 1), :]
                                 .rearrange("(k p) n -> p k n", p=P)).then_inc(sem, 16)

                for i in range(2):
                    load_half(wkvc, d.wkvc, i, w_in[i])
                    load_half(cT, d.ctxT[half * HALF_B], i, ctx_in[i])
                sp.dma_start(seg_i[:], d.seg[:, :]).then_inc(s.seg_in, 16)
                sp.dma_start(wkr[:], d.wkr.rearrange("(k p) n -> p k n", p=P)).then_inc(s.wkr_in, 16)
                with sp.Fori(1, HALF_B) as b:
                    sp.wait_ge(s.ctx_free, b)
                    for i in range(2):
                        load_half(cT, d.ctxT[b + half * HALF_B], i, ctx_in[i])

            @block.gpsimd
            def _(g):
                with g.Fori(0, HALF_B) as b:
                    hold(g, s.q_free, b + 1, s.spare)
                    for src, hi, _ in query_parts(b):
                        g.tensor_copy(hi, src).then_inc(s.q_hi, 1)

            @block.vector
            def _(v):
                v.sem_inc(s.kr_free, 1)
                v.sem_inc(s.score_free, DEEP)
                v.sem_inc(s.q_free, 1)
                v.wait_ge(s.seg_in, 16)
                v.tensor_copy(seg[:, 0, :], seg_i[:]).then_inc(s.seg_ready, 1)
                v.wait_ge(s.seg_ready, 1)
                v.tensor_scalar(seg[:, 1, :], seg[:, 0, :], -float(LOOKBACK), None, ALU.add).then_inc(s.seg_ready, 1)
                v.wait_ge(s.seg_ready, 2)

                def make_mask(n):
                    bb = n + half * HALF_B
                    v.tensor_scalar(mask[:], cst.iota[:], seg[:, 0, at(bb)], NEG, ALU.is_gt, ALU.mult)
                    v.tensor_scalar(late[:], cst.iota[:], seg[:, 1, at(bb)], NEG, ALU.is_lt, ALU.mult).then_inc(s.mstep, 1)
                    v.wait_ge(s.mstep, 2 * n + 1)
                    v.tensor_tensor(mask[:], mask[:], late[:], ALU.add).then_inc(s.mstep, 1)

                def split_latents(n, c):
                    v.wait_ge(s.kvT_hi, CC * n + c + 1)
                    v.tensor_tensor(kvT[1][:, c, :], kvT_raw[:, c, :], kvT[0][:, c, :], ALU.subtract).then_inc(s.kvT_lo, 1)

                def split_queries(n):
                    for i, (src, hi, lo) in enumerate(query_parts(n)):
                        v.wait_ge(s.q_hi, 3 * n + i + 1)
                        v.tensor_tensor(lo, src, hi, ALU.subtract).then_inc(s.q_lo, 1)

                def turn_keys(n):
                    v.wait_ge(s.kr_done, n + 1)
                    v.tensor_tensor(rp[:, 0, :], ps[KR_BANK][0:R, :], cst.rope_k[0:R, :], ALU.mult)
                    v.tensor_tensor(rp[:, 1, :], ps[KR_BANK][R:P, :], cst.rope_k[R:P, :], ALU.mult).then_inc(s.kr_free, 1)
                    v.wait_ge(s.kr_free, n + 2)
                    v.tensor_tensor(kr_raw[:], rp[:, 0, :], rp[:, 1, :], ALU.add).then_inc(s.kr_step, 1)
                    v.wait_ge(s.kr_step, 3 * n + 1)
                    v.tensor_copy(kr[0][:], kr_raw[:]).then_inc(s.kr_step, 1)
                    v.wait_ge(s.kr_step, 3 * n + 2)
                    v.tensor_tensor(kr[1][:], kr_raw[:], kr[0][:], ALU.subtract).then_inc(s.kr_step, 1)

                def split_turned(n):
                    for i in range(2):
                        v.wait_ge(s.kv_hi, 2 * n + i + 1)
                        v.tensor_tensor(kv[1][:, 2 * i:2 * i + 2, :], ps[i][:].rearrange("p (k c) -> p k c", c=KVC),
                                        kv[0][:, 2 * i:2 * i + 2, :], ALU.subtract).then_inc(s.kv_lo, 1)

                def prepare(n):
                    make_mask(n)
                    for c in range(CC):
                        split_latents(n, c)
                    split_queries(n)
                    turn_keys(n)
                    split_turned(n)

                def attend(b, follows):
                    v.wait_ge(s.mstep, 2 * b + 2)
                    v.wait_ge(s.kr_step, 3 * b + 3)

                    def softmax_head(r):
                        k = r % DEEP
                        v.wait_ge(s.score_done, b * RT + r + 1)
                        if r == RT - 1:
                            v.sem_inc(s.q_free, 1)
                        v.scalar_tensor_tensor(sc[:, k, :], ps[SC_BANK[k]][:], X_SCALE, mask[:],
                                               ALU.mult, ALU.add).then_inc(s.score_free, 1)
                        v.wait_ge(s.score_free, b * RT + r + DEEP + 1)
                        v.tensor_reduce(nmax[:, k:k + 1], sc[:, k, :], AX.X, ALU.max, negate=True).then_inc(s.rowmax, 1)

                    def softmax_tail(r):
                        k = r % DEEP
                        v.wait_ge(s.exp_done, b * RT + r + 1)
                        v.reciprocal(rsum[:, k:k + 1], rsum[:, k:k + 1]).then_inc(s.sm, 1)
                        v.wait_ge(s.sm, b * RT + r + 1)
                        v.tensor_scalar(sc[:, k, :], sc[:, k, :], rsum[:, k:k + 1], None, ALU.mult).then_inc(s.prob_ready, 1)

                    def split_pT(r):
                        at_r = slice((r % 4) * P, (r % 4 + 1) * P)
                        v.wait_ge(s.pT_hi, b * RT + r + 1)
                        v.tensor_tensor(pT[1][:, :, at_r], ps[TURN_BANK[r % 2]][:].rearrange("p (k m) -> p k m", m=P),
                                        pT[0][:, :, at_r], ALU.subtract).then_inc(s.pT_lo, 1)

                    for r in range(RT + 1):
                        if r < RT:
                            softmax_head(r)
                        if r > 0:
                            softmax_tail(r - 1)
                        if r > 1:
                            split_pT(r - 2)
                    if follows:
                        split_latents(b + 1, 0)
                    split_pT(RT - 1)
                    if follows:
                        make_mask(b + 1)
                        split_latents(b + 1, 1)
                        split_queries(b + 1)
                        turn_keys(b + 1)
                        split_turned(b + 1)

                each_row(v, prepare, attend)

            @block.scalar
            def _(act):
                act.sem_inc(s.out_free, 4)

                def take_latents(n, c):
                    act.wait_ge(s.kv_done, n * CC + c + 1)
                    act.activation(kvT_raw[:, c, :], ps[c][:], ACT.Copy).then_inc(s.kvT_raw, 1)
                    act.activation(kvT[0][:, c, :], ps[c][:], ACT.Copy).then_inc(s.kvT_hi, 1)

                def take_turned(n):
                    act.wait_ge(s.kvx_done, n + 1)
                    for i in range(2):
                        act.activation(kv[0][:, 2 * i:2 * i + 2, :], ps[i][:].rearrange("p (k c) -> p k c", c=KVC),
                                       ACT.Copy).then_inc(s.kv_hi, 1)

                def prepare(n):
                    for c in range(CC):
                        take_latents(n, c)
                    take_turned(n)

                def attend(b, follows):
                    def exps(r):
                        k = r % DEEP
                        act.wait_ge(s.prob_free, deep_free(b, r))
                        act.wait_ge(s.rowmax, b * RT + r + 1)
                        act.activation(sc[:, k, :], sc[:, k, :], ACT.Exp, bias=nmax[:, k:k + 1],
                                       scale=1.0, accum_out=rsum[:, k:k + 1]).then_inc(s.exp_done, 1)

                    def take_pT(r):
                        act.wait_ge(s.prob_free, b * RT + r + DEEP + 1)
                        act.activation(pT[0][:, :, (r % 4) * P:(r % 4 + 1) * P],
                                       ps[TURN_BANK[r % 2]][:].rearrange("p (k m) -> p k m", m=P), ACT.Copy).then_inc(s.pT_hi, 1)

                    def take_out(n):
                        for c in range(CC):
                            act.wait_ge(s.out_done, b * 4 + n * 2 + c + 1)
                            act.activation(qa[:, c, at(b), n * 8:n * 8 + 8, :].rearrange("p b h q -> p b (h q)"),
                                           ps[OUT_BANK[n][c]][:].rearrange("p (b r) -> p b r", b=1), ACT.Copy)\
                                .then_inc(s.out_free, 1)

                    exps(0)
                    exps(1)
                    for r in range(RT):
                        take_pT(r)
                        if r + 2 < RT:
                            exps(r + 2)
                        if r == 3:
                            take_out(0)
                        if r >= 6 and follows:
                            take_latents(b + 1, r - 6)
                    take_out(1)
                    if follows:
                        take_turned(b + 1)

                each_row(act, prepare, attend)

            @block.tensor
            def _(pe):
                pe.sem_inc(s.prob_free, DEEP)
                pe.sem_inc(s.pT_lo, 2)

                def latents(n, c, ks):
                    for k in ks:
                        if c == 0 and k % 4 == 0:
                            pe.wait_ge(w_in[k // 4], 16)
                            pe.wait_ge(ctx_in[k // 4], n * 16 + 16)
                        mm = pe.matmul(ps[c][:], wkvc[:, k, c * P:(c + 1) * P], cT[:, k, :],
                                       start=(k == 0), stop=(k == KC - 1))
                    if ks[-1] == KC - 1:
                        mm.then_inc(s.kv_done, 1)

                def keys(n):
                    pe.wait_ge(s.kvT_raw, CC * n + CC)
                    pe.sem_inc(s.ctx_free, 1)
                    pe.wait_ge(s.kr_free, n + 1)
                    pe.wait_ge(s.pT_lo, n * RT + 2)
                    pe.wait_ge(s.wkr_in, 16)
                    for c in range(CC):
                        mm = pe.matmul(ps[KR_BANK][:], wkr[:, c, :], kvT_raw[:, c, :], start=(c == 0), stop=(c == CC - 1))
                    mm.then_inc(s.kr_done, 1)

                def turn_latents(n):
                    pe.wait_ge(s.kvT_hi, CC * n + CC)
                    for k in range(4):
                        for c in range(CC):
                            mm = pe.transpose(ps[k // 2][:, (k % 2) * KVC + c * P:(k % 2) * KVC + (c + 1) * P],
                                              kvT_raw[:, c, k * P:(k + 1) * P], ident)
                    mm.then_inc(s.kvx_done, 1)

                def prepare(n):
                    for c in range(CC):
                        latents(n, c, range(KC))
                    keys(n)
                    turn_latents(n)

                def attend(b, follows):
                    def scores(r):
                        bank = ps[SC_BANK[r % DEEP]]
                        rows = slice(r * P, (r + 1) * P)
                        pe.wait_ge(s.score_free, deep_free(b, r))
                        for c in range(CC):
                            for q, k in THREE:
                                pe.matmul(bank[:], qs[q][:, c, rows], kvT[k][:, c, :], start=(c == 0 and q == 0 and k == 0),
                                          stop=False)
                        if r == 0:
                            pe.wait_ge(s.kr_step, 3 * b + 3)
                        for q, k in THREE:
                            mm = pe.matmul(bank[:], qrs[q][:, rows], kr[k][:], start=False, stop=(q == 1))
                        mm.then_inc(s.score_done, 1)

                    def turn(r):
                        pe.wait_ge(s.prob_ready, b * RT + r + 1)
                        pe.wait_ge(s.pT_lo, b * RT + r + 1)
                        if r == 1:
                            pe.wait_ge(s.out_free, 4 * b + 4)
                        for k in range(4):
                            mm = pe.transpose(ps[TURN_BANK[r % 2]][:, k * P:(k + 1) * P], sc[:, r % DEEP, k * P:(k + 1) * P], ident)
                        mm.then_inc(s.prob_free, 1)

                    def weighted(n):
                        if n == 0:
                            pe.wait_ge(s.kv_lo, 2 * b + 2)
                        pe.wait_ge(s.pT_hi, b * RT + 4 * n + 4)
                        for c in range(CC):
                            bank, cols = ps[OUT_BANK[n][c]], slice(c * P, (c + 1) * P)
                            if n == 1 and c == 1:
                                if follows:
                                    keys(b + 1)
                                pe.wait_ge(s.pT_lo, b * RT + RT + 2)
                            for i in range(2):
                                for k in range(4):
                                    pe.matmul(bank[:], kv[i][:, k, cols], pT[0][:, k, :], start=(i == 0 and k == 0), stop=False)
                            pe.wait_ge(s.pT_lo, b * RT + 4 * n + 6)
                            for k in range(4):
                                mm = pe.matmul(bank[:], kv[0][:, k, cols], pT[1][:, k, :], start=False, stop=(k == 3))
                            mm.then_inc(s.out_done, 1)

                    pe.wait_ge(s.kvT_lo, CC * b + CC)
                    pe.wait_ge(s.q_lo, 3 * b + 3)
                    for r in range(DEEP):
                        scores(r)
                    for r in range(RT):
                        turn(r)
                        if r == 3:
                            weighted(0)
                        if r + DEEP < RT:
                            scores(r + DEEP)
                        elif follows and r == 5:
                            pe.wait_ge(s.out_free, 4 * b + 6)
                            latents(b + 1, 0, range(0, 4))
                        elif follows and r == 6:
                            latents(b + 1, 0, range(4, 8))
                    if follows:
                        latents(b + 1, 1, range(KC))
                    weighted(1)
                    if follows:
                        turn_latents(b + 1)

                each_row(pe, prepare, attend)


def merge(nc, ps, d, half, qa):
    with ExitStack() as ctx:
        sb = lambda n, s, t=F32: ctx.enter_context(nc.sbuf_tensor(f"m{half}_{n}", s, t))
        RING = 4
        s = semaphores(nc, ctx, f"m{half}", "wv_in0 wv_in1 wv_in2 wv_in3 wv_free w_in0 w_in1 w_in2 w_in3 w_hi w_lo w_used"
                       " o_done o_hi o_lo x_in y_done y_ready y_st")
        pair = lambda n, s: [sb(n + "_hi", s, F32R), sb(n + "_lo", s, F32R)]
        TILES = HT // P
        wv = [sb(f"wv{i}", [P, CC * P]) for i in range(RING)]
        raw = [sb(f"raw{i}", [P, 512]) for i in range(RING)]
        w = [pair(f"w{i}", [P, 512]) for i in range(RING)]
        oT = pair("oT", [P, XH, HT])
        x = sb("x", [P, TILES, D])
        y = sb("y", [P, TILES, D])
        wv_in = (s.wv_in0, s.wv_in1, s.wv_in2, s.wv_in3)
        w_in = (s.w_in0, s.w_in1, s.w_in2, s.w_in3)
        TURNS = XH // RING
        EARLY = TURNS - 1
        rows = lambda z: z[half * HT:(half + 1) * HT, :].rearrange("(t p) n -> p t n", p=P)

        def pieces(engine, turns, body):
            with engine.Fori(turns.start, turns.stop) as turn:
                for i in range(RING):
                    body(turn * RING + i, i)

        with nc.Block() as block:

            @block.sync
            def _(sp):
                def load_wv(h, i):
                    sp.wait_ge(s.wv_free, h + 1)
                    sp.dma_start(wv[i][:], d.head_v[h]).then_inc(wv_in[i], 16)

                for i in range(RING):
                    load_wv(i, i)
                for h in range(RING):
                    sp.dma_start(raw[h][:], d.wo[h * P:(h + 1) * P, 0:512]).then_inc(w_in[h], 16)
                pieces(sp, range(1, TURNS), load_wv)
                sp.dma_start(x[:], rows(d.x)).then_inc(s.x_in, 16)
                for n in range(2):
                    with sp.Fori(1 - n, TURNS) as turn:
                        for i in range(RING):
                            h = turn * RING + i
                            sp.wait_ge(s.w_lo, h + n * XH - RING + 1)
                            sp.dma_start(raw[i][:], d.wo[bass.ds(h * P, P), n * 512:(n + 1) * 512]).then_inc(w_in[i], 16)

            @block.vector
            def _(v):
                def split_values(h, i):
                    v.wait_ge(s.o_hi, h + 1)
                    v.tensor_tensor(oT[1][:, at(h), :].rearrange("p h m -> p (h m)"), ps[4 + i][:],
                                    oT[0][:, at(h), :].rearrange("p h m -> p (h m)"), ALU.subtract).then_inc(s.o_lo, 1)

                def split_weights(p, i):
                    v.wait_ge(s.w_hi, p + 1)
                    v.tensor_tensor(w[i][1][:], raw[i][:], w[i][0][:], ALU.subtract).then_inc(s.w_lo, 1)

                def add_residual(n):
                    for t in range(TILES):
                        v.wait_ge(s.y_done, n * TILES + t + 1)
                        v.tensor_tensor(y[:, t, n * 512:(n + 1) * 512], ps[n * TILES + t][:], x[:, t, n * 512:(n + 1) * 512],
                                        ALU.add).then_inc(s.y_ready, 1)

                pieces(v, range(0, EARLY), split_values)
                for i in range(RING):
                    split_weights(i, i)
                pieces(v, range(EARLY, TURNS), split_values)
                pieces(v, range(1, TURNS + 1), split_weights)
                v.wait_ge(s.x_in, 16)
                add_residual(0)
                pieces(v, range(TURNS + 1, 2 * TURNS), split_weights)
                add_residual(1)

            @block.scalar
            def _(act):
                act.sem_inc(s.wv_free, RING)
                act.sem_inc(s.w_used, RING)

                def take_values(h, i):
                    act.wait_ge(s.o_done, h + 1)
                    act.sem_inc(s.wv_free, 1)
                    act.activation(oT[0][:, at(h), :].rearrange("p h m -> p (h m)"), ps[4 + i][:], ACT.Copy)\
                        .then_inc(s.o_hi, 1)

                def split_weights(p, i):
                    if isinstance(p, int):
                        act.wait_ge(w_in[i], 16)
                    else:
                        act.wait_ge(w_in[i], p * 4 + (16 - 4 * i))
                    act.wait_ge(s.w_used, p + 1)
                    act.activation(w[i][0][:], raw[i][:], ACT.Copy).then_inc(s.w_hi, 1)

                pieces(act, range(0, EARLY), take_values)
                for i in range(RING):
                    split_weights(i, i)
                pieces(act, range(EARLY, TURNS), take_values)
                pieces(act, range(1, 2 * TURNS), split_weights)
                for n in range(2):
                    act.wait_ge(s.y_ready, (n + 1) * TILES)
                    act.dma_start(rows(d.x1)[:, :, n * 512:(n + 1) * 512], y[:, :, n * 512:(n + 1) * 512]).then_inc(s.y_st, 16)
                act.wait_ge(s.y_st, 32)

            @block.tensor
            def _(pe):
                pe.sem_inc(s.o_lo, RING)

                def values(h, i):
                    pe.wait_ge(wv_in[i], h * 4 + (16 - 4 * i))
                    pe.wait_ge(s.o_lo, h + 1)
                    for c in range(CC):
                        mm = pe.matmul(ps[4 + i][:], wv[i][:, c * P:(c + 1) * P],
                                       qa[:, c, :, bass.ds(h, 1), :].rearrange("p b h q -> p b (h q)"),
                                       start=(c == 0), stop=(c == CC - 1))
                    mm.then_inc(s.o_done, 1)

                pieces(pe, range(0, TURNS), values)
                pe.wait_ge(s.o_lo, XH + RING)
                for n in range(2):
                    for h in range(XH):
                        pe.wait_ge(s.w_lo, n * XH + h + 1)
                        for t in range(TILES):
                            for o, k in THREE:
                                mm = pe.matmul(ps[n * TILES + t][:], oT[o][:, h, t * P:(t + 1) * P], w[h % RING][k][:],
                                               start=(h == 0 and o == 0 and k == 0), stop=(h == XH - 1 and o == 1))
                            if h == XH - 1:
                                mm.then_inc(s.y_done, 1)
                            elif t == TILES - 1:
                                mm.then_inc(s.w_used, 1)
                        if h == XH - 1:
                            pe.wait_ge(s.y_done, (n + 1) * TILES)
                            pe.sem_inc(s.w_used, 1)


def norm_tile(v, x, stats, mv, sd, rstd, xn, s, t, loads=1):
    v.wait_ge(s.x_in, t * (16 * loads) + 16 * loads)
    layernorm_steps(v, x, stats, mv, sd, rstd, xn, s, t)


def heads(nc, ps, d, ident):
    with ExitStack() as ctx:
        sb = lambda n, s, t=F32: ctx.enter_context(nc.sbuf_tensor(f"h_{n}", s, t))
        s = semaphores(nc, ctx, "h", "gspare pspare wq0_in wq1_in wk0_in wk1_in wv0_in wv1_in"
                       " bq_in bk_in bv_in c_in x_in x_free xn_ready xn_free ln sq spare x_psum_free proj_done"
                       " proj_free q_sum q_rot k_sum k_rot v_sum ring_done ring_free score_done score_free mx"
                       " shifted exp_done sm sm2 prob_ready o_st o_free")
        w_in = (s.wq0_in, s.wq1_in, s.wk0_in, s.wk1_in, s.wv0_in, s.wv1_in)
        b_in = (s.bq_in, s.bk_in, s.bv_in)
        w = [sb(f"w{n}", [P, KC, D]) for n in "qkv"]
        bias = [sb(f"b{n}", [P, D]) for n in "qkv"]
        cos = sb("cos", [P, D])
        sin = sb("sin", [P, D])
        bmask = sb("bmask", [P, 512])
        x = sb("x", [P, D])
        xn = sb("xn", [P, D])
        xT = sb("xT", [P, KC, P])
        stats = sb("stats", [P, 2, 6])
        mv = sb("mv", [P, 2])
        rstd = sb("rstd", [P, 1])
        sd = sb("sd", [P, 1])
        qkv = [sb(f"t{n}", [P, D]) for n in "qkv"]
        swp = [sb(f"s{n}", [P, D]) for n in "qk"]
        hT = [sb(f"T{n}", [DH, 16, NH, 8]) for n in "qkv"]
        sc = sb("sc", [P, 2, 4, P])
        rmax = sb("rmax", [P, 2, 4])
        rsum = sb("rsum", [P, 4, 4])
        pr = sb("pr", [P, 4, 512])
        pT = sb("pT", [P, 4, 512])
        vg = sb("vg", [P, 16, DH])
        og = sb("og", [P, 16, DH])
        RING = 20

        def rotate(eng, n, start, done, t):
            a, b = qkv[n], swp[n]
            v4 = lambda z: z[:].rearrange("p (h i j) -> p h i j", i=2, j=DH // 2)
            eng.wait_ge(start, 2 * t + 2)
            eng.tensor_tensor(v4(b)[:, :, 0, :], v4(a)[:, :, 1, :], v4(sin)[:, :, 0, :], ALU.mult)
            eng.tensor_tensor(v4(b)[:, :, 1, :], v4(a)[:, :, 0, :], v4(sin)[:, :, 1, :], ALU.mult).then_inc(done, 1)
            eng.wait_ge(done, 3 * t + 1)
            eng.tensor_tensor(a[:], a[:], cos[:], ALU.mult).then_inc(done, 1)
            eng.wait_ge(done, 3 * t + 2)
            eng.tensor_tensor(a[:], a[:], b[:], ALU.add).then_inc(done, 1)

        def tiles(engine, body):
            body(0, None)
            with engine.Fori(0, TT - 1) as t:
                body(t + 1, t)
            body(None, TT - 1)

        with nc.Block() as block:

            @block.sync
            def _(sp):
                rows = d.x1.rearrange("(b t g) n -> b g t n", g=8, t=8)

                def load_x(t):
                    if not isinstance(t, int) or t > 0:
                        sp.wait_ge(s.x_free, t)
                    for b in range(2):
                        sp.dma_start(x[b * LQ:(b + 1) * LQ, :], rows[2 * t + b]).then_inc(s.x_in, 16)

                load_x(0)
                for n, (src, b_src) in enumerate(((d.wq, d.bq), (d.wk, d.bk), (d.wv, d.bv))):
                    if n == 2:
                        load_x(1)
                    for h in range(2):
                        sp.dma_start(w[n][:, :, h * 512:(h + 1) * 512], src[:, h * 512:(h + 1) * 512]
                                     .rearrange("(k p) n -> p k n", p=P)).then_inc(w_in[2 * n + h], 16)
                        if h == 0:
                            sp.dma_start(bias[n][:], b_src[:, :]).then_inc(b_in[n], 16)
                    if n == 0:
                        sp.dma_start(cos[:], d.cos2[:, :]).then_inc(s.c_in, 16)
                        sp.dma_start(sin[:], d.sin2[:, :]).then_inc(s.c_in, 16)
                        sp.dma_start(bmask[:], d.bmask[:, :]).then_inc(s.c_in, 16)
                with sp.Fori(2, TT) as t:
                    load_x(t)

            @block.gpsimd
            def _(g):
                g.sem_inc(s.o_free, 1)
                g.wait_ge(s.c_in, 48)

                def body(p, a):
                    if p is not None:
                        rotate(g, 1, s.k_sum, s.k_rot, p)
                    if a is not None:
                        hold(g, s.ring_free, RING * a + 24, s.gspare)
                        g.dma_start((d.o2[2 * a:2 * a + 2] if isinstance(a, int) else d.o2[bass.ds(a * 2, 2)])
                                    .rearrange("b p n -> p b n"),
                                    og[:].rearrange("p (b g) n -> p b (g n)", b=2)).then_inc(s.o_st, 16)
                        g.wait_ge(s.o_st, a * 16 + 16)
                        g.sem_inc(s.o_free, 1)

                tiles(g, body)

            @block.vector
            def _(v):
                v.sem_inc(s.proj_free, 2)
                v.sem_inc(s.score_free, 4)
                norm_tile(v, x, stats, mv, sd, rstd, xn, s, 0, 2)

                def add_bias(p, a, g):
                    n, h = g // 2, g % 2
                    if a is not None and h == 0:
                        v.wait_ge(s.ring_done, RING * a + 4 * (n + 1))
                    if isinstance(p, int) and p == 0 and h == 0:
                        v.wait_ge(b_in[n], 16)
                    v.wait_ge(s.proj_done, 6 * p + g + 1)
                    add = v.tensor_tensor(qkv[n][:, h * 512:(h + 1) * 512], ps[2 + h][:],
                                          bias[n][:, h * 512:(h + 1) * 512], ALU.add)
                    add.then_inc(s.proj_free, 1)
                    v.wait_ge(s.proj_free, 6 * p + g + 3)
                    v.sem_inc((s.q_sum, s.k_sum, s.v_sum)[n], 1)

                def head(a, i):
                    k = i % 2
                    v.wait_ge(s.score_done, 4 * a + i + 1)
                    v.tensor_tensor(sc[:, k].rearrange("p g m -> p (g m)"), ps[4 + i][:], bmask[:], ALU.add)\
                        .then_inc(s.score_free, 1)
                    v.wait_ge(s.score_free, 4 * a + i + 5)
                    v.tensor_reduce(rmax[:, k, :], sc[:, k], AX.X, ALU.max).then_inc(s.mx, 1)
                    v.wait_ge(s.mx, 4 * a + i + 1)
                    v.tensor_tensor(sc[:, k], sc[:, k], rmax[:, k, :].unsqueeze(2).broadcast_to([P, 4, P]), ALU.subtract)\
                        .then_inc(s.shifted, 1)

                def tail(a, i):
                    v.wait_ge(s.exp_done, 4 * a + i + 1)
                    e = pr[:, i, :].rearrange("p (g m) -> p g m", m=P)
                    v.tensor_reduce(rsum[:, i, :], e, AX.X, ALU.add).then_inc(s.sm, 1)
                    v.wait_ge(s.sm, 4 * a + i + 1)
                    v.reciprocal(rsum[:, i, :], rsum[:, i, :]).then_inc(s.sm2, 1)
                    v.wait_ge(s.sm2, 4 * a + i + 1)
                    v.tensor_tensor(e, e, rsum[:, i, :].unsqueeze(2).broadcast_to([P, 4, P]), ALU.mult)\
                        .then_inc(s.prob_ready, 1)

                def body(p, a, norm=None):
                    if p is not None:
                        add_bias(p, a, 0)
                        add_bias(p, a, 1)
                    if a is not None:
                        head(a, 0)
                        for i in range(4):
                            if i < 3:
                                head(a, i + 1)
                            tail(a, i)
                    if p is not None:
                        add_bias(p, a, 2)
                        add_bias(p, a, 3)
                        if isinstance(p, int) and p == 0:
                            v.wait_ge(s.c_in, 48)
                        rotate(v, 0, s.q_sum, s.q_rot, p)
                        if norm is not None:
                            norm_tile(v, x, stats, mv, sd, rstd, xn, s, norm, 2)
                        add_bias(p, a, 4)
                        add_bias(p, a, 5)

                body(0, None, 1)
                with v.Fori(0, TT - 2) as t:
                    body(t + 1, t, t + 2)
                body(TT - 1, TT - 2)
                body(None, TT - 1)

            @block.scalar
            def _(act):
                act.sem_inc(s.x_psum_free, 1)
                act.sem_inc(s.ring_free, 4)

                def root(t):
                    act.wait_ge(s.sq, 3 * t + 1)
                    act.activation(sd[:], rstd[:], ACT.Sqrt).then_inc(s.sq, 1)

                def take_x(p):
                    act.wait_ge(s.xn_free, p + 2)
                    for i in range(2):
                        cp = act.activation(xT[:, 4 * i:4 * i + 4, :], ps[i][:].rearrange("p (k m) -> p k m", m=P), ACT.Copy)
                    cp.then_inc(s.x_psum_free, 1)

                def take(a, n, dst, src):
                    act.wait_ge(s.ring_done, RING * a + n + 1)
                    act.activation(dst, src, ACT.Copy).then_inc(s.ring_free, 1)

                def take_heads(a, n):
                    for i in range(4):
                        take(a, 4 * n + i, hT[n][:, :, 4 * i:4 * i + 4, :].rearrange("p g h t -> p h g t"),
                             ps[4 + i][0:DH, :].rearrange("p (h g t) -> p h g t", g=16, t=8))

                def body(p, a, norm):
                    if p is not None:
                        take_x(p)
                    if a is not None:
                        take_heads(a, 0)
                        take_heads(a, 1)
                        for i in range(4):
                            act.wait_ge(s.shifted, 4 * a + i + 1)
                            act.activation(pr[:, i, :], sc[:, i % 2].rearrange("p g m -> p (g m)"), ACT.Exp,
                                           scale=DH ** -0.5).then_inc(s.exp_done, 1)
                        take_heads(a, 2)
                    if norm is not None:
                        root(norm)
                    if a is not None:
                        for i in range(4):
                            take(a, 12 + i, pT[:, i, :], ps[4 + i][:])
                        for i in range(2):
                            take(a, 16 + i, vg[:, 8 * i:8 * i + 8, :].rearrange("p g n -> p (g n)"), ps[4 + i][:])
                        act.wait_ge(s.o_free, a + 1)
                        for i in range(2):
                            take(a, 18 + i, og[:, 8 * i:8 * i + 8, :].rearrange("p g n -> p (g n)"), ps[6 + i][:])

                root(0)
                body(0, None, 1)
                with act.Fori(0, TT - 2) as t:
                    body(t + 1, t, t + 2)
                body(TT - 1, TT - 2, None)
                body(None, TT - 1, None)

            @block.tensor
            def _(pe):
                pe.sem_inc(s.xn_free, 1)

                def project(p, g):
                    if isinstance(p, int) and p == 0:
                        pe.wait_ge(w_in[g], 16)
                    if g == 0:
                        pe.wait_ge(s.x_psum_free, p + 2)
                    pe.wait_ge(s.proj_free, 6 * p + g + 1)
                    n, h = g // 2, g % 2
                    for k in range(KC):
                        mm = pe.matmul(ps[2 + h][:], xT[:, k, :], w[n][:, k, h * 512:(h + 1) * 512],
                                       start=(k == 0), stop=(k == KC - 1))
                    mm.then_inc(s.proj_done, 1)

                def turn(a, n):
                    if n == 0:
                        pe.wait_ge(s.q_rot, 3 * a + 3)
                    elif n == 1:
                        pe.wait_ge(s.k_rot, 3 * a + 3)
                    else:
                        pe.wait_ge(s.v_sum, 2 * a + 2)
                    for i in range(4):
                        if n < 2:
                            hold(pe, s.ring_free, RING * a + 4 * n + i + 1, s.pspare)
                        else:
                            hold(pe, s.score_free, 4 * a + i + 5, s.pspare)
                        for j in range(4):
                            h = 4 * i + j
                            mm = pe.transpose(ps[4 + i][0:DH, j * P:(j + 1) * P], qkv[n][:, h * DH:(h + 1) * DH], ident)
                        mm.then_inc(s.ring_done, 1)

                group = lambda z, g: z[:, g].rearrange("p h t -> p (h t)")

                def body(p, a):
                    if p is not None:
                        pe.wait_ge(s.x_psum_free, p + 1)
                        pe.wait_ge(s.xn_ready, p + 1)
                        for k in range(KC):
                            mm = pe.transpose(ps[k // 4][:, (k % 4) * P:(k % 4 + 1) * P], xn[:, k * P:(k + 1) * P], ident)
                        mm.then_inc(s.xn_free, 1)
                    if a is not None:
                        turn(a, 0)
                    if p is not None:
                        project(p, 0)
                    if a is not None:
                        turn(a, 1)
                    if p is not None:
                        project(p, 1)
                    if a is not None:
                        pe.wait_ge(s.ring_free, RING * a + 12)
                        for i in range(4):
                            for j in range(4):
                                mm = pe.matmul(ps[4 + i][:, j * P:(j + 1) * P], group(hT[0], 4 * i + j),
                                               group(hT[1], 4 * i + j), start=True, stop=True)
                            mm.then_inc(s.score_done, 1)
                    if p is not None:
                        project(p, 2)
                        project(p, 3)
                    if a is not None:
                        turn(a, 2)
                    if p is not None:
                        project(p, 4)
                    if a is not None:
                        for i in range(4):
                            pe.wait_ge(s.prob_ready, 4 * a + i + 1)
                            pe.wait_ge(s.ring_free, RING * a + 13 + i)
                            for j in range(4):
                                mm = pe.transpose(ps[4 + i][:, j * P:(j + 1) * P], pr[:, i, j * P:(j + 1) * P], ident)
                            mm.then_inc(s.ring_done, 1)
                    if p is not None:
                        project(p, 5)
                    if a is not None:
                        for i in range(2):
                            hold(pe, s.ring_free, RING * a + 17 + i, s.pspare)
                            for j in range(8):
                                mm = pe.transpose(ps[4 + i][:, j * DH:(j + 1) * DH], group(hT[2], 8 * i + j),
                                                  ident[0:DH, 0:DH])
                            mm.then_inc(s.ring_done, 1)
                        pe.wait_ge(s.ring_free, RING * a + 22)
                        for i in range(2):
                            for j in range(8):
                                g = 8 * i + j
                                mm = pe.matmul(ps[6 + i][:, j * DH:(j + 1) * DH], pT[:, g // 4, (g % 4) * P:(g % 4 + 1) * P],
                                               vg[:, g, :], start=True, stop=True)
                            mm.then_inc(s.ring_done, 1)

                tiles(pe, body)


def route(nc, ps, d, ident, bounds, idx, pay, raw, raw_in):
    with ExitStack() as ctx:
        sb = lambda n, s, t=F32: ctx.enter_context(nc.sbuf_tensor(f"r_{n}", s, t))
        s = semaphores(nc, ctx, "r", "gspare w0_in w1_in g_in c_in z_ready z_st slots_st o_in r_in r_free xb_ready turned"
                       " o_psum_free y_done y_free x_in x_free xn_ready xn_free ln sq spare x2_st x3_st"
                       " x_psum_free gate_done gate_taken st_free sig step pe_step")
        wo = sb("wo", [P, KC, D])
        gw = sb("gw", [P, KC, E])
        bo = sb("bo", [P, D])
        o = sb("o", [P, D])
        oT = sb("oT", [P, KC, P])
        x1 = sb("x1", [P, D])
        x = sb("x", [P, D])
        xn = sb("xn", [P, D])
        xT = sb("xT", [P, KC, P])
        stats = sb("stats", [P, 2, 6])
        mv = sb("mv", [P, 2])
        rstd = sb("rstd", [P, 1])
        sd = sb("sd", [P, 1])
        tri = sb("tri", [P, P])
        ones = sb("ones", [P, P])
        zero = sb("zero", [P, D])
        logit = sb("logit", [P, TT, E])
        prob = sb("prob", [P, TT, E])
        W8 = 48
        g16 = sb("g16", [P, TT, 16])
        g8 = sb("g8", [P, TT, 8])
        gm = sb("gm", [P, TT, 16])
        keep = sb("keep", [P, TT, NG, 2])
        ms = sb("ms", [P, TT, W8])
        t8 = sb("t8", [P, TT, 8])
        rep = sb("rep", [P, TT, W8])
        sel = sb("sel", [P, TT, E])
        csum = sb("csum", [P, TT + 1, E])
        cw = sb("cw", [P, TT, E])
        cs = sb("cs", [P, TT])
        rank = sb("rank", [P, TT, E])
        quo = sb("quo", [P, TT, E])
        cnt = sb("cnt", [P, E])
        ntile = sb("ntile", [P, E])
        cum = sb("cum", [P, E])
        base = sb("base", [P, E])
        slot = sb("slot", [P, TT, W8])
        s8 = sb("s8", [P, TT, 8])
        tmp = sb("tmp", [P, TT, E])
        mine = sb("mine", [P, TT, TOP, E])
        tokens = sb("tokens", [P, TT, TOP], I32)
        o_rows = d.o2.rearrange("b p n -> (b p n)").rearrange("(r c) -> r c", c=D)

        def staggered(engine, turn_o, project, turn_x, gate):
            turn_o(0)
            project(0, 0)
            project(0, 1)
            turn_o(1)

            def step(t, more):
                project(t + 1, 0)
                turn_x(t)
                project(t + 1, 1)
                if more:
                    turn_o(t + 2)
                gate(t)

            with engine.Fori(0, TT - 2) as t:
                step(t, True)
            step(TT - 2, False)
            turn_x(TT - 1)
            gate(TT - 1)

        with nc.Block() as block:

            @block.sync
            def _(sp):
                def load_o(t):
                    if not isinstance(t, int):
                        sp.wait_ge(s.turned, t)
                    sp.dma_start(o[:], o_rows[t * P:(t + 1) * P, :] if isinstance(t, int) else o_rows[bass.ds(t * P, P), :])\
                        .then_inc(s.o_in, 16)

                load_o(0)
                for h in range(2):
                    sp.dma_start(wo[:, :, h * 512:(h + 1) * 512], d.wo2[:, h * 512:(h + 1) * 512]
                                 .rearrange("(k p) n -> p k n", p=P)).then_inc((s.w0_in, s.w1_in)[h], 16)
                sp.dma_start(x1[:], d.x1[0:P, :]).then_inc(s.r_in, 16)
                sp.dma_start(gw[:], d.gate_w.rearrange("(k p) n -> p k n", p=P)).then_inc(s.g_in, 16)
                sp.dma_start(bo[:], d.bo[:, :]).then_inc(s.c_in, 16)
                sp.dma_start(tri[:], d.tri[:, :]).then_inc(s.c_in, 16)
                sp.dma_start(ones[:], d.ones[:, :]).then_inc(s.c_in, 16)
                sp.dma_start(tokens[:], d.tokens[:, :, :]).then_inc(s.c_in, 16)
                sp.dma_start(d.slots[:, :], d.slots0[:, :]).then_inc(s.slots_st, 16)
                with sp.Fori(1, TT) as t:
                    load_o(t)
                    sp.wait_ge(s.r_free, t)
                    sp.dma_start(x1[:], d.x1[bass.ds(t * P, P), :]).then_inc(s.r_in, 16)
                sp.wait_ge(s.slots_st, 16)
                for j, src in enumerate((d.e_gate, d.e_gate, d.e_up)):
                    k = (j % 2) * 4
                    sp.dma_start(raw[j][:, 0:4 * F].rearrange("p (k n) -> p k n", n=F),
                                 src[0, k * P:(k + 4) * P, :].rearrange("(k p) n -> p k n", p=P)).then_inc(raw_in[j], 16)
                for j in range(3):
                    sp.wait_ge(raw_in[j], 16)

            @block.gpsimd
            def _(g):
                g.memset(zero[:], 0.0).then_inc(s.z_ready, 1)
                g.wait_ge(s.z_ready, 1)
                g.dma_start(d.xn3[T:T + PAD, :], zero[:]).then_inc(s.z_st, 16)
                g.dma_start(d.out[T:T + PAD, :], zero[:]).then_inc(s.z_st, 16)
                g.sem_inc(s.st_free, 1)
                g.wait_ge(s.c_in, 64)
                with g.Fori(0, TT) as t:
                    g.wait_ge(s.r_in, t * 16 + 16)
                    g.tensor_tensor(x1[:], x1[:], bo[:], ALU.add).then_inc(s.xb_ready, 1)
                    hold(g, s.y_free, 2 * t + 4, s.gspare)
                    g.dma_start(d.out[bass.ds(t * P, P), :], x[:]).then_inc(s.x2_st, 16)
                    hold(g, s.xn_ready, t + 1, s.gspare)
                    g.dma_start(d.xn3[bass.ds(t * P, P), :], xn[:]).then_inc(s.x3_st, 16)
                    g.wait_ge(s.x2_st, t * 16 + 16)
                    g.wait_ge(s.x3_st, t * 16 + 16)
                    g.sem_inc(s.st_free, 1)
                g.wait_ge(s.z_st, 32)

            @block.vector
            def _(v):
                v.sem_inc(s.y_free, 2)
                with v.Fori(0, TT) as t:
                    v.wait_ge(s.xb_ready, t + 1)
                    v.wait_ge(s.st_free, t + 1)
                    for h in range(2):
                        v.wait_ge(s.y_done, 2 * t + h + 1)
                        v.tensor_tensor(x[:, h * 512:(h + 1) * 512], ps[2 + h][:], x1[:, h * 512:(h + 1) * 512], ALU.add)\
                            .then_inc(s.y_free, 1)
                    v.wait_ge(s.y_free, 2 * t + 4)
                    v.sem_inc(s.r_free, 1)
                    layernorm_steps(v, x, stats, mv, sd, rstd, xn, s, t)

                n = [0]

                def link(op):
                    n[0] += 1
                    op.then_inc(s.step, 1)
                    v.wait_ge(s.step, n[0])

                v.memset(g16[:], -1.0)
                v.memset(ms[:], -2.0)
                v.memset(csum[:, 0, :], 0.0)
                link(v.memset(slot[:], 0.0))
                v.wait_ge(s.sig, 1)
                link(v.tensor_reduce(g16[:, :, 0:NG], prob[:].rearrange("p t (g e) -> p t g e", g=NG), AX.X, ALU.max))
                for t in range(TT):
                    op = v.max(g8[:, t, :], g16[:, t, :])
                link(op)
                link(v.memset(g8[:, :, KEEP_G:8], -1.0))
                for t in range(TT):
                    op = v.match_replace(gm[:, t, :], g8[:, t, :], g16[:, t, :], 2.0)
                link(op)
                link(v.tensor_scalar(keep[:, :, :, 0], gm[:, :, 0:NG], 2.0, None, ALU.is_equal))
                link(v.tensor_scalar(keep[:, :, :, 1], keep[:, :, :, 0], 1.0, None, ALU.subtract))
                grp = lambda z: z[:, :, 0:E].rearrange("p t (g e) -> p t g e", g=NG)
                ks = [keep[:, :, :, i:i + 1].broadcast_to([P, TT, NG, E // NG]) for i in range(2)]
                link(v.tensor_tensor(grp(tmp), grp(prob), ks[0], ALU.mult))
                link(v.tensor_tensor(grp(ms), grp(tmp), ks[1], ALU.add))
                for t in range(TT):
                    op = v.max(t8[:, t, :], ms[:, t, :])
                link(op)
                link(v.memset(t8[:, :, TOP:8], -2.0))
                for t in range(TT):
                    op = v.match_replace(rep[:, t, :], t8[:, t, :], ms[:, t, :], 2.0)
                link(op)
                link(v.tensor_scalar(sel[:], rep[:, :, 0:E], 2.0, None, ALU.is_equal))
                for t in range(TT):
                    link(v.tensor_tensor(csum[:, t + 1, :], csum[:, t, :], sel[:, t, :], ALU.add))
                v.sem_inc(s.pe_step, 1)
                link(v.tensor_tensor(cw[:], prob[:], sel[:], ALU.mult))
                link(v.tensor_reduce(cs[:], cw[:], AX.X, ALU.add))
                link(v.reciprocal(cs[:], cs[:]))
                link(v.tensor_tensor(cw[:], cw[:], cs[:].unsqueeze(2).broadcast_to([P, TT, E]), ALU.mult))
                v.wait_ge(s.pe_step, 3)
                v.tensor_copy(rank[:].rearrange("p t e -> p (t e)"), ps[0][:, 0:TT * E])
                link(v.tensor_copy(cnt[:], ps[1][:, 0:E]))
                v.memset(quo[:], 0.0)
                link(v.memset(ntile[:], 1.0))
                for j in range(1, T // P):
                    link(v.scalar_tensor_tensor(ntile[:], cnt[:], float(j * P), ntile[:], ALU.is_gt, ALU.add))
                    link(v.scalar_tensor_tensor(quo[:], rank[:], float(j * P), quo[:], ALU.is_ge, ALU.add))
                link(v.tensor_tensor_scan(cum[:], ones[:, 0:E], ntile[:], float(SH_TILES), ALU.mult, ALU.add))
                link(v.tensor_tensor(base[:], cum[:], ntile[:], ALU.subtract))
                v.memset(bounds[:, 0:1], 0)
                v.memset(bounds[:, 1:2], TT)
                v.memset(bounds[:, 2:3], SH_TILES)
                v.tensor_copy(bounds[:, 3:3 + E], cum[:])
                v.memset(bounds[:, NE + 1:NE + 2], TT - 1)
                v.memset(bounds[:, NE + 2:NE + 3], SH_TILES - 1)
                link(v.tensor_scalar(bounds[:, NE + 3:2 * NE + 1], cum[:], 1.0, None, ALU.subtract))
                link(v.tensor_scalar(rank[:], rank[:], float(NT), 1.0, ALU.mult, ALU.add))
                link(v.scalar_tensor_tensor(rank[:], quo[:], float(1 - P * NT), rank[:], ALU.mult, ALU.add))
                link(v.tensor_tensor(rank[:], rank[:], base[:].unsqueeze(1).broadcast_to([P, TT, E]), ALU.add))
                link(v.tensor_tensor(slot[:, :, 0:E], rank[:], sel[:], ALU.mult))
                for t in range(TT):
                    op = v.max(s8[:, t, :], slot[:, t, :])
                link(op)
                link(v.tensor_scalar(idx[:], s8[:, :, 0:TOP], 1.0, None, ALU.subtract))
                every = lambda z: z.unsqueeze(2).broadcast_to([P, TT, TOP, E])
                link(v.tensor_tensor(mine[:], every(slot[:, :, 0:E]), s8[:, :, 0:TOP].unsqueeze(3).broadcast_to([P, TT, TOP, E]),
                                     ALU.is_equal))
                link(v.tensor_tensor(mine[:], mine[:], every(cw[:]), ALU.mult))
                link(v.tensor_reduce(pay[:, :, :, 1], mine[:], AX.X, ALU.add))
                link(v.tensor_copy(pay[:, :, :, 0].bitcast(I32), tokens[:]))

            @block.scalar
            def _(act):
                act.sem_inc(s.o_psum_free, 1)
                act.sem_inc(s.x_psum_free, 1)

                def take_o(t):
                    act.wait_ge(s.turned, t + 1)
                    for i in range(2):
                        cp = act.activation(oT[:, 4 * i:4 * i + 4, :], ps[i][:].rearrange("p (k m) -> p k m", m=P), ACT.Copy)
                    cp.then_inc(s.o_psum_free, 1)

                def take_x(t):
                    act.wait_ge(s.sq, 3 * t + 1)
                    act.activation(sd[:], rstd[:], ACT.Sqrt).then_inc(s.sq, 1)
                    act.wait_ge(s.xn_free, t + 2)
                    for i in range(2):
                        cp = act.activation(xT[:, 4 * i:4 * i + 4, :], ps[4 + i][:].rearrange("p (k m) -> p k m", m=P), ACT.Copy)
                    cp.then_inc(s.x_psum_free, 1)

                def take_gate(t):
                    act.wait_ge(s.gate_done, t + 1)
                    act.activation(logit[:, at(t), :].rearrange("p t e -> p (t e)"), ps[6][:, 0:E], ACT.Copy)\
                        .then_inc(s.gate_taken, 1)

                staggered(act, take_o, lambda *_: None, take_x, take_gate)
                act.wait_ge(s.gate_taken, TT)
                act.activation(prob[:], logit[:], ACT.Sigmoid).then_inc(s.sig, 1)

            @block.tensor
            def _(pe):
                pe.sem_inc(s.xn_free, 1)

                def turn_o(t):
                    pe.wait_ge(s.o_in, t * 16 + 16)
                    pe.wait_ge(s.o_psum_free, t + 1)
                    for k in range(KC):
                        mm = pe.transpose(ps[k // 4][:, (k % 4) * P:(k % 4 + 1) * P], o[:, k * P:(k + 1) * P], ident)
                    mm.then_inc(s.turned, 1)

                def project(t, h):
                    if isinstance(t, int) and t == 0:
                        pe.wait_ge((s.w0_in, s.w1_in)[h], 16)
                    pe.wait_ge(s.o_psum_free, t + 2)
                    pe.wait_ge(s.y_free, 2 * t + h + 1)
                    for k in range(KC):
                        mm = pe.matmul(ps[2 + h][:], oT[:, k, :], wo[:, k, h * 512:(h + 1) * 512],
                                       start=(k == 0), stop=(k == KC - 1))
                    mm.then_inc(s.y_done, 1)

                def turn_x(t):
                    pe.wait_ge(s.xn_ready, t + 1)
                    pe.wait_ge(s.x_psum_free, t + 1)
                    for k in range(KC):
                        mm = pe.transpose(ps[4 + k // 4][:, (k % 4) * P:(k % 4 + 1) * P], xn[:, k * P:(k + 1) * P], ident)
                    mm.then_inc(s.xn_free, 1)

                def gate(t):
                    pe.wait_ge(s.g_in, 16)
                    pe.wait_ge(s.x_psum_free, t + 2)
                    for k in range(KC):
                        mm = pe.matmul(ps[6][:, 0:E], xT[:, k, :], gw[:, k, :], start=(k == 0), stop=(k == KC - 1))
                    mm.then_inc(s.gate_done, 1)

                staggered(pe, turn_o, project, turn_x, gate)
                pe.wait_ge(s.c_in, 64)
                pe.wait_ge(s.pe_step, 1)
                pe.matmul(ps[0][:, 0:TT * E], tri[:], sel[:].rearrange("p t e -> p (t e)"), start=True, stop=False)
                pe.matmul(ps[0][:, 0:TT * E], ones[:], csum[:, 0:TT, :].rearrange("p t e -> p (t e)"), start=False, stop=True)\
                    .then_inc(s.pe_step, 1)
                pe.matmul(ps[1][:, 0:E], ones[:], csum[:, TT, :], start=True, stop=True).then_inc(s.pe_step, 1)


def experts(nc, ps, d, ident, bounds, idx, pay, raw, raw_in):
    with ExitStack() as ctx:
        sb = lambda n, s, t=F32: ctx.enter_context(nc.sbuf_tensor(f"e_{n}", s, t))
        s = semaphores(nc, ctx, "e", "w_hi w_lo tab_in sent_ready sent_st x_in cols gate_done up_done up_free turned"
                       " xT_hi xT_lo h_turned hT_hi hT_lo down_done y_ready y_free y_st gspare gcol silu_done")
        SENT = 4
        SENDERS = TT * TOP // SENT
        assert SENDERS + 3 <= SH_TILES
        pair = lambda n, s: [sb(n + "_hi", s, F32R), sb(n + "_lo", s, F32R)]
        wg = pair("wg", [P, KC, F])
        wu = pair("wu", [P, KC, F])
        wd = pair("wd", [P, FC, D])
        tab = sb("tab", [P, NT, 2], I32)
        sent_idx = sb("sent_idx", [P, SENT], I32)
        sent = sb("sent", [P, SENT, 2], I32)
        gidx = sb("gidx", [P, 1], I32)
        sidx = sb("sidx", [P, 1], I32)
        wcol = sb("wcol", [P, 1])
        x = sb("x", [P, D])
        xT = pair("xT", [P, KC, P])
        g = sb("g", [P, F])
        h = sb("h", [P, F])
        hT = pair("hT", [P, FC, P])
        H_CHUNKS = (0, 1, 2, 5, 3, 4)
        FIRST = FH // P
        y = sb("y", [P, D])
        PIECES = 6
        COUNTS = (32, 32, 48)

        turned_h = [(ps[0][:, 0:FIRST * P].rearrange("p (k m) -> p k m", m=P), slice(0, FIRST)),
                    (ps[1][:, 0:(FC - FIRST) * P].rearrange("p (k m) -> p k m", m=P), slice(FIRST, FC))]

        def parts(j):
            slot = raw[j % 3]
            if j < 4:
                k = (j % 2) * 4
                return [((wg, wu)[j // 2], slice(0, P), slice(k, k + 4),
                         slot[:, 0:4 * F].rearrange("p (k n) -> p k n", n=F))]
            v = slot[:].rearrange("p (k n) -> p k n", n=D)
            if j == 4:
                return [(wd, slice(0, P), slice(0, 3), v)]
            return [(wd, slice(0, P), slice(3, 5), v[:, 0:2, :]), (wd, slice(0, 64), slice(5, 6), v[0:64, 2:3, :])]

        def loaded(e, j):
            return e * COUNTS[j % 3] + (16 if j < 3 else COUNTS[j % 3])

        def each_tile(engine, body, split=True):
            start = lambda e: engine.value_load(bounds[0:1, bass.ds(e, 1)], min_val=0, max_val=MAX_TILES)
            with engine.Fori(0, NE - 1) as e:
                first = start(e)
                if split:
                    final = engine.value_load(bounds[0:1, bass.ds(e + NE + 1, 1)], min_val=0, max_val=MAX_TILES - 1)
                    with engine.If(first < final):
                        with engine.Fori(first, final) as i:
                            body(e, i, False)
                    body(e, final, True)
                else:
                    with engine.Fori(first, start(e + 1)) as i:
                        body(e, i, False)
            with engine.Fori(start(NE - 1), start(NE)) as i:
                body(NE - 1, i, False)

        with nc.Block() as block:

            @block.sync
            def _(sp):
                def load(e, j):
                    sp.wait_ge(s.w_lo, PIECES * e + j - 2)
                    for w, rows, ks, dst in parts(j):
                        if j < 4:
                            r0, r1 = ks.start * P, ks.stop * P
                            src = (d.e_gate, d.e_up)[j // 2][e, r0:r1, :].rearrange("(k p) n -> p k n", p=P)
                        else:
                            r0, r1 = ks.start * P, min(ks.stop * P, F)
                            src = d.e_down[e, r0:r1, :].rearrange("(k p) n -> p k n", p=rows.stop)
                        sp.dma_start(dst, src).then_inc(raw_in[j % 3], 16)

                for j in range(3, PIECES):
                    load(0, j)
                with sp.Fori(1, NE) as e:
                    for j in range(PIECES):
                        load(e, j)

            @block.gpsimd
            def _(q):
                q.sem_inc(s.y_free, 1)
                rows = lambda z: z.rearrange("(p t) c -> p t c", p=P)
                q.dma_start(tab[:, 0:SH_TILES, :], rows(d.slots0)[:, 0:SH_TILES, :]).then_inc(s.tab_in, 16)
                q.wait_ge(s.tab_in, 16)

                def gather(i):
                    q.tensor_copy(gidx[:], tab[:, i:i + 1, 0] if isinstance(i, int) else tab[:, bass.ds(i, 1), 0])\
                        .then_inc(s.gcol, 1)
                    hold(q, s.gcol, i + 1, s.gspare)
                    q.indirect_dma_start(x[:], None, d.xn3[:, :], bass.IndirectOffsetOnAxis(ap=gidx[:, 0:1], axis=0))\
                        .then_inc(s.x_in, 16)

                gather(0)
                hold(q, s.x_in, 16, s.gspare)
                hold(q, s.turned, 2, s.gspare)
                gather(1)

                def body(e, i, _):
                    q.tensor_copy(sidx[:], tab[:, bass.ds(i, 1), 0])
                    q.tensor_copy(wcol[:].bitcast(I32), tab[:, bass.ds(i, 1), 1]).then_inc(s.cols, 1)
                    hold(q, s.cols, i + 1, s.gspare)
                    hold(q, s.x_in, i * 16 + 32, s.gspare)
                    hold(q, s.turned, i * 2 + 4, s.gspare)
                    gather(i + 2)
                    hold(q, s.y_ready, i * 2 + 2, s.gspare)
                    q.indirect_dma_start(d.out[:, :], bass.IndirectOffsetOnAxis(ap=sidx[:, 0:1], axis=0), y[:], None,
                                         compute_op=ALU.add).then_inc(s.y_st, 16)
                    q.wait_ge(s.y_st, i * 16 + 16)
                    q.sem_inc(s.y_free, 1)

                def send(i):
                    q.tensor_copy(sent_idx[:], idx[:].rearrange("p t k -> p (t k)")[:, bass.ds(i * SENT, SENT)])
                    q.tensor_copy(sent[:], pay[:].bitcast(I32).rearrange("p t k c -> p (t k) c")[:, bass.ds(i * SENT, SENT), :])\
                        .then_inc(s.sent_ready, 1)
                    hold(q, s.sent_ready, i + 1, s.gspare)
                    for k in range(SENT):
                        q.indirect_dma_start(d.slots[:, :], bass.IndirectOffsetOnAxis(ap=sent_idx[:, k:k + 1], axis=0),
                                             sent[:, k, :], None).then_inc(s.sent_st, 16)
                    hold(q, s.sent_st, i * 16 * SENT + 16 * SENT, s.gspare)

                with q.Fori(0, SENDERS) as i:
                    body(0, i, False)
                    send(i)
                q.dma_start(tab[:, SH_TILES:NT, :], rows(d.slots)[:, SH_TILES:NT, :]).then_inc(s.tab_in, 16)
                q.wait_ge(s.tab_in, 32)
                total = q.value_load(bounds[0:1, NE:NE + 1], min_val=SH_TILES + 1, max_val=MAX_TILES)
                with q.Fori(SENDERS, total) as i:
                    body(0, i, False)
                q.wait_ge(s.x_in, total * 16 + 32)

            @block.vector
            def _(v):
                v.sem_inc(s.up_free, 2)

                def split_weights(e, j):
                    v.wait_ge(s.w_hi, PIECES * e + j + 1)
                    for w, rows, ks, src in parts(j):
                        op = v.tensor_tensor(w[1][rows, ks, :], src, w[0][rows, ks, :], ALU.subtract)
                    op.then_inc(s.w_lo, 1)

                def split_tokens(tile):
                    for half in range(2):
                        v.wait_ge(s.xT_hi, 2 * tile + half + 1)
                        v.tensor_tensor(xT[1][:, 4 * half:4 * half + 4, :], ps[6 + half][:].rearrange("p (k m) -> p k m", m=P),
                                        xT[0][:, 4 * half:4 * half + 4, :], ALU.subtract).then_inc(s.xT_lo, 1)

                split_tokens(0)
                for j in range(PIECES):
                    split_weights(0, j)

                def body(e, i, split):
                    for n in range(2):
                        if split and n == 1:
                            split_weights(e + 1, 0)
                        v.wait_ge(s.silu_done, 2 * i + n + 1)
                        v.wait_ge(s.up_done, 2 * i + n + 1)
                        v.tensor_tensor(h[:, n * FH:(n + 1) * FH], g[:, n * FH:(n + 1) * FH], ps[2 + n][:, 0:FH], ALU.mult)\
                            .then_inc(s.up_free, 1)
                    for n, (bank, ks) in enumerate(turned_h):
                        v.wait_ge(s.hT_hi, 2 * i + n + 1)
                        v.tensor_tensor(hT[1][:, ks, :], bank, hT[0][:, ks, :], ALU.subtract).then_inc(s.hT_lo, 1)
                    split_tokens(i + 1)
                    if split:
                        split_weights(e + 1, 1)
                        split_weights(e + 1, 2)
                        split_weights(e + 1, 3)
                    v.wait_ge(s.cols, i + 1)
                    v.wait_ge(s.y_free, i + 1)
                    v.wait_ge(s.down_done, 2 * i + 2)
                    v.tensor_scalar(y[:, 512:D], ps[5][:], wcol[:, 0:1], None, ALU.mult).then_inc(s.y_ready, 1)
                    if split:
                        split_weights(e + 1, 4)
                        split_weights(e + 1, 5)

                each_tile(v, body)

            @block.scalar
            def _(act):
                def split_weights(e, j):
                    act.wait_ge(raw_in[j % 3], loaded(e, j))
                    for w, rows, ks, src in parts(j):
                        op = act.activation(w[0][rows, ks, :], src, ACT.Copy)
                    op.then_inc(s.w_hi, 1)

                def take_turned(tile, half):
                    act.wait_ge(s.turned, 2 * tile + half + 1)
                    act.activation(xT[0][:, 4 * half:4 * half + 4, :], ps[6 + half][:].rearrange("p (k m) -> p k m", m=P),
                                   ACT.Copy).then_inc(s.xT_hi, 1)

                take_turned(0, 0)
                take_turned(0, 1)
                for j in range(PIECES):
                    split_weights(0, j)

                def body(e, i, split):
                    for n in range(2):
                        act.wait_ge(s.gate_done, 2 * i + n + 1)
                        act.wait_ge(s.up_free, 2 * i + n + 1)
                        act.activation(g[:, n * FH:(n + 1) * FH], ps[n][:, 0:FH], ACT.Silu).then_inc(s.silu_done, 1)
                    if split:
                        split_weights(e + 1, 0)
                        split_weights(e + 1, 1)
                    for n, (bank, ks) in enumerate(turned_h):
                        act.wait_ge(s.h_turned, 2 * i + n + 1)
                        act.activation(hT[0][:, ks, :], bank, ACT.Copy).then_inc(s.hT_hi, 1)
                        if n == 0:
                            take_turned(i + 1, 0)
                            take_turned(i + 1, 1)
                    if split:
                        split_weights(e + 1, 2)
                        split_weights(e + 1, 3)
                    act.wait_ge(s.cols, i + 1)
                    act.wait_ge(s.y_free, i + 1)
                    act.wait_ge(s.down_done, 2 * i + 1)
                    act.activation(y[:, 0:512], ps[4][:], ACT.Copy, scale=wcol[:, 0:1]).then_inc(s.y_ready, 1)
                    if split:
                        act.wait_ge(s.down_done, 2 * i + 2)
                        split_weights(e + 1, 4)
                        split_weights(e + 1, 5)

                each_tile(act, body)

            @block.tensor
            def _(pe):
                def turn_tokens(i, half):
                    if half == 0:
                        pe.wait_ge(s.x_in, i * 16 + 16)
                    for k in range(4 * half, 4 * half + 4):
                        mm = pe.transpose(ps[6 + half][:, (k % 4) * P:(k % 4 + 1) * P], x[:, k * P:(k + 1) * P], ident)
                    mm.then_inc(s.turned, 1)

                def turn_h(bank, places):
                    for k in places:
                        c = H_CHUNKS[k]
                        at_k = (k - places[0]) * P
                        mm = pe.transpose(ps[bank][0:FCW[c], at_k:at_k + P], h[:, c * P:c * P + FCW[c]], ident)
                    mm.then_inc(s.h_turned, 1)

                def product(bank, at, w, chunks, widths, cols, lo_ready, from_chunk):
                    n = len(chunks)
                    for k in range(n):
                        if k in from_chunk:
                            pe.wait_ge(*from_chunk[k])
                        for side in range(2):
                            c = chunks[k]
                            pe.matmul(bank, at[0][0:widths[c], k, :], w[side][0:widths[c], c, cols],
                                      start=(k == 0 and side == 0), stop=False)
                    pe.wait_ge(*lo_ready)
                    for k in range(n):
                        c = chunks[k]
                        mm = pe.matmul(bank, at[1][0:widths[c], k, :], w[0][0:widths[c], c, cols],
                                       start=False, stop=(k == n - 1))
                    return mm

                turn_tokens(0, 0)
                turn_tokens(0, 1)
                pe.sem_inc(s.hT_lo, 2)

                def body(e, i, _):
                    pe.wait_ge(s.xT_lo, 2 * i + 2)
                    for n in range(2):
                        pe.wait_ge(s.hT_lo, 2 * i + 2)
                        product(ps[n][:, 0:FH], xT, wg, range(KC), [P] * KC, slice(n * FH, (n + 1) * FH), (s.xT_lo, 2 * i + 2),
                                {0: (s.w_lo, PIECES * e + 1), 4: (s.w_lo, PIECES * e + 2)})\
                            .then_inc(s.gate_done, 1)
                    for n in range(2):
                        pe.wait_ge(s.up_free, 2 * i + n + 1)
                        product(ps[2 + n][:, 0:FH], xT, wu, range(KC), [P] * KC, slice(n * FH, (n + 1) * FH), (s.xT_lo, 2 * i + 2),
                                {0: (s.w_lo, PIECES * e + 3), 4: (s.w_lo, PIECES * e + 4)})\
                            .then_inc(s.up_done, 1)
                    pe.wait_ge(s.silu_done, 2 * i + 2)
                    pe.wait_ge(s.up_free, 2 * i + 3)
                    turn_h(0, range(0, FIRST))
                    turn_tokens(i + 1, 0)
                    turn_tokens(i + 1, 1)
                    pe.wait_ge(s.up_free, 2 * i + 4)
                    turn_h(1, range(FIRST, FC))
                    pe.wait_ge(s.w_lo, PIECES * e + 6)
                    for n in range(2):
                        product(ps[4 + n][:], hT, wd, H_CHUNKS, FCW, slice(n * 512, (n + 1) * 512), (s.hT_lo, 2 * i + 4),
                                {0: (s.hT_hi, 2 * i + 1), FIRST: (s.hT_hi, 2 * i + 2)}).then_inc(s.down_done, 1)

                each_tile(pe, body, split=False)


def program(nc, d, stages="ahrm"):
    with ExitStack() as ctx:
        ps = [ctx.enter_context(nc.psum_tensor(f"bank{i}", [P, 512], F32)) for i in range(8)]
        ident = ctx.enter_context(nc.sbuf_tensor("ident", [P, P], F32))
        const_in = nc.alloc_semaphore("const_in")
        with nc.Block() as block:

            @block.sync
            def _(sp):
                sp.dma_start(ident[:], d.ident[:, :]).then_inc(const_in, 16)
                sp.wait_ge(const_in, 16)

        for half in range(2):
            with nc.sbuf_tensor(f"a{half}_qa", [P, CC, HALF_B, XH, LQ], F32) as qa:
                with ExitStack() as a:
                    sb = lambda n, s: a.enter_context(nc.sbuf_tensor(f"a{half}_{n}", s, F32))
                    qr = sb("qr", [R, HALF_B, XH, LQ])
                    cst = named({"rope_q": sb("rope_q", [P, HT]), "rope_k": sb("rope_k", [P, LK]), "iota": sb("iota", [P, LK])})
                    cin = nc.alloc_semaphore(f"a{half}_const_in")
                    with nc.Block() as block:

                        @block.sync
                        def _(sp):
                            sp.dma_start(cst.rope_q[:], d.rope_q[:, :]).then_inc(cin, 16)
                            sp.dma_start(cst.rope_k[:], d.rope_k[:, :]).then_inc(cin, 16)
                            sp.dma_start(cst.iota[:], d.iota[:, :]).then_inc(cin, 16)
                            sp.wait_ge(cin, 48)

                    queries(nc, ps, d, half, qa, qr, ident[:], cst)
                    contexts(nc, ps, d, half, qa, qr, ident[:], cst)
                merge(nc, ps, d, half, qa)
        if "h" in stages:
            heads(nc, ps, d, ident[:])
        if "r" in stages:
            with ExitStack() as m:
                bounds = m.enter_context(nc.sbuf_tensor("bounds", [P, 2 * NE + 1], I32))
                idx = m.enter_context(nc.sbuf_tensor("idx", [P, TT, TOP], I32))
                pay = m.enter_context(nc.sbuf_tensor("pay", [P, TT, TOP, 2], F32))
                raw = [m.enter_context(nc.sbuf_tensor(f"raw{i}", [P, 3 * D], F32)) for i in range(3)]
                raw_in = [nc.alloc_semaphore(f"raw_in{i}") for i in range(3)]
                route(nc, ps, d, ident[:], bounds, idx, pay, raw, raw_in)
                if "m" in stages:
                    experts(nc, ps, d, ident[:], bounds, idx, pay, raw, raw_in)


def laid_out(x, ctx_2048, itok_BxS_0_1023, L0_xattn_W_kvc, L0_xattn_W_dq, L0_xattn_W_uq, L0_xattn_W_qr, L0_xattn_W_uk,
             L0_xattn_W_kr, L0_xattn_W_uv, L0_xattn_W_o, L0_attn_Wq, L0_attn_bq, L0_attn_Wk, L0_attn_bk, L0_attn_Wv,
             L0_attn_bv, L0_attn_Wo, L0_attn_bo, L0_ffn_gate_w, L0_ffn_w_gate, L0_ffn_w_up, L0_ffn_w_down,
             L0_ffn_sw_gate, L0_ffn_sw_up, L0_ffn_sw_down):
    c = np.ascontiguousarray
    o = {}
    o["x"] = np.asarray(x).reshape(T, D)
    o["ctxT"] = c(np.asarray(ctx_2048).transpose(0, 2, 1))
    seg = np.asarray(itok_BxS_0_1023).T
    o["seg"] = c(np.concatenate([seg, seg], 0))
    o["wkvc"], o["wdq"] = np.asarray(L0_xattn_W_kvc), np.asarray(L0_xattn_W_dq)
    uq = np.asarray(L0_xattn_W_uq).reshape(QCC, P, XH, HD).transpose(2, 1, 0, 3)
    qr = np.asarray(L0_xattn_W_qr).reshape(QCC, P, XH, 2, R // 2).transpose(2, 1, 0, 3, 4)
    qr = np.concatenate([qr, qr[..., ::-1, :]], 3).reshape(XH, P, QCC, P)
    uk = np.asarray(L0_xattn_W_uk).reshape(KVC, XH, HD).transpose(1, 2, 0)
    o["head_w"] = c(np.concatenate([uq.reshape(XH, P, QCC * P), qr.reshape(XH, P, QCC * P), uk], 2))
    kr = np.asarray(L0_xattn_W_kr)
    o["wkr"] = c(np.concatenate([kr, kr[:, R // 2:], kr[:, :R // 2]], 1))
    o["head_v"] = c(np.asarray(L0_xattn_W_uv).reshape(CC, P, XH, HD).transpose(2, 1, 0, 3).reshape(XH, P, CC * P))
    o["wo"] = np.asarray(L0_xattn_W_o)
    split = lambda a: a.reshape((NH, DH // 2, 2) + a.shape[1:]).swapaxes(1, 2).reshape(a.shape)
    o["wq"], o["wk"] = c(split(np.asarray(L0_attn_Wq)).T), c(split(np.asarray(L0_attn_Wk)).T)
    o["wv"], o["wo2"] = c(np.asarray(L0_attn_Wv).T), c(np.asarray(L0_attn_Wo).T)
    rows = lambda a: c(np.broadcast_to(a, (P, D)))
    o["bq"], o["bk"] = rows(split(np.asarray(L0_attn_bq))), rows(split(np.asarray(L0_attn_bk)))
    o["bv"], o["bo"] = rows(np.asarray(L0_attn_bv)), rows(np.asarray(L0_attn_bo))
    cat = np.concatenate
    halves = lambda a: [np.asarray(a)[None, :, :F], np.asarray(a)[None, :, F:]]
    o["gate_w"] = np.asarray(L0_ffn_gate_w)
    o["e_gate"] = cat(halves(L0_ffn_sw_gate) + [np.asarray(L0_ffn_w_gate)])
    o["e_up"] = cat(halves(L0_ffn_sw_up) + [np.asarray(L0_ffn_w_up)])
    o["e_down"] = cat([np.asarray(L0_ffn_sw_down).reshape(SHARED, F, D), np.asarray(L0_ffn_w_down)])

    o["ident"] = np.eye(P, dtype=np.float32)
    o["iota"] = c(np.broadcast_to(np.arange(LK, dtype=np.float32), (P, LK)))

    def angles(half, length):
        inv = (np.float32(1.0) / np.float32(10000.0) ** (np.arange(half, dtype=np.float32) / np.float32(half)))
        return np.arange(length, dtype=np.float32)[:, None] * inv.astype(np.float32)

    ang = angles(R // 2, LK).T
    cs, sn = np.cos(ang), np.sin(ang)
    o["rope_k"] = c(cat([cs, cs, -sn, sn], 0)).astype(np.float32)
    o["rope_q"] = c(np.tile(o["rope_k"][:, :LQ], (1, HALF_B)))
    a2 = angles(DH // 2, LQ)
    order = (np.arange(8)[None, :] * 8 + np.arange(8)[:, None]).reshape(-1)
    a2 = np.tile(a2[order], (2, 1))
    o["cos2"] = c(np.tile(cat([np.cos(a2)] * 2, 1), (1, NH))).astype(np.float32)
    o["sin2"] = c(np.tile(cat([-np.sin(a2), np.sin(a2)], 1), (1, NH))).astype(np.float32)
    tok = np.arange(P) % 8
    same = tok[:, None] == tok[None, :]
    o["bmask"] = c(np.tile(np.where(same, 0.0, NEG).astype(np.float32), (1, 4)))
    o["tri"] = np.triu(np.ones((P, P), np.float32), 1)
    o["ones"] = np.ones((P, P), np.float32)
    slot = np.zeros((P, NT, 2), np.int32)
    slot[:, :, 0] = T + np.arange(P)[:, None]
    slot[:, :SH_TILES, 0] = (np.arange(SH_TILES)[None, :] % TT) * P + np.arange(P)[:, None]
    slot[:, :SH_TILES, 1] = np.float32(1.0).view(np.int32)
    o["slots0"] = slot.reshape(P * NT, 2)
    o["tokens"] = c((np.arange(TT)[None, :, None] * P + np.arange(P)[:, None, None]) * np.ones((1, 1, TOP))).astype(np.int32)
    return o


SCRATCH = {"x1": ([T, D], F32), "o2": ([B, P, 512], F32), "xn3": ([T + PAD, D], F32),
           "slots": ([P * NT, 2], I32)}


def build(nc, arrays, stages="ahrm", scratch="Internal"):
    d = {}
    for name, a in arrays.items():
        d[name] = nc.dram_tensor(f"in_{name}", a.shape, mybir.dt.from_np(a.dtype), kind="ExternalInput").ap()
    for name, (shape, dt) in SCRATCH.items():
        d[name] = nc.dram_tensor(f"tmp_{name}", shape, dt, kind=scratch).ap()
    d["out"] = nc.dram_tensor("out", [T + PAD, D], F32, kind="ExternalOutput").ap()
    program(nc, named(d), stages)


def kernel(**inputs):
    import concourse.bacc as bacc
    from concourse.bass_utils import run_bass_kernel_spmd

    arrays = laid_out(**inputs)
    nc = bacc.Bacc("TRN2", target_bir_lowering=False, num_devices=1)
    build(nc, arrays)
    r = run_bass_kernel_spmd(nc, [{f"in_{k}": v for k, v in arrays.items()}], core_ids=[0])
    return r.results[0]["out"][0:T].reshape(B, LQ, D)
```
